# Optimizing a Trainium2 kernel written in Bass

```python
import numpy as np
import jax
import jax.numpy as jnp

def _softmax(x, axis=-1):
    return jax.nn.softmax(x, axis=axis)

def _gelu(x):
    return jax.nn.gelu(x, approximate=True)

def _silu(x):
    return jax.nn.silu(x)

def _sigmoid(x):
    return jax.nn.sigmoid(x)

def _layernorm(x, axis=-1, eps=1e-05):
    m = jnp.mean(x, axis=axis, keepdims=True)
    v = jnp.var(x, axis=axis, keepdims=True)
    return (x - m) / jnp.sqrt(v + eps)

def _scatter_add(tgt, idx, src, axis=0):
    return tgt.at[idx].add(src)

def _segment_sum(src, seg, n):
    return jax.ops.segment_sum(src, seg, n)
kernel_name = 'mk_seq_preln_d1_jaxref_r8_666f2c'

def setup_inputs(seed: int=0):
    np.random.seed(seed)
    _w = jnp.asarray

    def _L0_attn_setup():
        import math
        import jax, jax.numpy as jnp
        import numpy as np
        D_MODEL = 128
        N_HEADS = 16
        HEAD_DIM = D_MODEL // N_HEADS
        B, L = (1, 512)

        def _slopes(n_heads):
            ratio = 2.0 ** (-8.0 / n_heads)
            return jnp.asarray([ratio ** (i + 1) for i in range(n_heads)], dtype=jnp.float32)
        key = jax.random.key(seed)
        ks = jax.random.split(key, 5)
        scale = 1.0 / math.sqrt(D_MODEL)
        return {'x': jax.random.normal(ks[0], (B, L, D_MODEL), dtype=jnp.float32), 'q_w': jax.random.normal(ks[1], (D_MODEL, D_MODEL), dtype=jnp.float32) * scale, 'k_w': jax.random.normal(ks[2], (D_MODEL, D_MODEL), dtype=jnp.float32) * scale, 'v_w': jax.random.normal(ks[3], (D_MODEL, D_MODEL), dtype=jnp.float32) * scale, 'o_w': jax.random.normal(ks[4], (D_MODEL, D_MODEL), dtype=jnp.float32) * scale}
    _L0_attn_in = _L0_attn_setup()

    def _L0_ffn_setup():
        import jax, jax.numpy as jnp
        import numpy as np
        DIM = 128
        DEPTH = 6
        HEADS = 16
        DIM_HEAD = 64
        WINDOW = 32
        INNER = HEADS * DIM_HEAD
        DIM_INNER = int(DIM * 4 * 2 / 3)
        QK_SCALE = 8.0

        def shift_tokens(t):
            a, s = jnp.split(t, 2, -1)
            s = jnp.pad(s, ((0, 0), (1, 0), (0, 0)))[:, :-1]
            return jnp.concatenate([a, s], -1)

        def l2norm(t):
            return t / jnp.maximum(jnp.linalg.norm(t, axis=-1, keepdims=True), 1e-12)

        def rotate_half(x):
            x1, x2 = jnp.split(x, 2, -1)
            return jnp.concatenate([-x2, x1], -1)

        def rotary_tables(n):
            half = jnp.arange(0, DIM_HEAD, 2, dtype=jnp.float32)
            inv_freq = 1.0 / 10000.0 ** (half / DIM_HEAD)
            t = jnp.arange(n, dtype=jnp.float32)
            freqs = t[:, None] * inv_freq[None, :]
            freqs = jnp.concatenate([freqs, freqs], -1)
            base_scale = (half + 0.4 * DIM_HEAD) / (1.4 * DIM_HEAD)
            power = (t - n // 2) / (WINDOW // 2)
            scale = base_scale[None, :] ** power[:, None]
            scale = jnp.concatenate([scale, scale], -1)
            return (freqs, scale)

        def local_attention(q, k, v):
            b, h, n, d = q.shape
            w = WINDOW
            nw = n // w
            bq = q.reshape(b, h, nw, w, d)
            bk = k.reshape(b, h, nw, w, d)
            bv = v.reshape(b, h, nw, w, d)

            def look(t):
                p = jnp.pad(t, ((0, 0), (0, 0), (1, 0), (0, 0), (0, 0)))
                return jnp.concatenate([p[:, :, :nw], p[:, :, 1:]], axis=3)
            bk2, bv2 = (look(bk), look(bv))
            seq = jnp.arange(n).reshape(nw, w)
            seq_p = jnp.pad(seq, ((1, 0), (0, 0)), constant_values=-1)
            jt = jnp.concatenate([seq_p[:nw], seq_p[1:]], axis=1)
            it = seq[:, :, None]
            jb = jt[:, None, :]
            mask = (it < jb) | (it > jb + w) | (jb == -1)
            sim = jnp.einsum('bhwie,bhwje->bhwij', bq, bk2) * QK_SCALE
            sim = jnp.where(mask, -jnp.finfo(sim.dtype).max, sim)
            attn = jax.nn.softmax(sim, -1)
            out = jnp.einsum('bhwij,bhwje->bhwie', attn, bv2)
            return out.reshape(b, h, n, d)

        def attn_layer(x, Wqkv, qs, ksc, Wo):
            b, n, _ = x.shape
            qkv = x @ Wqkv
            q, k, v = jnp.split(qkv, 3, -1)
            sh = lambda t: t.reshape(b, n, HEADS, DIM_HEAD).transpose(0, 2, 1, 3)
            q, k, v = (sh(q), sh(k), sh(v))
            q = l2norm(q) * qs
            k = l2norm(k) * ksc
            freqs, scale = rotary_tables(n)
            cos, sin = (jnp.cos(freqs), jnp.sin(freqs))
            q = q * cos * scale + rotate_half(q) * sin * scale
            inv = 1.0 / scale
            k = k * cos * inv + rotate_half(k) * sin * inv
            out = local_attention(q, k, v)
            out = out.transpose(0, 2, 1, 3).reshape(b, n, INNER)
            return out @ Wo

        def ffn_layer(x, g, bln, W1, b1, W2, b2):
            mu = x.mean(-1, keepdims=True)
            var = ((x - mu) ** 2).mean(-1, keepdims=True)
            xn = (x - mu) / jnp.sqrt(var + 1e-05) * g + bln
            hg = xn @ W1 + b1
            a, gate = jnp.split(hg, 2, -1)
            return a * jax.nn.gelu(gate, approximate=False) @ W2 + b2
        key = jax.random.key(seed)
        ks = jax.random.split(key, 8)
        B, N = (2, 256)
        init = lambda k, shape: jax.random.normal(k, shape, jnp.float32) * 0.02
        return {'x': jax.random.normal(ks[0], (B, N, DIM), jnp.float32), 'Wqkv': init(ks[1], (DEPTH, DIM, 3 * INNER)), 'q_scale': jnp.ones((DEPTH, DIM_HEAD), jnp.float32), 'k_scale': jnp.ones((DEPTH, DIM_HEAD), jnp.float32), 'Wo': init(ks[2], (DEPTH, INNER, DIM)), 'ln_g': jnp.ones((DEPTH, DIM), jnp.float32), 'ln_b': jnp.zeros((DEPTH, DIM), jnp.float32), 'W1': init(ks[3], (DEPTH, DIM, 2 * DIM_INNER)), 'b1': jnp.zeros((DEPTH, 2 * DIM_INNER), jnp.float32), 'W2': init(ks[4], (DEPTH, DIM_INNER, DIM)), 'b2': jnp.zeros((DEPTH, DIM), jnp.float32)}
    _L0_ffn_in = _L0_ffn_setup()
    _d = {'L0_attn_x': _L0_attn_in['x'], 'L0_attn_q_w': _L0_attn_in['q_w'], 'L0_attn_k_w': _L0_attn_in['k_w'], 'L0_attn_v_w': _L0_attn_in['v_w'], 'L0_attn_o_w': _L0_attn_in['o_w'], 'L0_ffn_Wqkv': _L0_ffn_in['Wqkv'], 'L0_ffn_q_scale': _L0_ffn_in['q_scale'], 'L0_ffn_k_scale': _L0_ffn_in['k_scale'], 'L0_ffn_Wo': _L0_ffn_in['Wo'], 'L0_ffn_ln_g': _L0_ffn_in['ln_g'], 'L0_ffn_ln_b': _L0_ffn_in['ln_b'], 'L0_ffn_W1': _L0_ffn_in['W1'], 'L0_ffn_b1': _L0_ffn_in['b1'], 'L0_ffn_W2': _L0_ffn_in['W2'], 'L0_ffn_b2': _L0_ffn_in['b2']}
    _x0 = _d['L0_attn_x']
    _d['L0_attn_x'] = jax.random.normal(jax.random.fold_in(jax.random.key(seed), 1), (4, 1024, 128), dtype=_x0.dtype)
    del _x0
    return _d

def reference(L0_attn_x, L0_attn_q_w, L0_attn_k_w, L0_attn_v_w, L0_attn_o_w, L0_ffn_Wqkv, L0_ffn_q_scale, L0_ffn_k_scale, L0_ffn_Wo, L0_ffn_ln_g, L0_ffn_ln_b, L0_ffn_W1, L0_ffn_b1, L0_ffn_W2, L0_ffn_b2):

    def _L0_attn_ref(x, q_w, k_w, v_w, o_w):
        import math
        import jax, jax.numpy as jnp
        import numpy as np
        D_MODEL = 128
        N_HEADS = 16
        HEAD_DIM = D_MODEL // N_HEADS
        B, L = (1, 512)

        def _slopes(n_heads):
            ratio = 2.0 ** (-8.0 / n_heads)
            return jnp.asarray([ratio ** (i + 1) for i in range(n_heads)], dtype=jnp.float32)
        b, l, _ = x.shape

        def proj(w):
            return (x @ w).reshape(b, l, N_HEADS, HEAD_DIM).transpose(0, 2, 1, 3)
        q, k, v = (proj(q_w), proj(k_w), proj(v_w))
        scale = math.sqrt(HEAD_DIM)
        scores = jnp.einsum('bhid,bhjd->bhij', q, k) / scale
        pos = jnp.arange(l)
        distance = jnp.abs(pos[None, :] - pos[:, None]).astype(jnp.float32)
        alibi = -distance[None, :, :] * _slopes(N_HEADS)[:, None, None]
        scores = scores + alibi[None]
        causal = pos[None, :] <= pos[:, None]
        scores = jnp.where(causal[None, None], scores, -jnp.inf)
        attn = jax.nn.softmax(scores, axis=-1)
        out = jnp.einsum('bhij,bhjd->bhid', attn, v)
        out = out.transpose(0, 2, 1, 3).reshape(b, l, D_MODEL)
        return out @ o_w

    def _L0_ffn_ref(x, Wqkv, q_scale, k_scale, Wo, ln_g, ln_b, W1, b1, W2, b2):
        import jax, jax.numpy as jnp
        import numpy as np
        DIM = 128
        DEPTH = 6
        HEADS = 16
        DIM_HEAD = 64
        WINDOW = 32
        INNER = HEADS * DIM_HEAD
        DIM_INNER = int(DIM * 4 * 2 / 3)
        QK_SCALE = 8.0

        def shift_tokens(t):
            a, s = jnp.split(t, 2, -1)
            s = jnp.pad(s, ((0, 0), (1, 0), (0, 0)))[:, :-1]
            return jnp.concatenate([a, s], -1)

        def l2norm(t):
            return t / jnp.maximum(jnp.linalg.norm(t, axis=-1, keepdims=True), 1e-12)

        def rotate_half(x):
            x1, x2 = jnp.split(x, 2, -1)
            return jnp.concatenate([-x2, x1], -1)

        def rotary_tables(n):
            half = jnp.arange(0, DIM_HEAD, 2, dtype=jnp.float32)
            inv_freq = 1.0 / 10000.0 ** (half / DIM_HEAD)
            t = jnp.arange(n, dtype=jnp.float32)
            freqs = t[:, None] * inv_freq[None, :]
            freqs = jnp.concatenate([freqs, freqs], -1)
            base_scale = (half + 0.4 * DIM_HEAD) / (1.4 * DIM_HEAD)
            power = (t - n // 2) / (WINDOW // 2)
            scale = base_scale[None, :] ** power[:, None]
            scale = jnp.concatenate([scale, scale], -1)
            return (freqs, scale)

        def local_attention(q, k, v):
            b, h, n, d = q.shape
            w = WINDOW
            nw = n // w
            bq = q.reshape(b, h, nw, w, d)
            bk = k.reshape(b, h, nw, w, d)
            bv = v.reshape(b, h, nw, w, d)

            def look(t):
                p = jnp.pad(t, ((0, 0), (0, 0), (1, 0), (0, 0), (0, 0)))
                return jnp.concatenate([p[:, :, :nw], p[:, :, 1:]], axis=3)
            bk2, bv2 = (look(bk), look(bv))
            seq = jnp.arange(n).reshape(nw, w)
            seq_p = jnp.pad(seq, ((1, 0), (0, 0)), constant_values=-1)
            jt = jnp.concatenate([seq_p[:nw], seq_p[1:]], axis=1)
            it = seq[:, :, None]
            jb = jt[:, None, :]
            mask = (it < jb) | (it > jb + w) | (jb == -1)
            sim = jnp.einsum('bhwie,bhwje->bhwij', bq, bk2) * QK_SCALE
            sim = jnp.where(mask, -jnp.finfo(sim.dtype).max, sim)
            attn = jax.nn.softmax(sim, -1)
            out = jnp.einsum('bhwij,bhwje->bhwie', attn, bv2)
            return out.reshape(b, h, n, d)

        def attn_layer(x, Wqkv, qs, ksc, Wo):
            b, n, _ = x.shape
            qkv = x @ Wqkv
            q, k, v = jnp.split(qkv, 3, -1)
            sh = lambda t: t.reshape(b, n, HEADS, DIM_HEAD).transpose(0, 2, 1, 3)
            q, k, v = (sh(q), sh(k), sh(v))
            q = l2norm(q) * qs
            k = l2norm(k) * ksc
            freqs, scale = rotary_tables(n)
            cos, sin = (jnp.cos(freqs), jnp.sin(freqs))
            q = q * cos * scale + rotate_half(q) * sin * scale
            inv = 1.0 / scale
            k = k * cos * inv + rotate_half(k) * sin * inv
            out = local_attention(q, k, v)
            out = out.transpose(0, 2, 1, 3).reshape(b, n, INNER)
            return out @ Wo

        def ffn_layer(x, g, bln, W1, b1, W2, b2):
            mu = x.mean(-1, keepdims=True)
            var = ((x - mu) ** 2).mean(-1, keepdims=True)
            xn = (x - mu) / jnp.sqrt(var + 1e-05) * g + bln
            hg = xn @ W1 + b1
            a, gate = jnp.split(hg, 2, -1)
            return a * jax.nn.gelu(gate, approximate=False) @ W2 + b2
        for i in range(DEPTH):
            x = attn_layer(shift_tokens(x), Wqkv[i], q_scale[i], k_scale[i], Wo[i]) + x
            x = ffn_layer(shift_tokens(x), ln_g[i], ln_b[i], W1[i], b1[i], W2[i], b2[i]) + x
        return x
    x = L0_attn_x
    x = x + _L0_attn_ref(_layernorm(x, axis=-1), L0_attn_q_w, L0_attn_k_w, L0_attn_v_w, L0_attn_o_w)
    x = x + _L0_ffn_ref(_layernorm(x, axis=-1), L0_ffn_Wqkv, L0_ffn_q_scale, L0_ffn_k_scale, L0_ffn_Wo, L0_ffn_ln_g, L0_ffn_ln_b, L0_ffn_W1, L0_ffn_b1, L0_ffn_W2, L0_ffn_b2)
    return x

_drawn_inputs = setup_inputs


def setup_inputs(seed=0):
    import zlib

    import numpy as np

    out = dict(_drawn_inputs(seed))
    spreads = {'L0_ffn_q_scale': (1.0, 0.6),
     'L0_ffn_k_scale': (1.0, 0.6),
     'L0_ffn_ln_g': (1.0, 0.6),
     'L0_ffn_ln_b': (0.0, 0.8),
     'L0_ffn_b1': (0.0, 0.8),
     'L0_ffn_b2': (0.0, 0.1)}
    factors = {'L0_ffn_W1': 3.748, 'L0_ffn_W2': 3.682}
    for name, (base, spread) in spreads.items():
        noise = np.random.default_rng([zlib.crc32(name.encode()), seed]).standard_normal(out[name].shape)
        drawn = base * np.exp(spread * noise) if base else spread * noise
        out[name] = jnp.asarray(drawn.astype(out[name].dtype))
    for name, factor in factors.items():
        out[name] = (out[name] * factor).astype(out[name].dtype)
    return out
```

```python
import numpy as np
import concourse.bass as bass
from concourse import mybir
from contextlib import ExitStack

F32 = mybir.dt.float32
F32R = mybir.dt.float32r
BF16 = mybir.dt.bfloat16
ALU = mybir.AluOpType
ACT = mybir.ActivationFunctionType
X = mybir.AxisListType.X

P = 128
MASKED = -1e37
ROOT = 12
I32 = mybir.dt.int32


class Geometry:

    def __init__(self, x, wqkv, q_scale, w1, wo):
        self.B, self.L, self.D = x.shape
        self.depth = wqkv.shape[0]
        self.inner = wqkv.shape[2] // 3
        self.hd = q_scale.shape[1]
        self.heads = self.inner // self.hd
        self.ffn = w1.shape[2] // 2
        self.blocks = self.L // P
        self.window = 32
        self.keys = P + self.window
        self.chunks = self.inner // P
        self.fchunks = -(-self.ffn // P)
        self.a_heads, self.a_hd = 16, self.D // 16


START = 1


def start_all(eng, sems):
    for s in sems:
        eng.sem_inc(s, START)


def inverse_root(dve, y, x, xh, t, source, floor, op, step, base):
    dve.tensor_scalar(x, source, floor, None, op).then_inc(step, 1)
    dve.wait_ge(step, START + base + 1)
    dve.tensor_scalar(y.bitcast(I32), x.bitcast(I32), -0.5, float(0x5f3759df), ALU.mult, ALU.add).then_inc(step, 1)
    dve.tensor_scalar(xh, x, -0.5, None, ALU.mult).then_inc(step, 1)
    dve.wait_ge(step, START + base + 3)
    for k in range(3):
        dve.tensor_tensor(t, y, y, ALU.mult).then_inc(step, 1)
        dve.wait_ge(step, START + base + 4 + 3 * k)
        dve.tensor_tensor(t, t, xh, ALU.mult).then_inc(step, 1)
        dve.wait_ge(step, START + base + 5 + 3 * k)
        dve.scalar_tensor_tensor(y, t, 1.5, y, ALU.add, ALU.mult).then_inc(step, 1)
        dve.wait_ge(step, START + base + 6 + 3 * k)


class TokenNorm:

    GROUP = 4

    def __init__(self, nc, ctx, name, x_all, ident, turned_ps):
        def sb(part, shape):
            return ctx.enter_context(nc.sbuf_tensor(f"{name}_{part}", shape, F32))

        self.sems = []

        def sem(part):
            self.sems.append(ctx.enter_context(nc.semaphore(f"{name}_{part}")))
            return self.sems[-1]
        n = self.GROUP
        self.x_all, self.ident, self.ps = x_all, ident, turned_ps
        self.stats, self.mv = sb("stats", [P, n, 6]), sb("mv", [P, n, 2])
        self.root = sb("root", [P, 4, n])
        self.xn = sb("xn", [P, n, P])
        self.stat_step, self.root_step = sem("stat_step"), sem("root_step")
        self.normed, self.turned = sem("normed"), sem("turned")
        self.gate = sem("gate")

    def vector(self, dve, t):
        n = self.GROUP
        for k in range(n):
            dve.bn_stats(self.stats[:, k, :], self.x_all[:, t * n + k, :]).then_inc(self.stat_step, 1)
        dve.wait_ge(self.stat_step, START + 2 * n * t + n)
        dve.sem_inc(self.gate, 1)
        for k in range(n):
            dve.bn_aggr(self.mv[:, k, :], self.stats[:, k, :]).then_inc(self.stat_step, 1)
        dve.wait_ge(self.stat_step, START + 2 * n * (t + 1))
        r = self.root
        inverse_root(dve, r[:, 0, :], r[:, 1, :], r[:, 2, :], r[:, 3, :], self.mv[:, :, 1], 1e-5, ALU.add,
                     self.root_step, ROOT * t)
        dve.wait_ge(self.turned, START + t)
        for k in range(n):
            dve.tensor_scalar(self.xn[:, k, :], self.x_all[:, t * n + k, :], self.mv[:, k, 0:1],
                              r[:, 0, k:k + 1], ALU.subtract, ALU.mult).then_inc(self.normed, 1)

    def tensor(self, pe, t):
        n = self.GROUP
        pe.wait_ge(self.normed, START + n * (t + 1))
        for k in range(n):
            mm = pe.transpose(self.ps[:, k * P:(k + 1) * P], self.xn[:, k, :], self.ident[:, :])
        mm.then_inc(self.turned, 1)


def prepare(nc, g, x_all, va, ident, x, q_w, k_w, v_w, parts_d):
    B, L, D = g.B, g.L, g.D
    HA, HDA = g.a_heads, g.a_hd
    GT = 4 * P
    GROUPS = B * L // GT
    PER = L // GT
    ctx = ExitStack()
    with ctx:
        def sb(name, shape, dt=F32):
            return ctx.enter_context(nc.sbuf_tensor(name, shape, dt))

        def ps(name, shape):
            return ctx.enter_context(nc.psum_tensor(name, shape, F32))

        sems = []

        def sem(name):
            sems.append(ctx.enter_context(nc.semaphore(name)))
            return sems[-1]

        w = sb("w_qkv_a", [P, 3, D])
        xnT = sb("xnT", [P, GT])
        qkf = sb("qkf", [P, 2, GT])
        rest = sb("rest", [P, 2, GT])
        parts = sb("parts", [P, 2, 3, GT], BF16)
        p_turn = ps("p_turn", [P, GT])
        p_qk = ps("p_qk", [P, 2, GT])
        p_v = ps("p_v", [P, GT])
        x_in = sem("x_in")
        w_in = sem("a_w_in")
        xnT_ok = sem("xnT_ok")
        qk_done = sem("a_qk_done")
        v_done = sem("a_v_done")
        qkf_ok = sem("qkf_ok")
        va_ok = sem("va_ok")
        va_pad = sem("va_pad")
        split = sem("split_step")
        stored = sem("parts_stored")
        ln = TokenNorm(nc, ctx, "ln_a", x_all, ident, p_turn)
        block = ctx.enter_context(nc.Block())

        @block.gpsimd
        def _(pool):
            start_all(pool, sems + ln.sems)

        @block.sync
        def _(sp):
            for b in range(B):
                n = L // P
                sp.dma_start(x_all[:, b * n:(b + 1) * n, :], x[b].rearrange("(k p) d -> p k d", p=P)).then_inc(x_in, 16)
            for i, t in enumerate((q_w, k_w, v_w)):
                sp.dma_start(w[:, i, :], t).then_inc(w_in, 16)
            with sp.Fori(0, B) as b:
                for h in range(PER):
                    t = b * PER + h
                    sp.wait_ge(split, START + 8 * (t + 1))
                    for i in range(2):
                        sp.dma_start(parts_d[b, i, :, :, h * GT:(h + 1) * GT].rearrange("s p n -> p s n"),
                                     parts[:, i, :, :]).then_inc(stored, 16)
            sp.wait_ge(stored, START + 32 * GROUPS)

        @block.tensor
        def _(pe):
            pe.wait_ge(w_in, START + 48)
            with pe.Fori(0, GROUPS) as t:
                ln.tensor(pe, t)
                pe.wait_ge(xnT_ok, START + t + 1)
                pe.wait_ge(qkf_ok, START + t * 2)
                pe.wait_ge(va_ok, START + t)
                for i in range(2):
                    pe.matmul(p_qk[:, i, :], w[:, i, :], xnT[:, :], start=True, stop=True).then_inc(qk_done, 1)
                for k in range(4):
                    mm = pe.matmul(p_v[:, k * P:(k + 1) * P], xnT[:, k * P:(k + 1) * P], w[:, 2, :], start=True, stop=True)
                mm.then_inc(v_done, 1)

        @block.scalar
        def _(act):
            act.wait_ge(va_pad, START + 1)
            with act.Fori(0, GROUPS) as t:
                act.wait_ge(ln.turned, START + t + 1)
                act.wait_ge(v_done, START + t)
                act.activation(xnT[:, :], p_turn[:, :], ACT.Copy).then_inc(xnT_ok, 1)
                act.wait_ge(split, START + 8 * t)
                for i in range(2):
                    act.wait_ge(qk_done, START + 2 * t + i + 1)
                    act.activation(qkf[:, i, :], p_qk[:, i, :], ACT.Copy,
                                   scale=1.0 / float(np.sqrt(HDA)) if i == 0 else 1.0).then_inc(qkf_ok, 1)
                act.wait_ge(v_done, START + t + 1)
                act.activation(va[:, bass.ds(t * 4, 4), :, 0:HDA],
                               p_v[:, :].rearrange("p (k h d) -> p k h d", k=4, d=HDA), ACT.Copy).then_inc(va_ok, 1)

        @block.vector
        def _(dve):
            dve.memset(va[:, :, :, :], 1.0).then_inc(va_pad, 1)
            dve.wait_ge(x_in, START + 16 * B)
            with dve.Fori(0, GROUPS) as t:
                ln.vector(dve, t)
                dve.wait_ge(stored, START + 32 * t)
                for i in range(2):
                    dve.wait_ge(qkf_ok, START + 2 * t + i + 1)
                    at = 8 * t + 4 * i
                    dve.tensor_copy(parts[:, i, 0, :], qkf[:, i, :]).then_inc(split, 1)
                    dve.wait_ge(split, START + at + 1)
                    dve.tensor_tensor(rest[:, i, :], qkf[:, i, :], parts[:, i, 0, :], ALU.subtract).then_inc(split, 1)
                    dve.wait_ge(split, START + at + 2)
                    dve.tensor_copy(parts[:, i, 1, :], rest[:, i, :]).then_inc(split, 1)
                    dve.wait_ge(split, START + at + 3)
                    dve.tensor_tensor(parts[:, i, 2, :], rest[:, i, :], parts[:, i, 1, :], ALU.subtract).then_inc(split, 1)


def hand_over(nc, g, x_all, hT, ident, x1_d):
    GT = 4 * P
    PER = g.L // GT
    ctx = ExitStack()
    with ctx:
        p_turn = ctx.enter_context(nc.psum_tensor("p_turn2", [P, GT], F32))
        kept = ctx.enter_context(nc.semaphore("hT_kept"))
        stored = ctx.enter_context(nc.semaphore("x1_stored"))
        ln = TokenNorm(nc, ctx, "ln_b", x_all, ident, p_turn)
        block = ctx.enter_context(nc.Block())

        @block.gpsimd
        def _(pool):
            start_all(pool, [kept, stored] + ln.sems)

        @block.sync
        def _(sp):
            sp.dma_start(x1_d, x_all[:, :, :]).then_inc(stored, 16)
            sp.wait_ge(stored, START + 16)

        @block.vector
        def _(dve):
            with dve.Fori(0, g.B * PER) as t:
                ln.vector(dve, t)

        @block.tensor
        def _(pe):
            with pe.Fori(0, g.B * PER) as t:
                pe.wait_ge(kept, START + t)
                ln.tensor(pe, t)

        @block.scalar
        def _(act):
            with act.Fori(0, g.B) as b:
                for h in range(PER):
                    act.wait_ge(ln.turned, START + b * PER + h + 1)
                    act.activation(hT[:, b, 1 + h * GT:1 + (h + 1) * GT], p_turn[:, :], ACT.Copy).then_inc(kept, 1)


def causal_attention(nc, g, x_all, va, ident, identb, cmask, o_w, parts_d, bias_d):
    B, L, D = g.B, g.L, g.D
    HA, HDA = g.a_heads, g.a_hd
    NB = L // P
    QUADS = HA // 4
    ROWS = 9 * HDA
    MROW = 96
    PIECES = [(I, c, min(c + 512, P * (I + 1))) for I in range(NB) for c in range(0, P * (I + 1), 512)]
    PACKS = [[(0, 0)], [(1, 0), (7, 7 * P)], [(2, 0), (6, 6 * P)], [(3, 0), (5, 5 * P)], [(4, 0)]]
    NP = len(PACKS)
    ctx = ExitStack()
    with ctx:
        def sb(name, shape, dt=F32):
            return ctx.enter_context(nc.sbuf_tensor(name, shape, dt))

        def ps(name, shape):
            return ctx.enter_context(nc.psum_tensor(name, shape, F32))

        sems = []

        def sem(name):
            sems.append(ctx.enter_context(nc.semaphore(name)))
            return sems[-1]

        qst = sb("q_stack", [P, 2, 4, L], BF16)
        kst = sb("k_stack", [P, 2, 4, L], BF16)
        pt = sb("p_t", [P, 3, 4, L])
        vc = sb("v_cur", [P, NB, HA, HDA + 1])
        mx = sb("mx", [P, 2, 4, NB])
        mrow = sb("mrow", [32, P])
        mrest = sb("mrest", [32, P])
        mparts = sb("mparts", [32, 3, P], BF16)
        ot = sb("ot", [P, L])
        osum = sb("osum", [P, NB, 4])
        on = sb("on", [P, NB, D])
        onT = sb("onT", [P, L])
        wo = sb("wo_a", [P, D])
        p_max = ps("p_max", [P, 2, 512])
        p_exp = ps("p_exp", [P, 2, L])
        p_pv = ps("p_pv", [P, L])

        stacks_clear = sem("stacks_clear")
        wo_in = sem("wo_a_in")
        stacked = [sem("stacked0"), sem("stacked1")]
        maxed = sem("max_scores")
        m_read = sem("max_read")
        m_all = sem("max_merged")
        m_turn = sem("max_turned")
        m_step = sem("max_split_step")
        m_rows = sem("max_rows_in")
        st_done = sem("scores_t")
        ex_done = sem("exponentials")
        pv_done = sem("pv_a_done")
        packs_used = sem("packs_used")
        ot_ok = sem("ot_ok")
        ot_turn = sem("ot_turned")
        o_rec = sem("o_reciprocal")
        on_ok = sem("on_ok")
        on_turn = sem("on_turned")
        onT_ok = sem("onT_ok")
        proj_a = sem("o_projected")
        x1_ok = sem("x1_ok")
        v_cur = sem("v_cur_ok")
        dve_gate = sem("dve_gate_a")
        block = ctx.enter_context(nc.Block())
        STACK_DMAS = 2 * 9 + 2

        @block.gpsimd
        def _(pool):
            start_all(pool, sems)

        @block.sync
        def _(sp):
            sp.dma_start(wo[:, :], o_w).then_inc(wo_in, 16)
            sp.wait_ge(stacks_clear, START + 1)

            def fill(b, q):
                s = q % 2
                G = b * QUADS + q
                if q >= 2:
                    sp.wait_ge(st_done, START + 4 * NP * (G - 1))
                else:
                    sp.wait_ge(st_done, START + 4 * NP * QUADS * b)
                for a in range(3):
                    for c in range(3):
                        r = (a * 3 + c) * HDA
                        for i, (st, part) in enumerate(((qst, a), (kst, c))):
                            src = parts_d[b, i, part, 32 * q:32 * q + 32, :].rearrange("(h d) n -> d h n", d=HDA)
                            sp.dma_start(st[r:r + HDA, s, :, :], src).then_inc(stacked[s], 16)
                for i, st in enumerate((qst, kst)):
                    sp.dma_start(st[ROWS:ROWS + 12, s, :, :],
                                 bias_d[4 * q:4 * q + 4, i, :, :].rearrange("h r n -> r h n")).then_inc(stacked[s], 16)

            def max_rows(b, q):
                G = b * QUADS + q
                sp.wait_ge(m_step, START + 4 * (G + 1))
                for h in range(4):
                    for part in range(3):
                        dst = qst[MROW + part:MROW + part + 1, q % 2, h, :].rearrange("p (i n) -> p i n", n=P)
                        sp.dma_start(dst, mparts[NB * h:NB * h + NB, part, :]).then_inc(m_rows, 16)

            with sp.Fori(0, B) as b:
                fill(b, 0)
                fill(b, 1)
                max_rows(b, 0)
                for q in range(1, QUADS):
                    max_rows(b, q)
                    if q + 1 < QUADS:
                        fill(b, q + 1)

        @block.tensor
        def _(pe):
            def max_piece(b, q, n):
                G = b * QUADS + q
                h, (I, c0, c1) = n // len(PIECES), PIECES[n % len(PIECES)]
                N = 4 * len(PIECES) + 1
                s = q % 2
                if n == 0:
                    pe.wait_ge(stacked[s], START + 16 * STACK_DMAS * (b * QUADS // 2 + q // 2 + 1))
                if n >= 2:
                    pe.wait_ge(m_read, START + N * G + n - 1)
                else:
                    pe.wait_ge(m_read, START + N * G)
                out = p_max[:, n % 2, 0:c1 - c0]
                diag = c1 == P * (I + 1)
                mm = pe.matmul(out, qst[0:MROW, s, h, P * I:P * (I + 1)], kst[0:MROW, s, h, c0:c1],
                               start=True, stop=not diag)
                if diag:
                    mm = pe.matmul(out[:, c1 - c0 - P:c1 - c0], identb[:, :], cmask[:, :], start=False, stop=True)
                mm.then_inc(maxed, 1)

            def turn_max(b, q):
                G = b * QUADS + q
                pe.wait_ge(m_all, START + G + 1)
                pe.transpose(p_max[0:32, 0, 0:P], mx[:, 0, :, :].rearrange("p h i -> p (h i)"),
                             ident[:, :]).then_inc(m_turn, 1)

            def scores_t(b, q, k, h):
                G = b * QUADS + q
                U = 4 * NP * G + 4 * k + h
                if k == 0 and h == 0:
                    pe.wait_ge(m_rows, START + 16 * 12 * (G + 1))
                if 4 * k + h >= 2:
                    pe.wait_ge(ex_done, START + U - 1)
                else:
                    pe.wait_ge(ex_done, START + 4 * NP * G)
                s = q % 2
                for J, at in PACKS[k]:
                    lo = J * P
                    while lo < L:
                        o = at + lo - J * P
                        hi = min(L, lo + 512 - o % 512)
                        diag = lo == J * P
                        mm = pe.matmul(p_exp[:, h % 2, o:o + hi - lo], kst[:, s, h, J * P:(J + 1) * P],
                                       qst[:, s, h, lo:hi], start=True, stop=not diag)
                        if diag:
                            mm = pe.matmul(p_exp[:, h % 2, o:o + P], cmask[:, :], identb[:, :],
                                           start=False, stop=True)
                        lo = hi
                mm.then_inc(st_done, 1)

            def pv(b, q, k):
                G = b * QUADS + q
                K = NP * q + k
                pe.wait_ge(ex_done, START + 4 * (NP * G + k + 1))
                if k == 0:
                    pe.wait_ge(v_cur, START + b + 1)
                    pe.wait_ge(on_ok, START + G)
                    pe.wait_ge(x1_ok, START + b)
                for J, at in PACKS[k]:
                    for seg in range(2):
                        lo, hi = max(J * P, 512 * seg), 512 * (seg + 1)
                        if lo >= hi:
                            continue
                        for h in range(4):
                            o = at + lo - J * P
                            mm = pe.matmul(p_pv[32 * h:32 * h + HDA + 1, lo:hi], vc[:, J, 4 * q + h, :],
                                           pt[:, K % 3, h, o:o + hi - lo], start=(J == 0), stop=(k == NP - 1),
                                           skip_group_check=True)
                mm.then_inc(pv_done, 1)

            def turn_o(b, q):
                G = b * QUADS + q
                pe.wait_ge(ot_ok, START + G + 1)
                for i in range(NB):
                    mm = pe.transpose(p_pv[:, i * P:(i + 1) * P], ot[:, i * P:(i + 1) * P], ident[:, :])
                mm.then_inc(ot_turn, 1)

            def out_proj(b):
                pe.wait_ge(on_ok, START + QUADS * (b + 1))
                for i in range(NB):
                    mm = pe.transpose(p_pv[:, i * P:(i + 1) * P], on[:, i, :], ident[:, :])
                mm.then_inc(on_turn, 1)
                pe.wait_ge(onT_ok, START + b + 1)
                for i in range(NB):
                    mm = pe.matmul(p_pv[:, i * P:(i + 1) * P], onT[:, i * P:(i + 1) * P], wo[:, :], start=True, stop=True)
                mm.then_inc(proj_a, 1)

            NPI = 4 * len(PIECES)
            pe.wait_ge(wo_in, START + 16)
            with pe.Fori(0, B) as b:
                for n in range(NPI):
                    max_piece(b, 0, n)
                turn_max(b, 0)
                for q in range(QUADS):
                    done = 0
                    for k in range(NP):
                        for h in range(4):
                            scores_t(b, q, k, h)
                            if q + 1 < QUADS:
                                while done < min(NPI, NPI * (4 * k + h + 1) // (4 * NP - 4)):
                                    max_piece(b, q + 1, done)
                                    done += 1
                        if k == NP - 1 and q + 1 < QUADS:
                            turn_max(b, q + 1)
                        if k >= 1:
                            pv(b, q, k - 1)
                    pv(b, q, NP - 1)
                    turn_o(b, q)
                out_proj(b)

        @block.scalar
        def _(act):
            with act.Fori(0, B) as b:
                for q in range(QUADS):
                    G = b * QUADS + q
                    for k in range(NP):
                        K = NP * q + k
                        for h in range(4):
                            U = 4 * NP * G + 4 * k + h
                            act.wait_ge(st_done, START + U + 1)
                            if h == 0:
                                if K >= 3:
                                    act.wait_ge(pv_done, START + NP * QUADS * b + K - 2)
                                else:
                                    act.wait_ge(pv_done, START + NP * QUADS * b)
                            w = L if k < NP - 1 else L // 2
                            act.activation(pt[:, K % 3, h, 0:w], p_exp[:, h % 2, 0:w], ACT.Exp).then_inc(ex_done, 1)
                    act.wait_ge(pv_done, START + NP * (G + 1))
                    act.activation(ot[:, :], p_pv[:, :], ACT.Copy).then_inc(ot_ok, 1)
                act.wait_ge(on_turn, START + b + 1)
                act.activation(onT[:, :], p_pv[:, :], ACT.Copy).then_inc(onT_ok, 1)

        @block.vector
        def _(dve):
            NPI = 4 * len(PIECES)

            def maxima(b, q):
                G = b * QUADS + q
                N = NPI + 1
                for n in range(NPI):
                    h, (I, c0, c1) = n // len(PIECES), PIECES[n % len(PIECES)]
                    dve.wait_ge(maxed, START + NPI * G + n + 1)
                    dve.tensor_reduce(mx[:, c0 // 512, h, I:I + 1], p_max[:, n % 2, 0:c1 - c0], X, ALU.max)\
                       .then_inc(m_read, 1)
                dve.wait_ge(m_read, START + N * G + NPI)
                half = 512 // P
                dve.tensor_tensor(mx[:, 0, :, half:NB], mx[:, 0, :, half:NB], mx[:, 1, :, half:NB], ALU.max)\
                   .then_inc(m_all, 1)
                dve.wait_ge(m_turn, START + G + 1)
                dve.wait_ge(m_rows, START + 16 * 12 * G)
                dve.tensor_scalar(mrow[:, :], p_max[0:32, 0, 0:P], -1.0, None, ALU.mult).then_inc(m_read, 1)
                dve.wait_ge(m_read, START + N * (G + 1))
                dve.tensor_copy(mparts[:, 0, :], mrow[:, :]).then_inc(m_step, 1)
                dve.wait_ge(m_step, START + 4 * G + 1)
                dve.tensor_tensor(mrest[:, :], mrow[:, :], mparts[:, 0, :], ALU.subtract).then_inc(m_step, 1)
                dve.wait_ge(m_step, START + 4 * G + 2)
                dve.tensor_copy(mparts[:, 1, :], mrest[:, :]).then_inc(m_step, 1)
                dve.wait_ge(m_step, START + 4 * G + 3)
                dve.tensor_tensor(mparts[:, 2, :], mrest[:, :], mparts[:, 1, :], ALU.subtract).then_inc(m_step, 1)

            def normalise(b, q):
                G = b * QUADS + q
                dve.wait_ge(ot_turn, START + G + 1)
                o = p_pv[:, :].rearrange("p (i h r) -> p i h r", h=4, r=32)
                dve.reciprocal(osum[:, :, :], o[:, :, :, HDA]).then_inc(o_rec, 1)
                dve.wait_ge(o_rec, START + G + 1)
                dve.wait_ge(on_turn, START + b)
                dve.tensor_tensor(on[:, :, 32 * q:32 * q + 32].rearrange("p i (h d) -> p i h d", d=HDA),
                                  o[:, :, :, 0:HDA], osum[:, :, :].unsqueeze(3).broadcast_to([P, NB, 4, HDA]),
                                  ALU.mult).then_inc(on_ok, 1)

            dve.memset(qst[:, :, :, :], 0.0)
            dve.memset(kst[0:MROW, :, :, :], 0.0)
            dve.memset(kst[MROW:P, :, :, :], 1.0)
            dve.memset(p_pv[:, :], 0.0).then_inc(stacks_clear, 1)
            with dve.Fori(0, B) as b:
                dve.wait_ge(proj_a, START + b)
                dve.sem_inc(dve_gate, 1)
                dve.tensor_copy(vc[:, :, :, :], va[:, bass.ds(b * NB, NB), :, :]).then_inc(v_cur, 1)
                maxima(b, 0)
                for q in range(QUADS):
                    if q + 1 < QUADS:
                        maxima(b, q + 1)
                    normalise(b, q)
                dve.wait_ge(proj_a, START + b + 1)
                xb = x_all[:, bass.ds(b * NB, NB), :]
                dve.tensor_tensor(xb, xb, p_pv[:, :].rearrange("p (i n) -> p i n", n=P), ALU.add).then_inc(x1_ok, 1)


def deep_layers(nc, g, hT, ident, tabs, maskt, wqkv, qsc, ksc, wo, ln_g, ln_b, w1, b1, w2, b2):
    B, L, D = g.B, g.L, g.D
    NB, H, HD, CH, W, KEYS = g.blocks, g.heads, g.hd, g.chunks, g.window, g.keys
    HALF = HD // 2
    IN = g.inner
    FC = g.fchunks
    F = g.ffn
    GT = 512
    NG = L // GT
    PAIRS = H // 2
    QUADS = H // 4

    ctx = ExitStack()
    with ctx:
        def sb(name, shape, dt=F32):
            return ctx.enter_context(nc.sbuf_tensor(name, shape, dt))

        def ps(name, shape):
            return ctx.enter_context(nc.psum_tensor(name, shape, F32))

        sems = []

        def sem(name):
            sems.append(ctx.enter_context(nc.semaphore(name)))
            return sems[-1]

        wqkv_in = sb("wqkv_in", [P, 3 * IN])
        wqkv_hi = sb("wqkv_hi", [P, 3 * IN], F32R)
        wqkv_lo = sb("wqkv_lo", [P, 3 * IN], F32R)
        wo_in = sb("wo_in", [P, CH, D])
        wo_s = sb("wo_s", [P, CH, D])
        w1_in = sb("w1_in", [P, 2 * FC, P])
        w1_hi = sb("w1_hi", [P, 2 * FC, P], F32R)
        w1_lo = sb("w1_lo", [P, 2 * FC, P], F32R)
        w2_in = sb("w2_in", [P, FC, D])
        w2_s = sb("w2_s", [P, FC, D])
        vec_in = sb("vec_in", [P, 2 * FC + 3])
        vec = sb("vec", [P, 2 * FC + 3])
        scl_in = sb("scl_in", [P, 2, HD])
        rot = sb("rot", [P, 2, 2, NB, HD])
        xs_hi = sb("xs_hi", [P, L], F32R)
        xs_lo = sb("xs_lo", [P, L], F32R)
        sq = sb("sq", [P, 2, IN])
        ss = sb("ss", [P, 2, H])
        rn = sb("rn", [P, 2, H])
        nx = sb("nx", [P, 2, H])
        nxh = sb("nxh", [P, 2, H])
        nt = sb("nt", [P, 2, H])
        mroot = sb("mroot", [P, 4, GT // P])
        one = sb("one", [P, P])
        qk = sb("qk", [P, 2, IN])
        qkc = sb("qkc", [P, 2, IN])
        qks = sb("qks", [P, 2, IN])
        v_s = sb("v_s", [P, 3, IN])
        qTz = sb("qTz", [P, CH, 2, P])
        kT = sb("kT", [P, CH, W + 2 * P])
        pr = sb("pr", [P, H, KEYS])
        nmax = sb("nmax", [P, H])
        psumr = sb("psumr", [P, H])
        rsum = sb("rsum", [P, H])
        pT = sb("pT", [P, H, P])
        pTp = sb("pTp", [P, H, W])
        oT = sb("oT", [P, CH, P])
        ones = sb("ones", [P, P])
        fs = sb("fs", [P, L])
        cen = sb("cen", [P, GT])
        csq = sb("csq", [P, GT])
        rstd = sb("rstd", [P, GT])
        xn = cen
        xg = csq
        xg_hi = sb("xg_hi", [P, GT], F32R)
        xg_lo = sb("xg_lo", [P, GT], F32R)
        gl = sb("gl", [P, FC, GT])
        u = gl

        pq = ps("pq", [P, 2, 2, 512])
        psc = ps("psc", [P, 2, 512])
        ptr = ps("ptr", [P, 2, 512])

        w_in = sem("w_in")
        w_used = sem("w_used")
        w_pool = sem("w_pool")
        w_dve = sem("w_dve")
        pads = sem("pads")
        dve_gate = sem("dve_gate")
        pe_gate = sem("pe_gate")
        xs_sem = sem("xs_split")
        proj = sem("projected")
        squared = sem("squared")
        summed = sem("squares_summed")
        norm_step = sem("norm_step")
        root_step = sem("mlp_root_step")
        normed = sem("normed")
        cosd = sem("cos_done")
        sind = sem("sin_done")
        rotated = sem("rotated")
        turned = sem("turned")
        evac = sem("turn_evac")
        kcopy = sem("k_prev_copied")
        scored = sem("scored")
        maxed = sem("maxed")
        exped = sem("exped")
        recip = sem("recip")
        scaled = sem("scaled")
        pprev = sem("prev_turned")
        v_ok = sem("v_ready")
        pvd = sem("pv_done")
        o_ok = sem("o_ready")
        wod = sem("wo_done")
        resid = sem("attn_residual")
        fsh = sem("ffn_shift")
        f_mean = sem("f_mean")
        f_cen = sem("f_cen")
        f_sq = sem("f_sq")
        f_var = sem("f_var")
        f_rstd = sem("f_rstd")
        f_spread = sem("f_spread")
        f_xn = sem("f_xn")
        f_xg = sem("f_xg")
        f_hi = sem("f_hi")
        f_lo = sem("f_lo")
        f_gate = sem("f_gate")
        f_a = sem("f_a")
        f_gelu = sem("f_gelu")
        f_u = sem("f_u")
        f_out = sem("f_out")
        f_res = sem("f_res")

        block = ctx.enter_context(nc.Block())

        NVEC = 2 * FC + 3
        b1v = b1.rearrange("l (s f) -> l s f", s=2)
        LOADS = 2 + 2 * (2 + FC) + 2 + 3 + 2
        POOL_STEPS = 2 * 3 + 2

        @block.sync
        def _(sp):
            sp.wait_ge(pads, START + 1)
            with sp.Fori(0, g.depth) as l:
                sp.wait_ge(w_used, START + l * 2)
                sp.dma_start(wqkv_in[:, :], wqkv[l]).then_inc(w_in, 16)
                sp.dma_start(wo_in[:, :, :], wo[l].rearrange("(c p) n -> p c n", p=P)).then_inc(w_in, 16)
                for s in range(2):
                    full = F // P * P
                    sp.dma_start(w1_in[:, s * FC:s * FC + F // P, :],
                                 w1[l, :, s * F:s * F + full].rearrange("d (c f) -> d c f", f=P)).then_inc(w_in, 16)
                    sp.dma_start(w1_in[:, s * FC + F // P, 0:F - full],
                                 w1[l, :, s * F + full:(s + 1) * F]).then_inc(w_in, 16)
                    for c in range(FC):
                        m = min(P, F - c * P)
                        sp.dma_start(vec_in[0:m, s * FC + c:s * FC + c + 1],
                                     b1v[l, s, c * P:c * P + m].unsqueeze(1)).then_inc(w_in, 16)
                sp.dma_start(w2_in[:, 0:F // P, :],
                             w2[l, 0:F // P * P, :].rearrange("(c p) n -> p c n", p=P)).then_inc(w_in, 16)
                sp.dma_start(w2_in[0:F - F // P * P, F // P, :], w2[l, F // P * P:F, :]).then_inc(w_in, 16)
                for i, t in enumerate((ln_g, ln_b, b2)):
                    sp.dma_start(vec_in[:, 2 * FC + i:2 * FC + i + 1], t[l].unsqueeze(1)).then_inc(w_in, 16)
                for i, t in enumerate((qsc, ksc)):
                    sp.dma_start(scl_in[:, i, :], t[l].partition_broadcast(P)).then_inc(w_in, 16)

        @block.tensor
        def _(pe):
            def project(n, j, part):
                G = n * NB + j
                bank = part % 2
                if part == 0:
                    pe.wait_ge(v_ok, START + G)
                if part == 1:
                    pe.wait_ge(normed, START + 2 * G)
                    pe.wait_ge(squared, START + 2 * G)
                if part == 2:
                    pe.wait_ge(normed, START + 2 * G + 1)
                    pe.wait_ge(squared, START + 2 * G + 1)
                tok = slice(j * P, (j + 1) * P)
                for c in range(IN // 512):
                    col = slice(part * IN + c * 512, part * IN + (c + 1) * 512)
                    out = pq[:, bank, c, :]
                    pe.matmul(out, xs_hi[:, tok], wqkv_hi[:, col], start=True, stop=False)
                    pe.matmul(out, xs_hi[:, tok], wqkv_lo[:, col], start=False, stop=False)
                    mm = pe.matmul(out, xs_lo[:, tok], wqkv_hi[:, col], start=False, stop=True)
                mm.then_inc(proj, 1)

            def turn_qk(n, j):
                G = n * NB + j
                for t in range(4):
                    part, half = t // 2, t % 2
                    pe.wait_ge(rotated, START + 2 * G + part + 1)
                    if t >= 2:
                        pe.wait_ge(evac, START + 8 * G + t - 1)
                    else:
                        pe.wait_ge(evac, START + 8 * G)
                    for c in range(4):
                        s = (half * 4 + c) * P
                        mm = pe.transpose(ptr[:, t % 2, c * P:(c + 1) * P], qkc[:, part, s:s + P], ident[:, :])
                    mm.then_inc(turned, 1)

            def scores(n, j, p):
                G = n * NB + j
                if p == 0:
                    pe.wait_ge(evac, START + 8 * G + 4)
                    pe.wait_ge(kcopy, START + n * (NB // 2 - 1) + j // 2)
                    pe.wait_ge(resid, START + G)
                    pe.wait_ge(o_ok, START + 2 * G)
                if p >= 2:
                    pe.wait_ge(maxed, START + PAIRS * G + p - 1)
                k0 = (j % 2) * P
                for h in range(2):
                    if j == 0:
                        rhs = kT[:, p, W:W + P]
                        out = psc[:, p % 2, h * 256 + W:h * 256 + KEYS]
                    else:
                        rhs = kT[:, p, k0:k0 + KEYS]
                        out = psc[:, p % 2, h * 256:h * 256 + KEYS]
                    mm = pe.matmul(out, qTz[:, p, h, :], rhs, start=True, stop=True)
                mm.then_inc(scored, 1)

            def turn_p(n, j, q):
                G = n * NB + j
                pe.wait_ge(scaled, START + QUADS * G + q + 1)
                pe.wait_ge(evac, START + 8 * G + 4 + q - 1)
                for i in range(4):
                    mm = pe.transpose(ptr[:, q % 2, i * P:(i + 1) * P], pr[:, 4 * q + i, W:KEYS], ident[:, :])
                mm.then_inc(turned, 1)

            def values(n, j, q):
                G = n * NB + j
                pe.wait_ge(evac, START + 8 * G + 5 + q)
                if q == 0:
                    pe.wait_ge(v_ok, START + G + 1)
                if q % 2 == 0:
                    pe.wait_ge(maxed, START + PAIRS * G + PAIRS - 1 + q // 2)
                if j > 0:
                    pe.wait_ge(pprev, START + n * (QUADS * (NB - 1)) + QUADS * (j - 1) + q + 1)
                for i in range(4):
                    h = 4 * q + i
                    lo = 64 * (h % 2)
                    c = h // 2 % 4
                    out = psc[lo:lo + 64, q // 2, c * P:(c + 1) * P]
                    mm = pe.matmul(out, v_s[:, j % 3, h * HD:(h + 1) * HD], pT[:, h, :], start=True, stop=(j == 0))
                    if j > 0:
                        mm = pe.matmul(out[:, 0:W], v_s[:, (j - 1) % 3, h * HD:(h + 1) * HD], pTp[:, h, :],
                                       start=False, stop=True)
                if q % 2:
                    mm.then_inc(pvd, 1)

            def out_proj(n, j):
                G = n * NB + j
                for c in range(CH):
                    if c % 4 == 0:
                        pe.wait_ge(o_ok, START + 2 * G + 1 + c // 4)
                    mm = pe.matmul(psc[:, 0, 0:P], wo_s[:, c, :], oT[:, c, :], start=(c == 0), stop=(c == CH - 1))
                mm.then_inc(wod, 1)

            def mlp(n, t):
                M = n * NG + t
                if t == 0:
                    pe.wait_ge(v_ok, START + (n + 1) * NB)
                    pe.wait_ge(normed, START + 2 * NB * (n + 1))
                else:
                    pe.wait_ge(f_u, START + FC * M)
                pe.wait_ge(fsh, START + n + 1)
                pe.matmul(pq[:, 0, 0, :], ones[:, :], fs[:, t * GT:(t + 1) * GT], start=True, stop=True).then_inc(f_mean, 1)
                pe.wait_ge(f_sq, START + M + 1)
                for k in range(GT // P):
                    mm = pe.matmul(pq[:, 0, 1, k:k + 1], csq[:, k * P:(k + 1) * P], ones[:, 0:1], start=True, stop=True)
                mm.then_inc(f_var, 1)
                pe.wait_ge(f_rstd, START + M + 1)
                pe.matmul(pq[:, 0, 1, :], one[:, :], rstd[:, :], start=True, stop=True).then_inc(f_spread, 1)
                pe.wait_ge(f_lo, START + M + 1)
                for c in range(FC):
                    for s in (1, 0):
                        out = pq[:, (c + 1) % 2, 1 - s, :]
                        if c == 2:
                            pe.wait_ge(f_gelu if s else f_u, START + FC * M + 1)
                        ch = s * FC + c
                        pe.matmul(out, w1_hi[:, ch, :], xg_hi[:, :], start=True, stop=False)
                        pe.matmul(out, w1_hi[:, ch, :], xg_lo[:, :], start=False, stop=False)
                        pe.matmul(out, w1_lo[:, ch, :], xg_hi[:, :], start=False, stop=True)\
                            .then_inc(f_gate if s else f_a, 1)
                pe.wait_ge(resid, START + (n + 1) * NB)
                pe.wait_ge(f_res, START + M)
                for c in range(FC):
                    pe.wait_ge(f_u, START + FC * M + c + 1)
                    mm = pe.matmul(psc[:, 1, :], w2_s[:, c, :], u[:, c, :], start=(c == 0), stop=(c == FC - 1))
                mm.then_inc(f_out, 1)

            pe.wait_ge(pads, START + 1)
            with pe.Fori(0, g.depth) as l:
                pe.wait_ge(w_dve, START + 5 * (l + 1))
                pe.wait_ge(w_pool, START + POOL_STEPS * (l + 1))
                pe.sem_inc(pe_gate, 1)
                with pe.Fori(0, B) as b:
                    n = l * B + b
                    pe.wait_ge(xs_sem, START + 4 * n + 4)
                    for i in range(NB + 1):
                        if i < NB:
                            project(n, i, 0)
                        if i >= 1:
                            turn_qk(n, i - 1)
                            for p in range(4):
                                scores(n, i - 1, p)
                        if i < NB:
                            project(n, i, 1)
                        if i >= 1:
                            for p in range(4, 8):
                                scores(n, i - 1, p)
                        if i < NB:
                            project(n, i, 2)
                        if i >= 1:
                            for q in range(QUADS):
                                turn_p(n, i - 1, q)
                                if q:
                                    values(n, i - 1, q - 1)
                            values(n, i - 1, QUADS - 1)
                            out_proj(n, i - 1)
                    for t in range(NG):
                        mlp(n, t)

        @block.scalar
        def _(act):
            def square(n, j, part):
                G = n * NB + j
                act.wait_ge(proj, START + 3 * G + part + 1)
                if part == 0:
                    act.wait_ge(summed, START + 2 * G)
                act.activation(sq[:, part, :], pq[:, part, :, :].rearrange("p a n -> p (a n)"),
                               ACT.Square).then_inc(squared, 1)

            def keep_v(n, j):
                G = n * NB + j
                act.wait_ge(proj, START + 3 * G + 3)
                act.activation(v_s[:, j % 3, :], pq[:, 0, :, :].rearrange("p a n -> p (a n)"),
                               ACT.Copy).then_inc(v_ok, 1)

            def keep_qk(n, j):
                G = n * NB + j
                for t in range(4):
                    part, half = t // 2, t % 2
                    act.wait_ge(turned, START + 8 * G + t + 1)
                    src = ptr[:, t % 2, :].rearrange("p (c n) -> p c n", c=4)
                    if part == 0:
                        act.activation(qTz[0:64, 4 * half:4 * half + 4, 0, :], src[0:64], ACT.Copy)
                        op = act.activation(qTz[64:P, 4 * half:4 * half + 4, 1, :], src[64:P], ACT.Copy)
                    else:
                        o = W + (j % 2) * P
                        op = act.activation(kT[:, 4 * half:4 * half + 4, o:o + P], src, ACT.Copy)
                    op.then_inc(evac, 1)
                    if t == 1 and j % 2 == 0 and j > 0:
                        act.wait_ge(evac, START + 8 * G)
                        act.activation(kT[:, :, 0:W], kT[:, :, 2 * P:2 * P + W], ACT.Copy).then_inc(kcopy, 1)

            def exps(n, j, p):
                G = n * NB + j
                act.wait_ge(maxed, START + PAIRS * G + p + 1)
                if p == 0:
                    act.wait_ge(recip, START + QUADS * G)
                k0 = W if j == 0 else 0
                for h in (2 * p, 2 * p + 1):
                    op = act.activation(pr[:, h, k0:KEYS], pr[:, h, k0:KEYS], ACT.Exp, bias=nmax[:, h:h + 1],
                                        scale=-1.0, accum_out=psumr[:, h:h + 1])
                op.then_inc(exped, 1)

            def keep_p(n, j, q):
                G = n * NB + j
                act.wait_ge(turned, START + 8 * G + 5 + q)
                act.activation(pT[:, 4 * q:4 * q + 4, :].rearrange("p h n -> p (h n)"), ptr[:, q % 2, :],
                               ACT.Copy).then_inc(evac, 1)

            def keep_o(n, j, c):
                G = n * NB + j
                act.wait_ge(pvd, START + 2 * G + c + 1)
                act.activation(oT[:, 4 * c:4 * c + 4, :].rearrange("p h n -> p (h n)"), psc[:, c, :],
                               ACT.Copy).then_inc(o_ok, 1)

            def mlp(n, t):
                M = n * NG + t
                act.wait_ge(f_cen, START + M + 1)
                act.activation(csq[:, :], cen[:, :], ACT.Square).then_inc(f_sq, 1)
                act.wait_ge(f_xn, START + M + 1)
                act.activation(xg[:, :], xn[:, :], ACT.Identity, bias=vec[:, 2 * FC + 1:2 * FC + 2],
                               scale=vec[:, 2 * FC:2 * FC + 1]).then_inc(f_xg, 1)
                for c in range(FC):
                    act.wait_ge(f_gate, START + FC * M + c + 1)
                    act.activation(gl[:, c, :], pq[:, (c + 1) % 2, 0, :], ACT.Gelu,
                                   bias=vec[:, FC + c:FC + c + 1]).then_inc(f_gelu, 1)

            act.wait_ge(pads, START + 1)
            with act.Fori(0, g.depth) as l:
                act.wait_ge(w_dve, START + 5 * (l + 1))
                with act.Fori(0, B) as b:
                    n = l * B + b
                    for i in range(NB + 1):
                        if i >= 1:
                            keep_qk(n, i - 1)
                        if i < NB:
                            square(n, i, 0)
                        if i >= 1:
                            for p in range(4):
                                exps(n, i - 1, p)
                        if i < NB:
                            square(n, i, 1)
                        if i >= 1:
                            for p in range(4, 8):
                                exps(n, i - 1, p)
                        if i < NB:
                            keep_v(n, i)
                        if i >= 1:
                            for q in range(QUADS):
                                keep_p(n, i - 1, q)
                                if q == 2:
                                    keep_o(n, i - 1, 0)
                            keep_o(n, i - 1, 1)
                    for t in range(NG):
                        mlp(n, t)

        @block.vector
        def _(dve):
            def sums(n, j, part):
                G = n * NB + j
                dve.wait_ge(squared, START + 2 * G + part + 1)
                dve.tensor_reduce(ss[:, part, :], sq[:, part, :].rearrange("p (h d) -> p h d", d=HD), X, ALU.add)\
                    .then_inc(summed, 1)

            def norms(n, j):
                G = n * NB + j
                dve.wait_ge(summed, START + 2 * G + 2)
                flat = [t[:, :, :].rearrange("p a h -> p (a h)") for t in (rn, nx, nxh, nt, ss)]
                inverse_root(dve, *flat, 1e-24, ALU.max, norm_step, ROOT * G)

            def norm(n, j, part):
                G = n * NB + j
                dve.wait_ge(sind, START + 2 * G + part - 1 + 0) if part else dve.wait_ge(sind, START + 2 * G)
                dve.tensor_tensor(qk[:, part, :].rearrange("p (h d) -> p h d", d=HD),
                                  pq[:, part, :, :].rearrange("p a (h d) -> p (a h) d", d=HD),
                                  rn[:, part, :].unsqueeze(2).broadcast_to([P, H, HD]), ALU.mult).then_inc(normed, 1)

            def times_cos(n, j, part):
                G = n * NB + j
                dve.wait_ge(normed, START + 2 * G + part + 1)
                dve.wait_ge(turned, START + 8 * G - 8 + 2 * (part + 1)) if j > 0 else None
                dve.tensor_tensor(qkc[:, part, :].rearrange("p (h d) -> p h d", d=HD),
                                  qk[:, part, :].rearrange("p (h d) -> p h d", d=HD),
                                  rot[:, part, 0, j, :].unsqueeze(1).broadcast_to([P, H, HD]), ALU.mult).then_inc(cosd, 1)

            def add_sin(n, j, part):
                G = n * NB + j
                dve.wait_ge(cosd, START + 2 * G + part + 1)
                dve.wait_ge(sind, START + 2 * G + part + 1)
                dve.tensor_tensor(qkc[:, part, :], qkc[:, part, :], qks[:, part, :], ALU.add).then_inc(rotated, 1)

            def smax(n, j, p):
                G = n * NB + j
                dve.wait_ge(scored, START + PAIRS * G + p + 1)
                k0 = W if j == 0 else 0
                dve.sem_inc(dve_gate, 1)
                for h in range(2):
                    op = dve.tensor_tensor_reduce(pr[:, 2 * p + h, k0:KEYS], psc[:, p % 2, h * 256 + k0:h * 256 + KEYS],
                                                  maskt[:, k0:KEYS], -1.0, 3e38, ALU.add, ALU.min,
                                                  nmax[:, 2 * p + h:2 * p + h + 1])
                op.then_inc(maxed, 1)

            def reciprocal(n, j, q):
                G = n * NB + j
                dve.wait_ge(exped, START + PAIRS * G + 2 * q + 2)
                if q == 0:
                    dve.wait_ge(scaled, START + QUADS * G)
                dve.reciprocal(rsum[:, 4 * q:4 * q + 4], psumr[:, 4 * q:4 * q + 4]).then_inc(recip, 1)

            def prev_turn(n, j, q):
                G = n * NB + j
                dve.wait_ge(scaled, START + QUADS * G + q + 1)
                if q == 0:
                    dve.wait_ge(pvd, START + 2 * G)
                dve.transpose(pTp[P - W:P, 4 * q:4 * q + 4, :], pr[0:W, 4 * q:4 * q + 4, 0:W]).then_inc(pprev, 1)

            def residual(n, b, j):
                G = n * NB + j
                dve.wait_ge(wod, START + G + 1)
                dve.tensor_tensor(hT[:, b, 1 + j * P:1 + (j + 1) * P], hT[:, b, 1 + j * P:1 + (j + 1) * P],
                                  psc[:, 0, 0:P], ALU.add).then_inc(resid, 1)

            def shifted(n, b):
                dve.wait_ge(f_res, START + NG * n)
                dve.sem_inc(dve_gate, 1)
                for s in range(2):
                    lo, off = 64 * s, 1 - s
                    dve.tensor_copy(xs_hi[lo:lo + 64, :], hT[lo:lo + 64, b, off:off + L]).then_inc(xs_sem, 1)
                dve.wait_ge(xs_sem, START + 4 * n + 2)
                for s in range(2):
                    lo, off = 64 * s, 1 - s
                    dve.tensor_tensor(xs_lo[lo:lo + 64, :], hT[lo:lo + 64, b, off:off + L],
                                      xs_hi[lo:lo + 64, :].bitcast(F32), ALU.subtract).then_inc(xs_sem, 1)

            def mlp(n, b, t):
                M = n * NG + t
                tok = slice(t * GT, (t + 1) * GT)
                dve.wait_ge(f_mean, START + M + 1)
                dve.tensor_tensor(cen[:, :], fs[:, tok], pq[:, 0, 0, :], ALU.subtract).then_inc(f_cen, 1)
                dve.wait_ge(f_var, START + M + 1)
                inverse_root(dve, mroot[:, 0, :], mroot[:, 1, :], mroot[:, 2, :], mroot[:, 3, :],
                             pq[:, 0, 1, 0:GT // P], 1e-5, ALU.add, root_step, ROOT * M)
                for k in range(GT // P):
                    op = dve.tensor_scalar(rstd[:, k * P:(k + 1) * P], ident[:, :], mroot[:, 0, k:k + 1], None, ALU.mult)
                op.then_inc(f_rstd, 1)
                dve.wait_ge(f_spread, START + M + 1)
                dve.wait_ge(f_cen, START + M + 1)
                dve.wait_ge(f_sq, START + M + 1)
                dve.tensor_tensor(xn[:, :], cen[:, :], pq[:, 0, 1, :], ALU.mult).then_inc(f_xn, 1)
                dve.wait_ge(f_xg, START + M + 1)
                dve.tensor_copy(xg_hi[:, :], xg[:, :]).then_inc(f_hi, 1)
                dve.wait_ge(f_hi, START + M + 1)
                dve.tensor_tensor(xg_lo[:, :], xg[:, :], xg_hi[:, :].bitcast(F32), ALU.subtract).then_inc(f_lo, 1)
                for c in range(FC):
                    dve.wait_ge(f_a, START + FC * M + c + 1)
                    dve.wait_ge(f_gelu, START + FC * M + c + 1)
                    dve.scalar_tensor_tensor(u[:, c, :], pq[:, (c + 1) % 2, 1, :], vec[:, c:c + 1], gl[:, c, :],
                                             ALU.add, ALU.mult).then_inc(f_u, 1)
                dve.wait_ge(f_out, START + M + 1)
                h = hT[:, b, 1 + t * GT:1 + (t + 1) * GT]
                dve.scalar_tensor_tensor(h, psc[:, 1, :], vec[:, 2 * FC + 2:2 * FC + 3], h,
                                         ALU.add, ALU.add).then_inc(f_res, 1)

            dve.memset(hT[:, :, 0:1], 0.0)
            dve.memset(ones[:, :], 1.0 / D)
            dve.memset(one[:, :], 1.0)
            dve.memset(qTz[:, :, :, :], 0.0)
            dve.memset(pTp[:, :, :], 0.0)
            dve.memset(w1_in[:, :, :], 0.0)
            dve.memset(w2_in[:, :, :], 0.0)
            dve.memset(vec_in[:, :], 0.0).then_inc(pads, 1)
            dve.wait_ge(pads, START + 1)
            with dve.Fori(0, g.depth) as l:
                dve.wait_ge(w_in, START + 16 * LOADS * (l + 1))
                dve.wait_ge(f_out, START + NG * B * l)
                dve.tensor_copy(wqkv_hi[:, :], wqkv_in[:, :]).then_inc(w_dve, 1)
                dve.tensor_copy(w1_hi[:, :, :], w1_in[:, :, :]).then_inc(w_dve, 1)
                dve.wait_ge(w_dve, START + 5 * l + 1)
                dve.tensor_tensor(wqkv_lo[:, :], wqkv_in[:, :], wqkv_hi[:, :].bitcast(F32), ALU.subtract).then_inc(w_dve, 1)
                dve.wait_ge(w_dve, START + 5 * l + 2)
                dve.tensor_tensor(w1_lo[:, :, :], w1_in[:, :, :], w1_hi[:, :, :].bitcast(F32), ALU.subtract).then_inc(w_dve, 1)
                dve.tensor_copy(vec[:, :], vec_in[:, :]).then_inc(w_dve, 1)
                dve.wait_ge(w_dve, START + 5 * l + 5)
                dve.sem_inc(w_used, 1)
                dve.wait_ge(w_pool, START + POOL_STEPS * (l + 1))
                dve.sem_inc(dve_gate, 1)
                with dve.Fori(0, B) as b:
                    n = l * B + b
                    shifted(n, b)
                    for i in range(NB + 1):
                        if i >= 1:
                            for p in range(4):
                                smax(n, i - 1, p)
                        if i < NB:
                            sums(n, i, 0)
                        if i >= 1:
                            for p in range(4, 8):
                                smax(n, i - 1, p)
                            for q in range(2):
                                reciprocal(n, i - 1, q)
                        if i < NB:
                            sums(n, i, 1)
                            norms(n, i)
                            norm(n, i, 0)
                            norm(n, i, 1)
                        if i >= 1:
                            for q in range(2, QUADS):
                                reciprocal(n, i - 1, q)
                            if i - 1 > 0:
                                for q in range(2):
                                    prev_turn(n, i - 1, q)
                        if i < NB:
                            times_cos(n, i, 0)
                        if i - 1 > 0:
                            for q in range(2, QUADS):
                                prev_turn(n, i - 1, q)
                        if i < NB:
                            add_sin(n, i, 0)
                            times_cos(n, i, 1)
                            add_sin(n, i, 1)
                        if i >= 1:
                            residual(n, b, i - 1)
                    dve.wait_ge(resid, START + (n + 1) * NB)
                    dve.sem_inc(dve_gate, 1)
                    dve.tensor_copy(fs[0:64, :], hT[0:64, b, 1:1 + L])
                    dve.tensor_copy(fs[64:P, :], hT[64:P, b, 0:L]).then_inc(fsh, 1)
                    for t in range(NG):
                        mlp(n, b, t)

        @block.gpsimd
        def _(pool):
            start_all(pool, sems)

            def scale_p(n, j, q):
                G = n * NB + j
                pool.wait_ge(recip, START + QUADS * G + q + 1)
                pool.wait_ge(exped, START + PAIRS * G + 2 * q + 2)
                k0 = W if j == 0 else 0
                v = pr[:, 4 * q:4 * q + 4, k0:KEYS]
                pool.tensor_tensor(v, v, rsum[:, 4 * q:4 * q + 4].unsqueeze(2).broadcast_to([P, 4, KEYS - k0]),
                                   ALU.mult).then_inc(scaled, 1)

            def times_sin(n, j, part):
                G = n * NB + j
                pool.wait_ge(normed, START + 2 * G + part + 1)
                pool.wait_ge(rotated, START + 2 * G + part - 1) if part else pool.wait_ge(rotated, START + 2 * G)
                src = qk[:, part, :].rearrange("p (h s d) -> p h s d", s=2, d=HALF)
                dst = qks[:, part, :].rearrange("p (h s d) -> p h s d", s=2, d=HALF)
                for s in range(2):
                    t = rot[:, part, 1, j, s * HALF:(s + 1) * HALF].unsqueeze(1).broadcast_to([P, H, HALF])
                    op = pool.tensor_tensor(dst[:, :, s, :], src[:, :, 1 - s, :], t, ALU.mult)
                op.then_inc(sind, 1)

            pool.wait_ge(pads, START + 1)
            with pool.Fori(0, g.depth) as l:
                pool.wait_ge(w_in, START + 16 * LOADS * (l + 1))
                pool.wait_ge(f_out, START + NG * B * l)
                pool.wait_ge(rotated, START + 2 * NB * B * l)
                for i in range(2):
                    s = scl_in[:, i, :].rearrange("p (s d) -> p s d", s=2)
                    pool.tensor_tensor(rot[:, i, 0, :, :], tabs[:, i, 0, :, :],
                                       scl_in[:, i, :].unsqueeze(1).broadcast_to([P, NB, HD]),
                                       ALU.mult).then_inc(w_pool, 1)
                    for a in range(2):
                        o = slice(a * HALF, (a + 1) * HALF)
                        pool.tensor_tensor(rot[:, i, 1, :, o], tabs[:, i, 1, :, o],
                                           s[:, 1 - a, :].unsqueeze(1).broadcast_to([P, NB, HALF]),
                                           ALU.mult).then_inc(w_pool, 1)
                pool.tensor_copy(wo_s[:, :, :], wo_in[:, :, :]).then_inc(w_pool, 1)
                pool.tensor_copy(w2_s[:, :, :], w2_in[:, :, :]).then_inc(w_pool, 1)
                pool.wait_ge(w_pool, START + POOL_STEPS * (l + 1))
                pool.sem_inc(w_used, 1)
                with pool.Fori(0, B) as b:
                    n = l * B + b
                    for i in range(NB + 1):
                        if i < NB:
                            times_sin(n, i, 0)
                        if i >= 1:
                            for q in range(2):
                                scale_p(n, i - 1, q)
                        if i < NB:
                            times_sin(n, i, 1)
                        if i >= 1:
                            for q in range(2, QUADS):
                                scale_p(n, i - 1, q)


def finish(nc, g, hT, ident, x1_d, out):
    GT = 4 * P
    PER = g.L // GT
    GROUPS = g.B * PER
    ctx = ExitStack()
    with ctx:
        x1 = ctx.enter_context(nc.sbuf_tensor("x1_back", [P, GROUPS, GT], F32))
        p_out = ctx.enter_context(nc.psum_tensor("p_out", [P, 2, GT], F32))
        loaded = ctx.enter_context(nc.semaphore("x1_loaded"))
        turned = ctx.enter_context(nc.semaphore("h_turned"))
        summed = ctx.enter_context(nc.semaphore("out_summed"))
        stored = ctx.enter_context(nc.semaphore("out_stored"))
        block = ctx.enter_context(nc.Block())

        @block.sync
        def _(sp):
            sp.dma_start(x1[:, :, :].rearrange("p g n -> p (g n)"), x1_d.rearrange("p k d -> p (k d)")).then_inc(loaded, 16)
            for t in range(GROUPS):
                b, h = t // PER, t % PER
                sp.wait_ge(summed, t + 1)
                sp.dma_start(out[b, h * GT:(h + 1) * GT, :].rearrange("(k p) d -> p k d", p=P),
                             x1[:, t, :].rearrange("p (k d) -> p k d", d=P)).then_inc(stored, 16)
            sp.wait_ge(stored, 16 * GROUPS)

        @block.tensor
        def _(pe):
            for t in range(GROUPS):
                if t >= 2:
                    pe.wait_ge(summed, t - 1)
                for k in range(4):
                    o = 1 + (t % PER) * GT + k * P
                    mm = pe.transpose(p_out[:, t % 2, k * P:(k + 1) * P], hT[:, t // PER, o:o + P], ident[:, :])
                mm.then_inc(turned, 1)

        @block.vector
        def _(dve):
            dve.wait_ge(loaded, 16)
            for t in range(GROUPS):
                dve.wait_ge(turned, t + 1)
                dve.tensor_tensor(x1[:, t, :], x1[:, t, :], p_out[:, t % 2, :], ALU.add).then_inc(summed, 1)


def build(nc, x, q_w, k_w, v_w, o_w, wqkv, qsc, ksc, wo, ln_g, ln_b, w1, b1, w2, b2,
          identity, identity_b, causal, bias, window_mask, rotary, out):
    g = Geometry(x, wqkv, qsc, w1, wo)
    parts_d = nc.dram_tensor("qk_parts", [g.B, 2, 3, g.D, g.L], BF16, kind="Internal").ap()
    x1_d = nc.dram_tensor("x1_kept", [P, g.B * g.blocks, g.D], F32, kind="Internal").ap()
    ctx = ExitStack()
    with ctx:
        def sb(name, shape, dt=F32):
            return ctx.enter_context(nc.sbuf_tensor(name, shape, dt))

        hT = sb("h_t", [P, g.B, 1 + g.L])
        ident = sb("ident", [P, P])
        identb = sb("ident_b", [P, P], BF16)
        cmask = sb("causal_mask", [P, P], BF16)
        maskt = sb("window_mask_s", [P, g.keys])
        consts = ctx.enter_context(nc.semaphore("consts"))
        with nc.Block() as block:
            @block.sync
            def _(sp):
                for dst, src in ((ident, identity), (identb, identity_b), (cmask, causal), (maskt, window_mask)):
                    sp.dma_start(dst[:, :], src).then_inc(consts, 16)
                sp.wait_ge(consts, 64)
        with ExitStack() as first:
            x_all = first.enter_context(nc.sbuf_tensor("x_all", [P, g.B * g.blocks, g.D], F32))
            va = first.enter_context(nc.sbuf_tensor("v_all", [P, g.B * g.blocks, g.a_heads, g.a_hd + 1], F32))
            prepare(nc, g, x_all, va, ident, x, q_w, k_w, v_w, parts_d)
            causal_attention(nc, g, x_all, va, ident, identb, cmask, o_w, parts_d, bias)
            hand_over(nc, g, x_all, hT, ident, x1_d)
        with ExitStack() as second:
            tabs = second.enter_context(nc.sbuf_tensor("rotary_s", [P, 2, 2, g.blocks, g.hd], F32))
            got = second.enter_context(nc.semaphore("rotary_in"))
            with nc.Block() as block:
                @block.sync
                def _(sp):
                    sp.dma_start(tabs[:, :, :, :, :], rotary).then_inc(got, 16)
                    sp.wait_ge(got, 16)
            deep_layers(nc, g, hT, ident, tabs, maskt, wqkv, qsc, ksc, wo, ln_g, ln_b, w1, b1, w2, b2)
        finish(nc, g, hT, ident, x1_d, out)


def _split3(a):
    bf = _bf16()
    h = a.astype(bf)
    m = (a - h.astype(np.float32)).astype(bf)
    low = (a - h.astype(np.float32) - m.astype(np.float32)).astype(bf)
    return [h, m, low]


def _bf16():
    return np.dtype("bfloat16")


def _alibi_rows(heads, length):
    ratio = 2.0 ** (-8.0 / heads)
    slopes = np.asarray([ratio ** (i + 1) for i in range(heads)], np.float32)
    pos = np.arange(length)
    at = [(pos // 8 * 8).astype(np.float32), (pos % 8).astype(np.float32)]
    rows = np.zeros((heads, 2, 12, length), _bf16())
    for n, s in enumerate(_split3(slopes)):
        for k in range(2):
            rows[:, 0, 2 * n + k] = s[:, None]
            rows[:, 1, 2 * n + k] = at[k]
            rows[:, 0, 6 + 2 * n + k] = at[k]
            rows[:, 1, 6 + 2 * n + k] = -s[:, None]
    return rows


def _rotary(length, hd, window, qk_scale):
    half = np.arange(0, hd, 2, dtype=np.float32)
    freq = (1.0 / 10000.0 ** (half / hd)).astype(np.float32)
    t = np.arange(length, dtype=np.float32)
    angle = np.tile(t[:, None] * freq[None, :], (1, 2)).astype(np.float64)
    base = ((half + 0.4 * hd) / (1.4 * hd)).astype(np.float64)
    scale = np.tile(base[None, :] ** ((t - length // 2) / (window // 2))[:, None], (1, 2))
    sign = np.repeat([-1.0, 1.0], hd // 2)
    c, s = np.cos(angle), np.sin(angle) * sign
    t4 = np.stack([np.stack([c * scale, s * scale]) * qk_scale, np.stack([c / scale, s / scale])])
    return np.ascontiguousarray(t4.reshape(2, 2, length // P, P, hd).transpose(3, 0, 1, 2, 4).astype(np.float32))


def _window_mask(window):
    q = np.arange(P)[:, None]
    k = np.arange(P + window)[None, :] - window
    seen = (k <= q) & (k >= q - window)
    return np.where(seen, 0.0, MASKED).astype(np.float32)


def kernel(**inputs):
    import concourse.bacc as _bacc
    from concourse.bass_utils import run_bass_kernel_spmd as _run

    nc = _bacc.Bacc("TRN2", target_bir_lowering=False, num_devices=1)
    names = ["L0_attn_x", "L0_attn_q_w", "L0_attn_k_w", "L0_attn_v_w", "L0_attn_o_w", "L0_ffn_Wqkv",
             "L0_ffn_q_scale", "L0_ffn_k_scale", "L0_ffn_Wo", "L0_ffn_ln_g", "L0_ffn_ln_b", "L0_ffn_W1",
             "L0_ffn_b1", "L0_ffn_W2", "L0_ffn_b2"]
    arrays = {f"in_{n}": np.ascontiguousarray(inputs[n]) for n in names}
    length = arrays["in_L0_attn_x"].shape[1]
    bf = _bf16()
    causal = np.where(np.arange(P)[None, :] > np.arange(P)[:, None], -1e30, 0.0)
    arrays |= {
        "c_identity": np.eye(P, dtype=np.float32),
        "c_identity_b": np.eye(P, dtype=np.float32).astype(bf),
        "c_causal": causal.astype(np.float32).astype(bf),
        "c_bias": _alibi_rows(16, length),
        "c_window": _window_mask(32),
        "c_rotary": _rotary(length, arrays["in_L0_ffn_q_scale"].shape[1], 32, 8.0),
    }
    args = [nc.dram_tensor(n, a.shape, mybir.dt.from_np(a.dtype), kind="ExternalInput").ap() for n, a in arrays.items()]
    shape = arrays["in_L0_attn_x"].shape
    args.append(nc.dram_tensor("out_0", shape, F32, kind="ExternalOutput").ap())
    build(nc, *args)
    r = _run(nc, [arrays], core_ids=[0])
    return r.results[0]["out_0"]
```

```python
import numpy as np
import concourse.bass as bass
from concourse import mybir
from contextlib import ExitStack

F32 = mybir.dt.float32
F32R = mybir.dt.float32r
BF16 = mybir.dt.bfloat16
ALU = mybir.AluOpType
ACT = mybir.ActivationFunctionType
X = mybir.AxisListType.X

P = 128
MASKED = -1e26
ROOT = 12
I32 = mybir.dt.int32


class Geometry:

    def __init__(self, x, wqkv, q_scale, w1, wo):
        self.B, self.L, self.D = x.shape
        self.depth = wqkv.shape[0]
        self.inner = wqkv.shape[2] // 3
        self.hd = q_scale.shape[1]
        self.heads = self.inner // self.hd
        self.ffn = w1.shape[2] // 2
        self.blocks = self.L // P
        self.window = 32
        self.keys = P + self.window
        self.chunks = self.inner // P
        self.fchunks = -(-self.ffn // P)
        self.a_heads, self.a_hd = 16, self.D // 16


START = 1


def start_all(eng, sems):
    for s in sems:
        eng.sem_inc(s, START)


def inverse_root(dve, y, x, xh, t, source, floor, op, step, base):
    dve.tensor_scalar(x, source, floor, None, op).then_inc(step, 1)
    dve.wait_ge(step, START + base + 1)
    dve.tensor_scalar(y.bitcast(I32), x.bitcast(I32), -0.5, float(0x5f3759df), ALU.mult, ALU.add).then_inc(step, 1)
    dve.tensor_scalar(xh, x, -0.5, None, ALU.mult).then_inc(step, 1)
    dve.wait_ge(step, START + base + 3)
    for k in range(3):
        dve.tensor_tensor(t, y, y, ALU.mult).then_inc(step, 1)
        dve.wait_ge(step, START + base + 4 + 3 * k)
        dve.tensor_tensor(t, t, xh, ALU.mult).then_inc(step, 1)
        dve.wait_ge(step, START + base + 5 + 3 * k)
        dve.scalar_tensor_tensor(y, t, 1.5, y, ALU.add, ALU.mult).then_inc(step, 1)
        dve.wait_ge(step, START + base + 6 + 3 * k)


class TokenNorm:

    GROUP = 4

    def __init__(self, nc, ctx, name, x_all, ident, turned_ps):
        def sb(part, shape):
            return ctx.enter_context(nc.sbuf_tensor(f"{name}_{part}", shape, F32))

        self.sems = []

        def sem(part):
            self.sems.append(ctx.enter_context(nc.semaphore(f"{name}_{part}")))
            return self.sems[-1]
        n = self.GROUP
        self.x_all, self.ident, self.ps = x_all, ident, turned_ps
        self.stats, self.mv = sb("stats", [P, n, 6]), sb("mv", [P, n, 2])
        self.root = sb("root", [P, 4, n])
        self.xn = sb("xn", [P, n, P])
        self.stat_step, self.root_step = sem("stat_step"), sem("root_step")
        self.normed, self.turned = sem("normed"), sem("turned")
        self.gate = sem("gate")

    def vector(self, dve, t):
        n = self.GROUP
        for k in range(n):
            dve.bn_stats(self.stats[:, k, :], self.x_all[:, t * n + k, :]).then_inc(self.stat_step, 1)
        dve.wait_ge(self.stat_step, START + 2 * n * t + n)
        dve.sem_inc(self.gate, 1)
        for k in range(n):
            dve.bn_aggr(self.mv[:, k, :], self.stats[:, k, :]).then_inc(self.stat_step, 1)
        dve.wait_ge(self.stat_step, START + 2 * n * (t + 1))
        r = self.root
        inverse_root(dve, r[:, 0, :], r[:, 1, :], r[:, 2, :], r[:, 3, :], self.mv[:, :, 1], 1e-5, ALU.add,
                     self.root_step, ROOT * t)
        dve.wait_ge(self.turned, START + t)
        for k in range(n):
            dve.tensor_scalar(self.xn[:, k, :], self.x_all[:, t * n + k, :], self.mv[:, k, 0:1],
                              r[:, 0, k:k + 1], ALU.subtract, ALU.mult).then_inc(self.normed, 1)

    def tensor(self, pe, t):
        n = self.GROUP
        pe.wait_ge(self.normed, START + n * (t + 1))
        for k in range(n):
            mm = pe.transpose(self.ps[:, k * P:(k + 1) * P], self.xn[:, k, :], self.ident[:, :])
        mm.then_inc(self.turned, 1)


def prepare(nc, g, x_all, va, ident, x, q_w, k_w, v_w, parts_d):
    B, L, D = g.B, g.L, g.D
    HA, HDA = g.a_heads, g.a_hd
    GT = 4 * P
    GROUPS = B * L // GT
    PER = L // GT
    ctx = ExitStack()
    with ctx:
        def sb(name, shape, dt=F32):
            return ctx.enter_context(nc.sbuf_tensor(name, shape, dt))

        def ps(name, shape):
            return ctx.enter_context(nc.psum_tensor(name, shape, F32))

        sems = []

        def sem(name):
            sems.append(ctx.enter_context(nc.semaphore(name)))
            return sems[-1]

        w = sb("w_qkv_a", [P, 3, D])
        xnT = sb("xnT", [P, GT])
        qkf = sb("qkf", [P, 2, GT])
        rest = sb("rest", [P, 2, GT])
        parts = sb("parts", [P, 2, 3, GT], BF16)
        p_turn = ps("p_turn", [P, GT])
        p_qk = ps("p_qk", [P, 2, GT])
        p_v = ps("p_v", [P, GT])
        x_in = sem("x_in")
        w_in = sem("a_w_in")
        xnT_ok = sem("xnT_ok")
        qk_done = sem("a_qk_done")
        v_done = sem("a_v_done")
        qkf_ok = sem("qkf_ok")
        va_ok = sem("va_ok")
        va_pad = sem("va_pad")
        split = sem("split_step")
        stored = sem("parts_stored")
        ln = TokenNorm(nc, ctx, "ln_a", x_all, ident, p_turn)
        block = ctx.enter_context(nc.Block())

        @block.gpsimd
        def _(pool):
            start_all(pool, sems + ln.sems)

        @block.sync
        def _(sp):
            for b in range(B):
                n = L // P
                sp.dma_start(x_all[:, b * n:(b + 1) * n, :], x[b].rearrange("(k p) d -> p k d", p=P)).then_inc(x_in, 16)
            for i, t in enumerate((q_w, k_w, v_w)):
                sp.dma_start(w[:, i, :], t).then_inc(w_in, 16)
            with sp.Fori(0, B) as b:
                for h in range(PER):
                    t = b * PER + h
                    sp.wait_ge(split, START + 8 * (t + 1))
                    for i in range(2):
                        sp.dma_start(parts_d[b, i, :, :, h * GT:(h + 1) * GT].rearrange("s p n -> p s n"),
                                     parts[:, i, :, :]).then_inc(stored, 16)
            sp.wait_ge(stored, START + 32 * GROUPS)

        @block.tensor
        def _(pe):
            pe.wait_ge(w_in, START + 48)
            with pe.Fori(0, GROUPS) as t:
                ln.tensor(pe, t)
                pe.wait_ge(xnT_ok, START + t + 1)
                pe.wait_ge(qkf_ok, START + t * 2)
                pe.wait_ge(va_ok, START + t)
                for i in range(2):
                    pe.matmul(p_qk[:, i, :], w[:, i, :], xnT[:, :], start=True, stop=True).then_inc(qk_done, 1)
                for k in range(4):
                    mm = pe.matmul(p_v[:, k * P:(k + 1) * P], xnT[:, k * P:(k + 1) * P], w[:, 2, :], start=True, stop=True)
                mm.then_inc(v_done, 1)

        @block.scalar
        def _(act):
            act.wait_ge(va_pad, START + 1)
            with act.Fori(0, GROUPS) as t:
                act.wait_ge(ln.turned, START + t + 1)
                act.wait_ge(v_done, START + t)
                act.activation(xnT[:, :], p_turn[:, :], ACT.Copy).then_inc(xnT_ok, 1)
                act.wait_ge(split, START + 8 * t)
                for i in range(2):
                    act.wait_ge(qk_done, START + 2 * t + i + 1)
                    act.activation(qkf[:, i, :], p_qk[:, i, :], ACT.Copy,
                                   scale=1.0 / float(np.sqrt(HDA)) if i == 0 else 1.0).then_inc(qkf_ok, 1)
                act.wait_ge(v_done, START + t + 1)
                act.activation(va[:, bass.ds(t * 4, 4), :, 0:HDA],
                               p_v[:, :].rearrange("p (k h d) -> p k h d", k=4, d=HDA), ACT.Copy).then_inc(va_ok, 1)

        @block.vector
        def _(dve):
            dve.memset(va[:, :, :, :], 1.0).then_inc(va_pad, 1)
            dve.wait_ge(x_in, START + 16 * B)
            with dve.Fori(0, GROUPS) as t:
                ln.vector(dve, t)
                dve.wait_ge(stored, START + 32 * t)
                for i in range(2):
                    dve.wait_ge(qkf_ok, START + 2 * t + i + 1)
                    at = 8 * t + 4 * i
                    dve.tensor_copy(parts[:, i, 0, :], qkf[:, i, :]).then_inc(split, 1)
                    dve.wait_ge(split, START + at + 1)
                    dve.tensor_tensor(rest[:, i, :], qkf[:, i, :], parts[:, i, 0, :], ALU.subtract).then_inc(split, 1)
                    dve.wait_ge(split, START + at + 2)
                    dve.tensor_copy(parts[:, i, 1, :], rest[:, i, :]).then_inc(split, 1)
                    dve.wait_ge(split, START + at + 3)
                    dve.tensor_tensor(parts[:, i, 2, :], rest[:, i, :], parts[:, i, 1, :], ALU.subtract).then_inc(split, 1)


def hand_over(nc, g, x_all, hT, ident, x1_d):
    GT = 4 * P
    PER = g.L // GT
    ctx = ExitStack()
    with ctx:
        p_turn = ctx.enter_context(nc.psum_tensor("p_turn2", [P, GT], F32))
        kept = ctx.enter_context(nc.semaphore("hT_kept"))
        stored = ctx.enter_context(nc.semaphore("x1_stored"))
        ln = TokenNorm(nc, ctx, "ln_b", x_all, ident, p_turn)
        block = ctx.enter_context(nc.Block())

        @block.gpsimd
        def _(pool):
            start_all(pool, [kept, stored] + ln.sems)

        @block.sync
        def _(sp):
            sp.dma_start(x1_d, x_all[:, :, :]).then_inc(stored, 16)
            sp.wait_ge(stored, START + 16)

        @block.vector
        def _(dve):
            with dve.Fori(0, g.B * PER) as t:
                ln.vector(dve, t)

        @block.tensor
        def _(pe):
            with pe.Fori(0, g.B * PER) as t:
                pe.wait_ge(kept, START + t)
                ln.tensor(pe, t)

        @block.scalar
        def _(act):
            with act.Fori(0, g.B) as b:
                for h in range(PER):
                    act.wait_ge(ln.turned, START + b * PER + h + 1)
                    act.activation(hT[:, b, 1 + h * GT:1 + (h + 1) * GT], p_turn[:, :], ACT.Copy).then_inc(kept, 1)


def causal_attention(nc, g, x_all, va, ident, identb, cmask, o_w, parts_d, bias_d):
    B, L, D = g.B, g.L, g.D
    HA, HDA = g.a_heads, g.a_hd
    NB = L // P
    QUADS = HA // 4
    ROWS = 9 * HDA
    MROW = 96
    PIECES = [(I, c, min(c + 512, P * (I + 1))) for I in range(NB) for c in range(0, P * (I + 1), 512)]
    PACKS = [[(0, 0)], [(1, 0), (7, 7 * P)], [(2, 0), (6, 6 * P)], [(3, 0), (5, 5 * P)], [(4, 0)]]
    NP = len(PACKS)
    ctx = ExitStack()
    with ctx:
        def sb(name, shape, dt=F32):
            return ctx.enter_context(nc.sbuf_tensor(name, shape, dt))

        def ps(name, shape):
            return ctx.enter_context(nc.psum_tensor(name, shape, F32))

        sems = []

        def sem(name):
            sems.append(ctx.enter_context(nc.semaphore(name)))
            return sems[-1]

        qst = sb("q_stack", [P, 2, 4, L], BF16)
        kst = sb("k_stack", [P, 2, 4, L], BF16)
        pt = sb("p_t", [P, 3, 4, L])
        vc = sb("v_cur", [P, NB, HA, HDA + 1])
        mx = sb("mx", [P, 2, 4, NB])
        mrow = sb("mrow", [32, P])
        mrest = sb("mrest", [32, P])
        mparts = sb("mparts", [32, 3, P], BF16)
        ot = sb("ot", [P, L])
        osum = sb("osum", [P, NB, 4])
        on = sb("on", [P, NB, D])
        onT = sb("onT", [P, L])
        wo = sb("wo_a", [P, D])
        p_max = ps("p_max", [P, 2, 512])
        p_exp = ps("p_exp", [P, 2, L])
        p_pv = ps("p_pv", [P, L])

        stacks_clear = sem("stacks_clear")
        wo_in = sem("wo_a_in")
        stacked = [sem("stacked0"), sem("stacked1")]
        maxed = sem("max_scores")
        m_read = sem("max_read")
        m_all = sem("max_merged")
        m_turn = sem("max_turned")
        m_step = sem("max_split_step")
        m_rows = sem("max_rows_in")
        st_done = sem("scores_t")
        ex_done = sem("exponentials")
        pv_done = sem("pv_a_done")
        packs_used = sem("packs_used")
        ot_ok = sem("ot_ok")
        ot_turn = sem("ot_turned")
        o_rec = sem("o_reciprocal")
        on_ok = sem("on_ok")
        on_turn = sem("on_turned")
        onT_ok = sem("onT_ok")
        proj_a = sem("o_projected")
        x1_ok = sem("x1_ok")
        v_cur = sem("v_cur_ok")
        dve_gate = sem("dve_gate_a")
        block = ctx.enter_context(nc.Block())
        STACK_DMAS = 2 * 9 + 2

        @block.gpsimd
        def _(pool):
            start_all(pool, sems)

        @block.sync
        def _(sp):
            sp.dma_start(wo[:, :], o_w).then_inc(wo_in, 16)
            sp.wait_ge(stacks_clear, START + 1)

            def fill(b, q):
                s = q % 2
                G = b * QUADS + q
                if q >= 2:
                    sp.wait_ge(st_done, START + 4 * NP * (G - 1))
                else:
                    sp.wait_ge(st_done, START + 4 * NP * QUADS * b)
                for a in range(3):
                    for c in range(3):
                        r = (a * 3 + c) * HDA
                        for i, (st, part) in enumerate(((qst, a), (kst, c))):
                            src = parts_d[b, i, part, 32 * q:32 * q + 32, :].rearrange("(h d) n -> d h n", d=HDA)
                            sp.dma_start(st[r:r + HDA, s, :, :], src).then_inc(stacked[s], 16)
                for i, st in enumerate((qst, kst)):
                    sp.dma_start(st[ROWS:ROWS + 12, s, :, :],
                                 bias_d[4 * q:4 * q + 4, i, :, :].rearrange("h r n -> r h n")).then_inc(stacked[s], 16)

            def max_rows(b, q):
                G = b * QUADS + q
                sp.wait_ge(m_step, START + 4 * (G + 1))
                for h in range(4):
                    for part in range(3):
                        dst = qst[MROW + part:MROW + part + 1, q % 2, h, :].rearrange("p (i n) -> p i n", n=P)
                        sp.dma_start(dst, mparts[NB * h:NB * h + NB, part, :]).then_inc(m_rows, 16)

            with sp.Fori(0, B) as b:
                fill(b, 0)
                fill(b, 1)
                max_rows(b, 0)
                for q in range(1, QUADS):
                    max_rows(b, q)
                    if q + 1 < QUADS:
                        fill(b, q + 1)

        @block.tensor
        def _(pe):
            def max_piece(b, q, n):
                G = b * QUADS + q
                h, (I, c0, c1) = n // len(PIECES), PIECES[n % len(PIECES)]
                N = 4 * len(PIECES) + 1
                s = q % 2
                if n == 0:
                    pe.wait_ge(stacked[s], START + 16 * STACK_DMAS * (b * QUADS // 2 + q // 2 + 1))
                if n >= 2:
                    pe.wait_ge(m_read, START + N * G + n - 1)
                else:
                    pe.wait_ge(m_read, START + N * G)
                out = p_max[:, n % 2, 0:c1 - c0]
                diag = c1 == P * (I + 1)
                mm = pe.matmul(out, qst[0:MROW, s, h, P * I:P * (I + 1)], kst[0:MROW, s, h, c0:c1],
                               start=True, stop=not diag)
                if diag:
                    mm = pe.matmul(out[:, c1 - c0 - P:c1 - c0], identb[:, :], cmask[:, :], start=False, stop=True)
                mm.then_inc(maxed, 1)

            def turn_max(b, q):
                G = b * QUADS + q
                pe.wait_ge(m_all, START + G + 1)
                pe.transpose(p_max[0:32, 0, 0:P], mx[:, 0, :, :].rearrange("p h i -> p (h i)"),
                             ident[:, :]).then_inc(m_turn, 1)

            def scores_t(b, q, k, h):
                G = b * QUADS + q
                U = 4 * NP * G + 4 * k + h
                if k == 0 and h == 0:
                    pe.wait_ge(m_rows, START + 16 * 12 * (G + 1))
                if 4 * k + h >= 2:
                    pe.wait_ge(ex_done, START + U - 1)
                else:
                    pe.wait_ge(ex_done, START + 4 * NP * G)
                s = q % 2
                for J, at in PACKS[k]:
                    lo = J * P
                    while lo < L:
                        o = at + lo - J * P
                        hi = min(L, lo + 512 - o % 512)
                        diag = lo == J * P
                        mm = pe.matmul(p_exp[:, h % 2, o:o + hi - lo], kst[:, s, h, J * P:(J + 1) * P],
                                       qst[:, s, h, lo:hi], start=True, stop=not diag)
                        if diag:
                            mm = pe.matmul(p_exp[:, h % 2, o:o + P], cmask[:, :], identb[:, :],
                                           start=False, stop=True)
                        lo = hi
                mm.then_inc(st_done, 1)

            def pv(b, q, k):
                G = b * QUADS + q
                K = NP * q + k
                pe.wait_ge(ex_done, START + 4 * (NP * G + k + 1))
                if k == 0:
                    pe.wait_ge(v_cur, START + b + 1)
                    pe.wait_ge(on_ok, START + G)
                    pe.wait_ge(x1_ok, START + b)
                for J, at in PACKS[k]:
                    for seg in range(2):
                        lo, hi = max(J * P, 512 * seg), 512 * (seg + 1)
                        if lo >= hi:
                            continue
                        for h in range(4):
                            o = at + lo - J * P
                            mm = pe.matmul(p_pv[32 * h:32 * h + HDA + 1, lo:hi], vc[:, J, 4 * q + h, :],
                                           pt[:, K % 3, h, o:o + hi - lo], start=(J == 0), stop=(k == NP - 1),
                                           skip_group_check=True)
                mm.then_inc(pv_done, 1)

            def turn_o(b, q):
                G = b * QUADS + q
                pe.wait_ge(ot_ok, START + G + 1)
                for i in range(NB):
                    mm = pe.transpose(p_pv[:, i * P:(i + 1) * P], ot[:, i * P:(i + 1) * P], ident[:, :])
                mm.then_inc(ot_turn, 1)

            def out_proj(b):
                pe.wait_ge(on_ok, START + QUADS * (b + 1))
                for i in range(NB):
                    mm = pe.transpose(p_pv[:, i * P:(i + 1) * P], on[:, i, :], ident[:, :])
                mm.then_inc(on_turn, 1)
                pe.wait_ge(onT_ok, START + b + 1)
                for i in range(NB):
                    mm = pe.matmul(p_pv[:, i * P:(i + 1) * P], onT[:, i * P:(i + 1) * P], wo[:, :], start=True, stop=True)
                mm.then_inc(proj_a, 1)

            NPI = 4 * len(PIECES)
            pe.wait_ge(wo_in, START + 16)
            with pe.Fori(0, B) as b:
                for n in range(NPI):
                    max_piece(b, 0, n)
                turn_max(b, 0)
                for q in range(QUADS):
                    done = 0
                    for k in range(NP):
                        for h in range(4):
                            scores_t(b, q, k, h)
                            if q + 1 < QUADS:
                                while done < min(NPI, NPI * (4 * k + h + 1) // (4 * NP - 4)):
                                    max_piece(b, q + 1, done)
                                    done += 1
                        if k == NP - 1 and q + 1 < QUADS:
                            turn_max(b, q + 1)
                        if k >= 1:
                            pv(b, q, k - 1)
                    pv(b, q, NP - 1)
                    turn_o(b, q)
                out_proj(b)

        @block.scalar
        def _(act):
            with act.Fori(0, B) as b:
                for q in range(QUADS):
                    G = b * QUADS + q
                    for k in range(NP):
                        K = NP * q + k
                        for h in range(4):
                            U = 4 * NP * G + 4 * k + h
                            act.wait_ge(st_done, START + U + 1)
                            if h == 0:
                                if K >= 3:
                                    act.wait_ge(pv_done, START + NP * QUADS * b + K - 2)
                                else:
                                    act.wait_ge(pv_done, START + NP * QUADS * b)
                            w = L if k < NP - 1 else L // 2
                            act.activation(pt[:, K % 3, h, 0:w], p_exp[:, h % 2, 0:w], ACT.Exp).then_inc(ex_done, 1)
                    act.wait_ge(pv_done, START + NP * (G + 1))
                    act.activation(ot[:, :], p_pv[:, :], ACT.Copy).then_inc(ot_ok, 1)
                act.wait_ge(on_turn, START + b + 1)
                act.activation(onT[:, :], p_pv[:, :], ACT.Copy).then_inc(onT_ok, 1)

        @block.vector
        def _(dve):
            NPI = 4 * len(PIECES)

            def maxima(b, q):
                G = b * QUADS + q
                N = NPI + 1
                for n in range(NPI):
                    h, (I, c0, c1) = n // len(PIECES), PIECES[n % len(PIECES)]
                    dve.wait_ge(maxed, START + NPI * G + n + 1)
                    dve.tensor_reduce(mx[:, c0 // 512, h, I:I + 1], p_max[:, n % 2, 0:c1 - c0], X, ALU.max)\
                       .then_inc(m_read, 1)
                dve.wait_ge(m_read, START + N * G + NPI)
                half = 512 // P
                dve.tensor_tensor(mx[:, 0, :, half:NB], mx[:, 0, :, half:NB], mx[:, 1, :, half:NB], ALU.max)\
                   .then_inc(m_all, 1)
                dve.wait_ge(m_turn, START + G + 1)
                dve.wait_ge(m_rows, START + 16 * 12 * G)
                dve.tensor_scalar(mrow[:, :], p_max[0:32, 0, 0:P], -1.0, None, ALU.mult).then_inc(m_read, 1)
                dve.wait_ge(m_read, START + N * (G + 1))
                dve.tensor_copy(mparts[:, 0, :], mrow[:, :]).then_inc(m_step, 1)
                dve.wait_ge(m_step, START + 4 * G + 1)
                dve.tensor_tensor(mrest[:, :], mrow[:, :], mparts[:, 0, :], ALU.subtract).then_inc(m_step, 1)
                dve.wait_ge(m_step, START + 4 * G + 2)
                dve.tensor_copy(mparts[:, 1, :], mrest[:, :]).then_inc(m_step, 1)
                dve.wait_ge(m_step, START + 4 * G + 3)
                dve.tensor_tensor(mparts[:, 2, :], mrest[:, :], mparts[:, 1, :], ALU.subtract).then_inc(m_step, 1)

            def normalise(b, q):
                G = b * QUADS + q
                dve.wait_ge(ot_turn, START + G + 1)
                o = p_pv[:, :].rearrange("p (i h r) -> p i h r", h=4, r=32)
                dve.reciprocal(osum[:, :, :], o[:, :, :, HDA]).then_inc(o_rec, 1)
                dve.wait_ge(o_rec, START + G + 1)
                dve.wait_ge(on_turn, START + b)
                dve.tensor_tensor(on[:, :, 32 * q:32 * q + 32].rearrange("p i (h d) -> p i h d", d=HDA),
                                  o[:, :, :, 0:HDA], osum[:, :, :].unsqueeze(3).broadcast_to([P, NB, 4, HDA]),
                                  ALU.mult).then_inc(on_ok, 1)

            dve.memset(qst[:, :, :, :], 0.0)
            dve.memset(kst[0:MROW, :, :, :], 0.0)
            dve.memset(kst[MROW:P, :, :, :], 1.0)
            dve.memset(p_pv[:, :], 0.0).then_inc(stacks_clear, 1)
            with dve.Fori(0, B) as b:
                dve.wait_ge(proj_a, START + b)
                dve.sem_inc(dve_gate, 1)
                dve.tensor_copy(vc[:, :, :, :], va[:, bass.ds(b * NB, NB), :, :]).then_inc(v_cur, 1)
                maxima(b, 0)
                for q in range(QUADS):
                    if q + 1 < QUADS:
                        maxima(b, q + 1)
                    normalise(b, q)
                dve.wait_ge(proj_a, START + b + 1)
                xb = x_all[:, bass.ds(b * NB, NB), :]
                dve.tensor_tensor(xb, xb, p_pv[:, :].rearrange("p (i n) -> p i n", n=P), ALU.add).then_inc(x1_ok, 1)


def deep_layers(nc, g, hT, ident, tabs, maskt, wqkv, qsc, ksc, wo, ln_g, ln_b, w1, b1, w2, b2):
    B, L, D = g.B, g.L, g.D
    NB, H, HD, CH, W, KEYS = g.blocks, g.heads, g.hd, g.chunks, g.window, g.keys
    HALF = HD // 2
    IN = g.inner
    FC = g.fchunks
    F = g.ffn
    GT = 512
    NG = L // GT
    PAIRS = H // 2
    QUADS = H // 4

    ctx = ExitStack()
    with ctx:
        def sb(name, shape, dt=F32):
            return ctx.enter_context(nc.sbuf_tensor(name, shape, dt))

        def ps(name, shape):
            return ctx.enter_context(nc.psum_tensor(name, shape, F32))

        sems = []

        def sem(name):
            sems.append(ctx.enter_context(nc.semaphore(name)))
            return sems[-1]

        wqkv_in = sb("wqkv_in", [P, 3 * IN])
        wqkv_hi = sb("wqkv_hi", [P, 3 * IN], F32R)
        wqkv_lo = sb("wqkv_lo", [P, 3 * IN], F32R)
        wo_in = sb("wo_in", [P, CH, D])
        wo_s = sb("wo_s", [P, CH, D])
        w1_in = sb("w1_in", [P, 2 * FC, P])
        w1_hi = sb("w1_hi", [P, 2 * FC, P], F32R)
        w1_lo = sb("w1_lo", [P, 2 * FC, P], F32R)
        w2_in = sb("w2_in", [P, FC, D])
        w2_s = sb("w2_s", [P, FC, D])
        vec_in = sb("vec_in", [P, 2 * FC + 3])
        vec = sb("vec", [P, 2 * FC + 3])
        scl_in = sb("scl_in", [P, 2, HD])
        rot = sb("rot", [P, 2, 2, NB, HD])
        xs_hi = sb("xs_hi", [P, L], F32R)
        xs_lo = sb("xs_lo", [P, L], F32R)
        sq = sb("sq", [P, 2, IN])
        ss = sb("ss", [P, 2, H])
        rn = sb("rn", [P, 2, 2, H])
        nrq = sb("nrq", [P, 2, H])
        bias = sb("bias", [P, H])
        nx = sb("nx", [P, 2, H])
        nxh = sb("nxh", [P, 2, H])
        nt = sb("nt", [P, 2, H])
        mroot = sb("mroot", [P, 4, GT // P])
        one = sb("one", [P, P])
        byc = sb("byc", [P, 2, IN])
        bys = sb("bys", [P, 2, IN])
        qkr = sb("qkr", [P, 2, IN])
        v_s = sb("v_s", [P, 3, IN])
        v_mix = sb("v_mix", [P, IN])
        qTz = sb("qTz", [P, CH, 2, P])
        kT = sb("kT", [P, CH, W + 2 * P])
        pr = sb("pr", [P, H, KEYS])
        nmax = sb("nmax", [P, H])
        psumr = sb("psumr", [P, H])
        rsum = sb("rsum", [P, H])
        pT = sb("pT", [P, H, P])
        oT = sb("oT", [P, CH, P])
        ones = sb("ones", [P, P])
        fs = sb("fs", [P, L])
        cen = sb("cen", [P, GT])
        csq = sb("csq", [P, GT])
        rstd = sb("rstd", [P, GT])
        xn = cen
        xg = csq
        xg_hi = sb("xg_hi", [P, GT], F32R)
        xg_lo = sb("xg_lo", [P, GT], F32R)
        gl = sb("gl", [P, FC, GT])
        u = gl
        o_s = gl

        pq = ps("pq", [P, 2, 2, 512])
        psc = ps("psc", [P, 2, 512])
        ptr = ps("ptr", [P, 2, 512])

        w_in = sem("w_in")
        w_used = sem("w_used")
        w_pool = sem("w_pool")
        w_dve = sem("w_dve")
        pads = sem("pads")
        dve_gate = sem("dve_gate")
        pe_gate = sem("pe_gate")
        pool_gate = sem("pool_gate")
        xs_sem = sem("xs_split")
        proj = sem("projected")
        squared = sem("squared")
        summed = sem("squares_summed")
        norm_step = sem("norm_step")
        root_step = sem("mlp_root_step")
        rot_mul = sem("rotary_products")
        added = sem("k_added")
        biased = sem("bias_ready")
        rotated = sem("rotated")
        qk_turned = sem("qk_turned")
        qk_kept = sem("qk_kept")
        p_turned = sem("p_turned")
        p_kept = sem("p_kept")
        o_turned = sem("o_turned")
        o_kept = sem("o_kept")
        kcopy = sem("k_prev_copied")
        scored = sem("scored")
        maxed = sem("maxed")
        exped = sem("exped")
        recip = sem("recip")
        pprev = sem("prev_turned")
        mixed = sem("v_mixed")
        v_ok = sem("v_ready")
        pvd = sem("pv_done")
        o_norm = sem("o_normalised")
        wod = sem("wo_done")
        resid = sem("attn_residual")
        fsh = sem("ffn_shift")
        f_mean = sem("f_mean")
        f_cen = sem("f_cen")
        f_sq = sem("f_sq")
        f_var = sem("f_var")
        f_rstd = sem("f_rstd")
        f_spread = sem("f_spread")
        f_xn = sem("f_xn")
        f_xg = sem("f_xg")
        f_hi = sem("f_hi")
        f_lo = sem("f_lo")
        f_gate = sem("f_gate")
        f_a = sem("f_a")
        f_gelu = sem("f_gelu")
        f_u = sem("f_u")
        f_out = sem("f_out")
        f_res = sem("f_res")

        def mlp_banks(t):
            if t == 0:
                return pq[:, 0, 0, :], pq[:, 0, 1, :], pq[:, 1, 0, :], pq[:, 1, 1, :]
            return psc[:, 0, :], psc[:, 1, :], ptr[:, 0, :], ptr[:, 1, :]

        block = ctx.enter_context(nc.Block())

        NVEC = 2 * FC + 3
        b1v = b1.rearrange("l (s f) -> l s f", s=2)
        LOADS = 2 + 2 * (2 + FC) + 2 + 3 + 2
        POOL_STEPS = 2 * 3 + 2

        @block.sync
        def _(sp):
            sp.wait_ge(pads, START + 1)
            with sp.Fori(0, g.depth) as l:
                sp.wait_ge(w_used, START + l * 2)
                sp.dma_start(wqkv_in[:, :], wqkv[l]).then_inc(w_in, 16)
                sp.dma_start(wo_in[:, :, :], wo[l].rearrange("(c p) n -> p c n", p=P)).then_inc(w_in, 16)
                for s in range(2):
                    full = F // P * P
                    sp.dma_start(w1_in[:, s * FC:s * FC + F // P, :],
                                 w1[l, :, s * F:s * F + full].rearrange("d (c f) -> d c f", f=P)).then_inc(w_in, 16)
                    sp.dma_start(w1_in[:, s * FC + F // P, 0:F - full],
                                 w1[l, :, s * F + full:(s + 1) * F]).then_inc(w_in, 16)
                    for c in range(FC):
                        m = min(P, F - c * P)
                        sp.dma_start(vec_in[0:m, s * FC + c:s * FC + c + 1],
                                     b1v[l, s, c * P:c * P + m].unsqueeze(1)).then_inc(w_in, 16)
                sp.dma_start(w2_in[:, 0:F // P, :],
                             w2[l, 0:F // P * P, :].rearrange("(c p) n -> p c n", p=P)).then_inc(w_in, 16)
                sp.dma_start(w2_in[0:F - F // P * P, F // P, :], w2[l, F // P * P:F, :]).then_inc(w_in, 16)
                for i, t in enumerate((ln_g, ln_b, b2)):
                    sp.dma_start(vec_in[:, 2 * FC + i:2 * FC + i + 1], t[l].unsqueeze(1)).then_inc(w_in, 16)
                for i, t in enumerate((qsc, ksc)):
                    sp.dma_start(scl_in[:, i, :], t[l].partition_broadcast(P)).then_inc(w_in, 16)

        @block.tensor
        def _(pe):
            def project(n, j, part):
                G = n * NB + j
                if part == 0 and j > 0:
                    pe.wait_ge(rot_mul, START + 2 * n * NB + 2 * j - 1)
                    pe.wait_ge(squared, START + 2 * n * NB + 2 * j - 1)
                if part == 1:
                    pe.wait_ge(v_ok, START + G)
                if part == 2:
                    pe.wait_ge(rot_mul, START + 2 * G + 2)
                    pe.wait_ge(squared, START + 2 * G + 2)
                tok = slice(j * P, (j + 1) * P)
                for c in range(IN // 512):
                    col = slice(part * IN + c * 512, part * IN + (c + 1) * 512)
                    out = pq[:, min(part, 1), c, :]
                    pe.matmul(out, xs_hi[:, tok], wqkv_hi[:, col], start=True, stop=False)
                    pe.matmul(out, xs_hi[:, tok], wqkv_lo[:, col], start=False, stop=False)
                    mm = pe.matmul(out, xs_lo[:, tok], wqkv_hi[:, col], start=False, stop=True)
                mm.then_inc(proj, 1)

            def turn_qk(n, j, which):
                G = n * NB + j
                for t in which:
                    part, half = t // 2, t % 2
                    pe.wait_ge(rotated, START + 2 * G + part + 1)
                    if t >= 2:
                        pe.wait_ge(qk_kept, START + 4 * G + t - 1)
                    for c in range(4):
                        s = (half * 4 + c) * P
                        mm = pe.transpose(ptr[:, t % 2, c * P:(c + 1) * P], qkr[:, part, s:s + P], ident[:, :])
                    mm.then_inc(qk_turned, 1)

            def scores(n, j, p):
                G = n * NB + j
                if p == 0:
                    pe.wait_ge(qk_kept, START + 4 * G + 4)
                    pe.wait_ge(kcopy, START + n * (NB // 2 - 1) + j // 2)
                    pe.wait_ge(maxed, START + PAIRS * G)
                if p == 1 and j > 0:
                    pe.wait_ge(resid, START + G)
                if p >= 2:
                    pe.wait_ge(maxed, START + PAIRS * G + p - 1)
                k0 = (j % 2) * P
                for h in range(2):
                    if j == 0:
                        rhs = kT[:, p, W:W + P]
                        out = psc[:, p % 2, h * 256 + W:h * 256 + KEYS]
                    else:
                        rhs = kT[:, p, k0:k0 + KEYS]
                        out = psc[:, p % 2, h * 256:h * 256 + KEYS]
                    mm = pe.matmul(out, qTz[:, p, h, :], rhs, start=True, stop=True)
                mm.then_inc(scored, 1)

            def turn_p(n, j, q):
                G = n * NB + j
                pe.wait_ge(exped, START + PAIRS * G + 2 * q + 2)
                for i in range(4):
                    mm = pe.transpose(ptr[:, q % 2, i * P:(i + 1) * P], pr[:, 4 * q + i, W:KEYS], ident[:, :])
                mm.then_inc(p_turned, 1)

            def values(n, j, q):
                G = n * NB + j
                pe.wait_ge(p_kept, START + 4 * G + 1 + q)
                if q == 0:
                    pe.wait_ge(v_ok, START + G + 1)
                    pe.wait_ge(maxed, START + PAIRS * (G + 1))
                    if j > 0:
                        pe.wait_ge(mixed, START + 2 * n * (NB - 1) + 2 * j)
                if j > 0:
                    pe.wait_ge(pprev, START + n * (QUADS * (NB - 1)) + QUADS * (j - 1) + q + 1)
                for i in range(4):
                    h = 4 * q + i
                    for s in range(2):
                        v = v_mix[:, h * HD:(h + 1) * HD] if s == 0 and j > 0 else v_s[:, j % 3, h * HD:(h + 1) * HD]
                        mm = pe.matmul(psc[64 * s:64 * s + 64, q // 2, h % 8 * HD:(h % 8 + 1) * HD],
                                       pT[:, h, 64 * s:64 * s + 64], v, start=True, stop=True)
                if q % 2:
                    mm.then_inc(pvd, 1)

            def turn_o(n, j, c):
                G = n * NB + j
                pe.wait_ge(o_norm, START + 2 * G + c + 1)
                if j + 1 < NB:
                    pe.wait_ge(qk_kept, START + 4 * G + 7 + c)
                for i in range(4):
                    mm = pe.transpose(ptr[:, c, i * P:(i + 1) * P], o_s[:, c, i * P:(i + 1) * P], ident[:, :])
                mm.then_inc(o_turned, 1)

            def out_proj(n, j):
                G = n * NB + j
                for c in range(CH):
                    if c % 4 == 0:
                        pe.wait_ge(o_kept, START + 2 * G + 1 + c // 4)
                    mm = pe.matmul(psc[:, 1, 0:P], wo_s[:, c, :], oT[:, c, :], start=(c == 0), stop=(c == CH - 1))
                mm.then_inc(wod, 1)

            def mlp_mean(n, t):
                M = n * NG + t
                if t == 0:
                    pe.wait_ge(rot_mul, START + 2 * NB * n + 2 * NB)
                    pe.wait_ge(squared, START + 2 * NB * n + 2 * NB)
                    pe.wait_ge(v_ok, START + NB * n + NB)
                pe.wait_ge(fsh, START + M + 1)
                pe.matmul(mlp_banks(t)[0], ones[:, :], fs[:, t * GT:(t + 1) * GT], start=True, stop=True).then_inc(f_mean, 1)

            def mlp_var(n, t):
                M = n * NG + t
                pe.wait_ge(f_sq, START + M + 1)
                for k in range(GT // P):
                    mm = pe.matmul(mlp_banks(t)[1][:, k:k + 1], csq[:, k * P:(k + 1) * P], ones[:, 0:1], start=True, stop=True)
                mm.then_inc(f_var, 1)

            def mlp_spread(n, t):
                M = n * NG + t
                pe.wait_ge(f_rstd, START + M + 1)
                pe.matmul(mlp_banks(t)[1], one[:, :], rstd[:, :], start=True, stop=True).then_inc(f_spread, 1)

            def mlp_up(n, t, c):
                M = n * NG + t
                bank = mlp_banks(t)
                if c == 0:
                    pe.wait_ge(f_lo, START + M + 1)
                for s in (1, 0):
                    if c == 2:
                        pe.wait_ge(f_gelu if s else f_u, START + FC * M + 1)
                    ch = s * FC + c
                    out = bank[(3 if c % 2 == 0 else 1) - s]
                    pe.matmul(out, w1_hi[:, ch, :], xg_hi[:, :], start=True, stop=False)
                    pe.matmul(out, w1_hi[:, ch, :], xg_lo[:, :], start=False, stop=False)
                    pe.matmul(out, w1_lo[:, ch, :], xg_hi[:, :], start=False, stop=True)\
                        .then_inc(f_gate if s else f_a, 1)

            def mlp_down(n, t):
                M = n * NG + t
                for c in (1, 0, 2):
                    pe.wait_ge(f_u, START + FC * M + max(c, 1) + 1)
                    mm = pe.matmul(mlp_banks(t)[0], w2_s[:, c, :], u[:, c, :], start=(c == 1), stop=(c == 2))
                mm.then_inc(f_out, 1)

            def sequence(n, ahead):
                for i in range(NB + 1):
                    last = i == NB
                    if i >= 1:
                        turn_p(n, i - 1, 0)
                        turn_p(n, i - 1, 1)
                    if i + 1 < NB:
                        project(n, i + 1, 0)
                        project(n, i + 1, 1)
                    if last:
                        mlp_mean(n, 0)
                    if i >= 1:
                        values(n, i - 1, 0)
                        turn_p(n, i - 1, 2)
                        values(n, i - 1, 1)
                        turn_p(n, i - 1, 3)
                    if last:
                        mlp_var(n, 0)
                    if i >= 1:
                        values(n, i - 1, 2)
                        values(n, i - 1, 3)
                    if not last:
                        if i == 0:
                            pe.wait_ge(f_res, START + NG * n)
                        turn_qk(n, i, range(4))
                    if last:
                        mlp_spread(n, 0)
                    if i >= 1:
                        turn_o(n, i - 1, 0)
                        turn_o(n, i - 1, 1)
                    if i + 1 < NB:
                        project(n, i + 1, 2)
                    if i >= 1:
                        out_proj(n, i - 1)
                    if not last:
                        for p in range(PAIRS):
                            scores(n, i, p)
                mlp_up(n, 0, 0)
                mlp_up(n, 0, 1)
                mlp_mean(n, 1)
                mlp_up(n, 0, 2)
                mlp_var(n, 1)
                mlp_down(n, 0)
                if ahead:
                    pe.wait_ge(xs_sem, START + 4 * n + 8)
                    pe.wait_ge(f_res, START + NG * n + 1)
                    project(n + 1, 0, 0)
                    project(n + 1, 0, 1)
                mlp_spread(n, 1)
                for c in range(FC):
                    mlp_up(n, 1, c)
                if ahead:
                    project(n + 1, 0, 2)
                mlp_down(n, 1)

            pe.wait_ge(pads, START + 1)
            with pe.Fori(0, g.depth) as l:
                pe.wait_ge(w_dve, START + 5 * (l + 1))
                pe.wait_ge(w_pool, START + POOL_STEPS * (l + 1))
                pe.wait_ge(xs_sem, START + 4 * B * l + 4)
                for part in range(3):
                    project(l * B, 0, part)
                with pe.Fori(0, B - 1) as b:
                    sequence(l * B + b, True)
                sequence(l * B + (B - 1), False)

        @block.scalar
        def _(act):
            def square(n, j, part):
                G = n * NB + j
                act.wait_ge(rot_mul, START + 2 * G + part + 1)
                act.wait_ge(summed, START + 2 * G)
                act.activation(sq[:, part, :], pq[:, part, :, :].rearrange("p a n -> p (a n)"),
                               ACT.Square).then_inc(squared, 1)

            def keep_v(n, j):
                G = n * NB + j
                act.wait_ge(proj, START + 3 * G + 3)
                if j > 2:
                    act.wait_ge(mixed, START + 2 * n * (NB - 1) + 2 * j - 4)
                act.activation(v_s[:, j % 3, :], pq[:, 1, :, :].rearrange("p a n -> p (a n)"),
                               ACT.Copy).then_inc(v_ok, 1)

            def keep_qk(n, j, which):
                G = n * NB + j
                for t in which:
                    part, half = t // 2, t % 2
                    act.wait_ge(qk_turned, START + 4 * G + t + 1)
                    src = ptr[:, t % 2, :].rearrange("p (c n) -> p c n", c=4)
                    if part == 0:
                        act.activation(qTz[0:64, 4 * half:4 * half + 4, 0, :], src[0:64], ACT.Copy)
                        op = act.activation(qTz[64:P, 4 * half:4 * half + 4, 1, :], src[64:P], ACT.Copy)
                    else:
                        o = W + (j % 2) * P
                        op = act.activation(kT[:, 4 * half:4 * half + 4, o:o + P], src, ACT.Copy)
                    op.then_inc(qk_kept, 1)
                    if t == 1 and j % 2 == 0 and j > 0:
                        act.wait_ge(qk_kept, START + 4 * G)
                        act.activation(kT[:, :, 0:W], kT[:, :, 2 * P:2 * P + W], ACT.Copy).then_inc(kcopy, 1)

            def exps(n, j, p):
                G = n * NB + j
                act.wait_ge(biased, START + PAIRS * G + p + 1)
                if p == 0:
                    act.wait_ge(recip, START + G)
                k0 = W if j == 0 else 0
                for h in (2 * p, 2 * p + 1):
                    op = act.activation(pr[:, h, k0:KEYS], pr[:, h, k0:KEYS], ACT.Exp, bias=bias[:, h:h + 1],
                                        scale=nrq[:, j % 2, h:h + 1], accum_out=psumr[:, h:h + 1])
                op.then_inc(exped, 1)

            def keep_p(n, j, q):
                G = n * NB + j
                act.wait_ge(p_turned, START + 4 * G + 1 + q)
                act.activation(pT[:, 4 * q:4 * q + 4, :].rearrange("p h n -> p (h n)"), ptr[:, q % 2, :],
                               ACT.Copy).then_inc(p_kept, 1)

            def keep_o(n, j, c):
                G = n * NB + j
                act.wait_ge(o_turned, START + 2 * G + c + 1)
                act.activation(oT[:, 4 * c:4 * c + 4, :].rearrange("p h n -> p (h n)"), ptr[:, c, :],
                               ACT.Copy).then_inc(o_kept, 1)

            def mlp_square(n, t):
                M = n * NG + t
                act.wait_ge(f_cen, START + M + 1)
                act.wait_ge(f_lo, START + M)
                act.activation(csq[:, :], cen[:, :], ACT.Square).then_inc(f_sq, 1)

            def mlp_gain(n, t):
                M = n * NG + t
                act.wait_ge(f_xn, START + M + 1)
                act.activation(xg[:, :], xn[:, :], ACT.Identity, bias=vec[:, 2 * FC + 1:2 * FC + 2],
                               scale=vec[:, 2 * FC:2 * FC + 1]).then_inc(f_xg, 1)

            def mlp_gelu(n, t, c):
                M = n * NG + t
                act.wait_ge(f_gate, START + FC * M + c + 1)
                if c == 0:
                    if t == 0:
                        act.wait_ge(o_turned, START + 2 * NB * n + 2 * NB)
                    act.wait_ge(f_out, START + M)
                act.activation(gl[:, c, :], mlp_banks(t)[2 if c % 2 == 0 else 0], ACT.Gelu,
                               bias=vec[:, FC + c:FC + c + 1]).then_inc(f_gelu, 1)

            def sequence(n, ahead):
                for i in range(NB):
                    if i + 1 < NB:
                        square(n, i + 1, 0)
                    if i >= 1:
                        keep_p(n, i - 1, 2)
                        keep_p(n, i - 1, 3)
                    if i + 1 < NB:
                        square(n, i + 1, 1)
                    keep_qk(n, i, range(4))
                    if i >= 1:
                        keep_o(n, i - 1, 0)
                        keep_o(n, i - 1, 1)
                    if i + 1 < NB:
                        keep_v(n, i + 1)
                    for p in range(PAIRS - 2):
                        exps(n, i, p)
                    keep_p(n, i, 0)
                    exps(n, i, PAIRS - 2)
                    exps(n, i, PAIRS - 1)
                    keep_p(n, i, 1)
                mlp_square(n, 0)
                keep_p(n, NB - 1, 2)
                keep_p(n, NB - 1, 3)
                keep_o(n, NB - 1, 0)
                keep_o(n, NB - 1, 1)
                mlp_gain(n, 0)
                mlp_gelu(n, 0, 0)
                mlp_gelu(n, 0, 1)
                mlp_square(n, 1)
                mlp_gelu(n, 0, 2)
                mlp_gain(n, 1)
                if ahead:
                    square(n + 1, 0, 0)
                    square(n + 1, 0, 1)
                for c in range(FC):
                    mlp_gelu(n, 1, c)
                if ahead:
                    keep_v(n + 1, 0)

            act.wait_ge(pads, START + 1)
            with act.Fori(0, g.depth) as l:
                act.wait_ge(w_dve, START + 5 * (l + 1))
                square(l * B, 0, 0)
                square(l * B, 0, 1)
                keep_v(l * B, 0)
                with act.Fori(0, B - 1) as b:
                    sequence(l * B + b, True)
                sequence(l * B + (B - 1), False)

        @block.vector
        def _(dve):
            def sums(n, j, part):
                G = n * NB + j
                dve.wait_ge(squared, START + 2 * G + part + 1)
                dve.tensor_reduce(ss[:, part, :], sq[:, part, :].rearrange("p (h d) -> p h d", d=HD), X, ALU.add)\
                    .then_inc(summed, 1)

            def norms(n, j):
                G = n * NB + j
                dve.wait_ge(summed, START + 2 * G + 2)
                flat = [t.rearrange("p a h -> p (a h)") for t in (rn[:, j % 2, :, :], nx[:, :, :], nxh[:, :, :],
                                                                  nt[:, :, :], ss[:, :, :])]
                inverse_root(dve, *flat, 1e-24, ALU.max, norm_step, (ROOT + 1) * G)
                dve.tensor_scalar(nrq[:, j % 2, :], rn[:, j % 2, 0, :], -1.0, None, ALU.mult).then_inc(norm_step, 1)

            def rotary_products(n, j, part):
                G = n * NB + j
                dve.wait_ge(proj, START + 3 * G + part + 1)
                dve.wait_ge(rotated, START + 2 * G)
                src = pq[:, part, :, :].rearrange("p a (h s d) -> p (a h) s d", s=2, d=HALF)
                dst = bys[:, part, :].rearrange("p (h s d) -> p h s d", s=2, d=HALF)
                for s in range(2):
                    t = rot[:, part, 1, j, s * HALF:(s + 1) * HALF].unsqueeze(1).broadcast_to([P, H, HALF])
                    dve.tensor_tensor(dst[:, :, s, :], src[:, :, 1 - s, :], t, ALU.mult)
                dve.tensor_tensor(byc[:, part, :].rearrange("p (h d) -> p h d", d=HD),
                                  pq[:, part, :, :].rearrange("p a (h d) -> p (a h) d", d=HD),
                                  rot[:, part, 0, j, :].unsqueeze(1).broadcast_to([P, H, HD]),
                                  ALU.mult).then_inc(rot_mul, 1)

            def smax(n, j, p):
                G = n * NB + j
                dve.wait_ge(scored, START + PAIRS * G + p + 1)
                k0 = W if j == 0 else 0
                dve.sem_inc(dve_gate, 1)
                for h in range(2):
                    op = dve.tensor_tensor_reduce(pr[:, 2 * p + h, k0:KEYS], psc[:, p % 2, h * 256 + k0:h * 256 + KEYS],
                                                  maskt[:, k0:KEYS], -1.0, 3e38, ALU.add, ALU.min,
                                                  nmax[:, 2 * p + h:2 * p + h + 1])
                op.then_inc(maxed, 1)
                dve.wait_ge(maxed, START + PAIRS * G + p + 1)
                dve.wait_ge(norm_step, START + (ROOT + 1) * (G + 1))
                dve.tensor_tensor(bias[:, 2 * p:2 * p + 2], nmax[:, 2 * p:2 * p + 2],
                                  rn[:, j % 2, 0, 2 * p:2 * p + 2], ALU.mult).then_inc(biased, 1)

            def reciprocal(n, j):
                G = n * NB + j
                dve.wait_ge(exped, START + PAIRS * (G + 1))
                dve.reciprocal(rsum[:, :], psumr[:, :]).then_inc(recip, 1)

            def prev_turn(n, j, q):
                G = n * NB + j
                dve.wait_ge(p_kept, START + 4 * G + 1 + q)
                dve.transpose(pT[P - W:P, 4 * q:4 * q + 4, 0:W], pr[0:W, 4 * q:4 * q + 4, 0:W]).then_inc(pprev, 1)

            def normalise(n, j, c):
                G = n * NB + j
                dve.wait_ge(pvd, START + 2 * G + c + 1)
                dve.wait_ge(recip, START + G + 1)
                dve.wait_ge(o_turned, START + 2 * G)
                dve.tensor_tensor(o_s[:, c, :].rearrange("p (h d) -> p h d", d=HD),
                                  psc[:, c, :].rearrange("p (h d) -> p h d", d=HD),
                                  rsum[:, 8 * c:8 * c + 8].unsqueeze(2).broadcast_to([P, 8, HD]),
                                  ALU.mult).then_inc(o_norm, 1)

            def residual(n, b, j):
                G = n * NB + j
                dve.wait_ge(wod, START + G + 1)
                dve.tensor_tensor(hT[:, b, 1 + j * P:1 + (j + 1) * P], hT[:, b, 1 + j * P:1 + (j + 1) * P],
                                  psc[:, 1, 0:P], ALU.add).then_inc(resid, 1)

            def shifted(n, b):
                dve.sem_inc(dve_gate, 1)
                for s in range(2):
                    lo, off = 64 * s, 1 - s
                    dve.tensor_copy(xs_hi[lo:lo + 64, :], hT[lo:lo + 64, b, off:off + L]).then_inc(xs_sem, 1)
                dve.wait_ge(xs_sem, START + 4 * n + 2)
                for s in range(2):
                    lo, off = 64 * s, 1 - s
                    dve.tensor_tensor(xs_lo[lo:lo + 64, :], hT[lo:lo + 64, b, off:off + L],
                                      xs_hi[lo:lo + 64, :].bitcast(F32), ALU.subtract).then_inc(xs_sem, 1)

            def mlp_shift(n, b, t):
                dve.wait_ge(resid, START + NB * n + (t + 1) * (NB // NG))
                dve.sem_inc(dve_gate, 1)
                dve.tensor_copy(fs[0:64, t * GT:(t + 1) * GT], hT[0:64, b, 1 + t * GT:1 + (t + 1) * GT])
                lo, hi = t * GT + min(t, 1), min((t + 1) * GT + 1, L)
                dve.tensor_copy(fs[64:P, lo:hi], hT[64:P, b, lo:hi]).then_inc(fsh, 1)

            def mlp_centre(n, t):
                M = n * NG + t
                dve.wait_ge(f_mean, START + M + 1)
                dve.wait_ge(f_xg, START + M)
                dve.tensor_tensor(cen[:, :], fs[:, t * GT:(t + 1) * GT], mlp_banks(t)[0], ALU.subtract).then_inc(f_cen, 1)

            def mlp_deviation(n, t):
                M = n * NG + t
                dve.wait_ge(f_var, START + M + 1)
                inverse_root(dve, mroot[:, 0, :], mroot[:, 1, :], mroot[:, 2, :], mroot[:, 3, :],
                             mlp_banks(t)[1][:, 0:GT // P], 1e-5, ALU.add, root_step, ROOT * M)
                for k in range(GT // P):
                    op = dve.tensor_scalar(rstd[:, k * P:(k + 1) * P], ident[:, :], mroot[:, 0, k:k + 1], None, ALU.mult)
                op.then_inc(f_rstd, 1)

            def mlp_normalise(n, t):
                M = n * NG + t
                dve.wait_ge(f_spread, START + M + 1)
                dve.wait_ge(f_cen, START + M + 1)
                dve.wait_ge(f_sq, START + M + 1)
                dve.tensor_tensor(xn[:, :], cen[:, :], mlp_banks(t)[1], ALU.mult).then_inc(f_xn, 1)

            def mlp_split(n, t):
                M = n * NG + t
                dve.wait_ge(f_xg, START + M + 1)
                dve.wait_ge(f_a, START + FC * M)
                dve.sem_inc(dve_gate, 1)
                dve.tensor_copy(xg_hi[:, :], xg[:, :]).then_inc(f_hi, 1)
                dve.wait_ge(f_hi, START + M + 1)
                dve.tensor_tensor(xg_lo[:, :], xg[:, :], xg_hi[:, :].bitcast(F32), ALU.subtract).then_inc(f_lo, 1)

            def mlp_gate(n, t, c):
                M = n * NG + t
                dve.wait_ge(f_a, START + FC * M + c + 1)
                dve.wait_ge(f_gelu, START + FC * M + c + 1)
                dve.scalar_tensor_tensor(u[:, c, :], mlp_banks(t)[3 if c % 2 == 0 else 1], vec[:, c:c + 1], gl[:, c, :],
                                         ALU.add, ALU.mult).then_inc(f_u, 1)

            def mlp_residual(n, b, t):
                M = n * NG + t
                dve.wait_ge(f_out, START + M + 1)
                h = hT[:, b, 1 + t * GT:1 + (t + 1) * GT]
                dve.scalar_tensor_tensor(h, mlp_banks(t)[0], vec[:, 2 * FC + 2:2 * FC + 3], h,
                                         ALU.add, ALU.add).then_inc(f_res, 1)

            def sequence(n, b, ahead):
                for i in range(NB):
                    if i + 1 < NB:
                        rotary_products(n, i + 1, 0)
                    if i > 1:
                        prev_turn(n, i - 1, 0)
                        prev_turn(n, i - 1, 1)
                    if i >= 1:
                        reciprocal(n, i - 1)
                    if i + 1 < NB:
                        rotary_products(n, i + 1, 1)
                    if i > 1:
                        prev_turn(n, i - 1, 2)
                        prev_turn(n, i - 1, 3)
                    if i >= 1:
                        normalise(n, i - 1, 0)
                        normalise(n, i - 1, 1)
                    if i + 1 < NB:
                        sums(n, i + 1, 0)
                        sums(n, i + 1, 1)
                        norms(n, i + 1)
                    if i >= 1:
                        residual(n, b, i - 1)
                    for p in range(PAIRS):
                        smax(n, i, p)
                j = NB - 1
                mlp_shift(n, b, 0)
                mlp_centre(n, 0)
                prev_turn(n, j, 0)
                prev_turn(n, j, 1)
                reciprocal(n, j)
                prev_turn(n, j, 2)
                prev_turn(n, j, 3)
                mlp_deviation(n, 0)
                normalise(n, j, 0)
                normalise(n, j, 1)
                if ahead:
                    dve.wait_ge(proj, START + 3 * NB * (n + 1))
                    shifted(n + 1, b + 1)
                mlp_normalise(n, 0)
                mlp_split(n, 0)
                residual(n, b, j)
                mlp_shift(n, b, 1)
                mlp_gate(n, 0, 0)
                mlp_centre(n, 1)
                mlp_gate(n, 0, 1)
                mlp_gate(n, 0, 2)
                mlp_deviation(n, 1)
                mlp_residual(n, b, 0)
                mlp_normalise(n, 1)
                if ahead:
                    rotary_products(n + 1, 0, 0)
                mlp_split(n, 1)
                if ahead:
                    rotary_products(n + 1, 0, 1)
                    sums(n + 1, 0, 0)
                mlp_gate(n, 1, 0)
                mlp_gate(n, 1, 1)
                if ahead:
                    sums(n + 1, 0, 1)
                mlp_gate(n, 1, 2)
                if ahead:
                    norms(n + 1, 0)
                mlp_residual(n, b, 1)

            dve.memset(hT[:, :, 0:1], 0.0)
            dve.memset(ones[:, :], 1.0 / D)
            dve.memset(one[:, :], 1.0)
            dve.memset(qTz[:, :, :, :], 0.0)
            dve.memset(w1_in[:, :, :], 0.0)
            dve.memset(w2_in[:, :, :], 0.0)
            dve.memset(vec_in[:, :], 0.0).then_inc(pads, 1)
            dve.wait_ge(pads, START + 1)
            with dve.Fori(0, g.depth) as l:
                dve.wait_ge(w_in, START + 16 * LOADS * (l + 1))
                dve.wait_ge(f_out, START + NG * B * l)
                dve.tensor_copy(wqkv_hi[:, :], wqkv_in[:, :]).then_inc(w_dve, 1)
                dve.tensor_copy(w1_hi[:, :, :], w1_in[:, :, :]).then_inc(w_dve, 1)
                dve.wait_ge(w_dve, START + 5 * l + 1)
                dve.tensor_tensor(wqkv_lo[:, :], wqkv_in[:, :], wqkv_hi[:, :].bitcast(F32), ALU.subtract).then_inc(w_dve, 1)
                dve.wait_ge(w_dve, START + 5 * l + 2)
                dve.tensor_tensor(w1_lo[:, :, :], w1_in[:, :, :], w1_hi[:, :, :].bitcast(F32), ALU.subtract).then_inc(w_dve, 1)
                dve.tensor_copy(vec[:, :], vec_in[:, :]).then_inc(w_dve, 1)
                dve.wait_ge(w_dve, START + 5 * l + 5)
                dve.sem_inc(w_used, 1)
                dve.wait_ge(w_pool, START + POOL_STEPS * (l + 1))
                dve.sem_inc(dve_gate, 1)
                dve.wait_ge(f_res, START + NG * B * l)
                shifted(l * B, 0)
                rotary_products(l * B, 0, 0)
                rotary_products(l * B, 0, 1)
                sums(l * B, 0, 0)
                sums(l * B, 0, 1)
                norms(l * B, 0)
                with dve.Fori(0, B - 1) as b:
                    sequence(l * B + b, b, True)
                sequence(l * B + (B - 1), B - 1, False)

        @block.gpsimd
        def _(pool):
            start_all(pool, sems)

            def mix(n, j):
                G = n * NB + j
                pool.wait_ge(v_ok, START + G + 1)
                pool.wait_ge(pvd, START + 2 * G)
                pool.sem_inc(pool_gate, 1)
                pool.tensor_copy(v_mix[0:P - W, :], v_s[0:P - W, j % 3, :]).then_inc(mixed, 1)
                pool.wait_ge(mixed, START + 2 * n * (NB - 1) + 2 * j - 1)
                pool.sem_inc(pool_gate, 1)
                pool.tensor_copy(v_mix[P - W:P, :], v_s[P - W:P, (j - 1) % 3, :]).then_inc(mixed, 1)
                pool.wait_ge(mixed, START + 2 * n * (NB - 1) + 2 * j)

            def rotate_q(n, j):
                G = n * NB + j
                pool.wait_ge(rot_mul, START + 2 * G + 1)
                if j > 0:
                    pool.wait_ge(qk_turned, START + 4 * n * NB + 4 * j - 2)
                pool.tensor_tensor(qkr[:, 0, :], byc[:, 0, :], bys[:, 0, :], ALU.add).then_inc(rotated, 1)

            def add_k(n, j):
                G = n * NB + j
                pool.wait_ge(rot_mul, START + 2 * G + 2)
                pool.tensor_tensor(byc[:, 1, :], byc[:, 1, :], bys[:, 1, :], ALU.add).then_inc(added, 1)

            def rotate_k(n, j):
                G = n * NB + j
                pool.wait_ge(added, START + G + 1)
                pool.wait_ge(norm_step, START + (ROOT + 1) * (G + 1))
                if j > 0:
                    pool.wait_ge(qk_turned, START + 4 * n * NB + 4 * j)
                pool.tensor_tensor(qkr[:, 1, :].rearrange("p (h d) -> p h d", d=HD),
                                   byc[:, 1, :].rearrange("p (h d) -> p h d", d=HD),
                                   rn[:, j % 2, 1, :].unsqueeze(2).broadcast_to([P, H, HD]),
                                   ALU.mult).then_inc(rotated, 1)

            def rotate(n, j):
                rotate_q(n, j)
                add_k(n, j)
                if j > 1:
                    mix(n, j - 1)
                rotate_k(n, j)

            def sequence(n, ahead):
                for j in range(1, NB):
                    rotate(n, j)
                mix(n, NB - 1)
                if ahead:
                    rotate(n + 1, 0)

            pool.wait_ge(pads, START + 1)
            with pool.Fori(0, g.depth) as l:
                pool.wait_ge(w_in, START + 16 * LOADS * (l + 1))
                pool.wait_ge(f_out, START + NG * B * l)
                pool.wait_ge(rotated, START + 2 * NB * B * l)
                for i in range(2):
                    s = scl_in[:, i, :].rearrange("p (s d) -> p s d", s=2)
                    pool.tensor_tensor(rot[:, i, 0, :, :], tabs[:, i, 0, :, :],
                                       scl_in[:, i, :].unsqueeze(1).broadcast_to([P, NB, HD]),
                                       ALU.mult).then_inc(w_pool, 1)
                    for a in range(2):
                        o = slice(a * HALF, (a + 1) * HALF)
                        pool.tensor_tensor(rot[:, i, 1, :, o], tabs[:, i, 1, :, o],
                                           s[:, 1 - a, :].unsqueeze(1).broadcast_to([P, NB, HALF]),
                                           ALU.mult).then_inc(w_pool, 1)
                pool.tensor_copy(wo_s[:, :, :], wo_in[:, :, :]).then_inc(w_pool, 1)
                pool.tensor_copy(w2_s[:, :, :], w2_in[:, :, :]).then_inc(w_pool, 1)
                pool.wait_ge(w_pool, START + POOL_STEPS * (l + 1))
                pool.sem_inc(w_used, 1)
                rotate(l * B, 0)
                with pool.Fori(0, B - 1) as b:
                    sequence(l * B + b, True)
                sequence(l * B + (B - 1), False)


def finish(nc, g, hT, ident, x1_d, out):
    GT = 4 * P
    PER = g.L // GT
    GROUPS = g.B * PER
    ctx = ExitStack()
    with ctx:
        x1 = ctx.enter_context(nc.sbuf_tensor("x1_back", [P, GROUPS, GT], F32))
        p_out = ctx.enter_context(nc.psum_tensor("p_out", [P, 2, GT], F32))
        loaded = ctx.enter_context(nc.semaphore("x1_loaded"))
        turned = ctx.enter_context(nc.semaphore("h_turned"))
        summed = ctx.enter_context(nc.semaphore("out_summed"))
        stored = ctx.enter_context(nc.semaphore("out_stored"))
        block = ctx.enter_context(nc.Block())

        @block.sync
        def _(sp):
            sp.dma_start(x1[:, :, :].rearrange("p g n -> p (g n)"), x1_d.rearrange("p k d -> p (k d)")).then_inc(loaded, 16)
            for t in range(GROUPS):
                b, h = t // PER, t % PER
                sp.wait_ge(summed, t + 1)
                sp.dma_start(out[b, h * GT:(h + 1) * GT, :].rearrange("(k p) d -> p k d", p=P),
                             x1[:, t, :].rearrange("p (k d) -> p k d", d=P)).then_inc(stored, 16)
            sp.wait_ge(stored, 16 * GROUPS)

        @block.tensor
        def _(pe):
            for t in range(GROUPS):
                if t >= 2:
                    pe.wait_ge(summed, t - 1)
                for k in range(4):
                    o = 1 + (t % PER) * GT + k * P
                    mm = pe.transpose(p_out[:, t % 2, k * P:(k + 1) * P], hT[:, t // PER, o:o + P], ident[:, :])
                mm.then_inc(turned, 1)

        @block.vector
        def _(dve):
            dve.wait_ge(loaded, 16)
            for t in range(GROUPS):
                dve.wait_ge(turned, t + 1)
                dve.tensor_tensor(x1[:, t, :], x1[:, t, :], p_out[:, t % 2, :], ALU.add).then_inc(summed, 1)


def build(nc, x, q_w, k_w, v_w, o_w, wqkv, qsc, ksc, wo, ln_g, ln_b, w1, b1, w2, b2,
          identity, identity_b, causal, bias, window_mask, rotary, out):
    g = Geometry(x, wqkv, qsc, w1, wo)
    parts_d = nc.dram_tensor("qk_parts", [g.B, 2, 3, g.D, g.L], BF16, kind="Internal").ap()
    x1_d = nc.dram_tensor("x1_kept", [P, g.B * g.blocks, g.D], F32, kind="Internal").ap()
    ctx = ExitStack()
    with ctx:
        def sb(name, shape, dt=F32):
            return ctx.enter_context(nc.sbuf_tensor(name, shape, dt))

        hT = sb("h_t", [P, g.B, 1 + g.L])
        ident = sb("ident", [P, P])
        identb = sb("ident_b", [P, P], BF16)
        cmask = sb("causal_mask", [P, P], BF16)
        maskt = sb("window_mask_s", [P, g.keys])
        consts = ctx.enter_context(nc.semaphore("consts"))
        with nc.Block() as block:
            @block.sync
            def _(sp):
                for dst, src in ((ident, identity), (identb, identity_b), (cmask, causal), (maskt, window_mask)):
                    sp.dma_start(dst[:, :], src).then_inc(consts, 16)
                sp.wait_ge(consts, 64)
        with ExitStack() as first:
            x_all = first.enter_context(nc.sbuf_tensor("x_all", [P, g.B * g.blocks, g.D], F32))
            va = first.enter_context(nc.sbuf_tensor("v_all", [P, g.B * g.blocks, g.a_heads, g.a_hd + 1], F32))
            prepare(nc, g, x_all, va, ident, x, q_w, k_w, v_w, parts_d)
            causal_attention(nc, g, x_all, va, ident, identb, cmask, o_w, parts_d, bias)
            hand_over(nc, g, x_all, hT, ident, x1_d)
        with ExitStack() as second:
            tabs = second.enter_context(nc.sbuf_tensor("rotary_s", [P, 2, 2, g.blocks, g.hd], F32))
            got = second.enter_context(nc.semaphore("rotary_in"))
            with nc.Block() as block:
                @block.sync
                def _(sp):
                    sp.dma_start(tabs[:, :, :, :, :], rotary).then_inc(got, 16)
                    sp.wait_ge(got, 16)
            deep_layers(nc, g, hT, ident, tabs, maskt, wqkv, qsc, ksc, wo, ln_g, ln_b, w1, b1, w2, b2)
        finish(nc, g, hT, ident, x1_d, out)


def _split3(a):
    bf = _bf16()
    h = a.astype(bf)
    m = (a - h.astype(np.float32)).astype(bf)
    low = (a - h.astype(np.float32) - m.astype(np.float32)).astype(bf)
    return [h, m, low]


def _bf16():
    return np.dtype("bfloat16")


def _alibi_rows(heads, length):
    ratio = 2.0 ** (-8.0 / heads)
    slopes = np.asarray([ratio ** (i + 1) for i in range(heads)], np.float32)
    pos = np.arange(length)
    at = [(pos // 8 * 8).astype(np.float32), (pos % 8).astype(np.float32)]
    rows = np.zeros((heads, 2, 12, length), _bf16())
    for n, s in enumerate(_split3(slopes)):
        for k in range(2):
            rows[:, 0, 2 * n + k] = s[:, None]
            rows[:, 1, 2 * n + k] = at[k]
            rows[:, 0, 6 + 2 * n + k] = at[k]
            rows[:, 1, 6 + 2 * n + k] = -s[:, None]
    return rows


def _rotary(length, hd, window, qk_scale):
    half = np.arange(0, hd, 2, dtype=np.float32)
    freq = (1.0 / 10000.0 ** (half / hd)).astype(np.float32)
    t = np.arange(length, dtype=np.float32)
    angle = np.tile(t[:, None] * freq[None, :], (1, 2)).astype(np.float64)
    base = ((half + 0.4 * hd) / (1.4 * hd)).astype(np.float64)
    scale = np.tile(base[None, :] ** ((t - length // 2) / (window // 2))[:, None], (1, 2))
    sign = np.repeat([-1.0, 1.0], hd // 2)
    c, s = np.cos(angle), np.sin(angle) * sign
    t4 = np.stack([np.stack([c * scale, s * scale]) * qk_scale, np.stack([c / scale, s / scale])])
    return np.ascontiguousarray(t4.reshape(2, 2, length // P, P, hd).transpose(3, 0, 1, 2, 4).astype(np.float32))


def _window_mask(window):
    q = np.arange(P)[:, None]
    k = np.arange(P + window)[None, :] - window
    seen = (k <= q) & (k >= q - window)
    return np.where(seen, 0.0, MASKED).astype(np.float32)


def kernel(**inputs):
    import concourse.bacc as _bacc
    from concourse.bass_utils import run_bass_kernel_spmd as _run

    nc = _bacc.Bacc("TRN2", target_bir_lowering=False, num_devices=1)
    names = ["L0_attn_x", "L0_attn_q_w", "L0_attn_k_w", "L0_attn_v_w", "L0_attn_o_w", "L0_ffn_Wqkv",
             "L0_ffn_q_scale", "L0_ffn_k_scale", "L0_ffn_Wo", "L0_ffn_ln_g", "L0_ffn_ln_b", "L0_ffn_W1",
             "L0_ffn_b1", "L0_ffn_W2", "L0_ffn_b2"]
    arrays = {f"in_{n}": np.ascontiguousarray(inputs[n]) for n in names}
    length = arrays["in_L0_attn_x"].shape[1]
    bf = _bf16()
    causal = np.where(np.arange(P)[None, :] > np.arange(P)[:, None], -1e30, 0.0)
    arrays |= {
        "c_identity": np.eye(P, dtype=np.float32),
        "c_identity_b": np.eye(P, dtype=np.float32).astype(bf),
        "c_causal": causal.astype(np.float32).astype(bf),
        "c_bias": _alibi_rows(16, length),
        "c_window": _window_mask(32),
        "c_rotary": _rotary(length, arrays["in_L0_ffn_q_scale"].shape[1], 32, 8.0),
    }
    args = [nc.dram_tensor(n, a.shape, mybir.dt.from_np(a.dtype), kind="ExternalInput").ap() for n, a in arrays.items()]
    shape = arrays["in_L0_attn_x"].shape
    args.append(nc.dram_tensor("out_0", shape, F32, kind="ExternalOutput").ap())
    build(nc, *args)
    r = _run(nc, [arrays], core_ids=[0])
    return r.results[0]["out_0"]
```

```python
import numpy as np
import concourse.bass as bass
from concourse import mybir
from contextlib import ExitStack

F32 = mybir.dt.float32
F32R = mybir.dt.float32r
BF16 = mybir.dt.bfloat16
ALU = mybir.AluOpType
ACT = mybir.ActivationFunctionType
X = mybir.AxisListType.X

P = 128
MASKED = -1e26
ROOT = 12
I32 = mybir.dt.int32


class Geometry:

    def __init__(self, x, wqkv, q_scale, w1, wo):
        self.B, self.L, self.D = x.shape
        self.depth = wqkv.shape[0]
        self.inner = wqkv.shape[2] // 3
        self.hd = q_scale.shape[1]
        self.heads = self.inner // self.hd
        self.ffn = w1.shape[2] // 2
        self.blocks = self.L // P
        self.window = 32
        self.keys = P + self.window
        self.chunks = self.inner // P
        self.fchunks = -(-self.ffn // P)
        self.a_heads, self.a_hd = 16, self.D // 16


START = 1


def start_all(eng, sems):
    for s in sems:
        eng.sem_inc(s, START)


def inverse_root(dve, y, x, xh, t, source, floor, op, step, base):
    dve.tensor_scalar(x, source, floor, None, op).then_inc(step, 1)
    dve.wait_ge(step, START + base + 1)
    dve.tensor_scalar(y.bitcast(I32), x.bitcast(I32), -0.5, float(0x5f3759df), ALU.mult, ALU.add).then_inc(step, 1)
    dve.tensor_scalar(xh, x, -0.5, None, ALU.mult).then_inc(step, 1)
    dve.wait_ge(step, START + base + 3)
    for k in range(3):
        dve.tensor_tensor(t, y, y, ALU.mult).then_inc(step, 1)
        dve.wait_ge(step, START + base + 4 + 3 * k)
        dve.tensor_tensor(t, t, xh, ALU.mult).then_inc(step, 1)
        dve.wait_ge(step, START + base + 5 + 3 * k)
        dve.scalar_tensor_tensor(y, t, 1.5, y, ALU.add, ALU.mult).then_inc(step, 1)
        dve.wait_ge(step, START + base + 6 + 3 * k)


class TokenNorm:

    GROUP = 4

    def __init__(self, nc, ctx, name, x_all, ident, turned_ps):
        def sb(part, shape):
            return ctx.enter_context(nc.sbuf_tensor(f"{name}_{part}", shape, F32))

        self.sems = []

        def sem(part):
            self.sems.append(ctx.enter_context(nc.semaphore(f"{name}_{part}")))
            return self.sems[-1]
        n = self.GROUP
        self.x_all, self.ident, self.ps = x_all, ident, turned_ps
        self.stats, self.mv = sb("stats", [P, n, 6]), sb("mv", [P, n, 2])
        self.root = sb("root", [P, 4, n])
        self.xn = sb("xn", [P, n, P])
        self.stat_step, self.root_step = sem("stat_step"), sem("root_step")
        self.normed, self.turned = sem("normed"), sem("turned")
        self.gate = sem("gate")

    def vector(self, dve, t):
        n = self.GROUP
        for k in range(n):
            dve.bn_stats(self.stats[:, k, :], self.x_all[:, t * n + k, :]).then_inc(self.stat_step, 1)
        dve.wait_ge(self.stat_step, START + 2 * n * t + n)
        dve.sem_inc(self.gate, 1)
        for k in range(n):
            dve.bn_aggr(self.mv[:, k, :], self.stats[:, k, :]).then_inc(self.stat_step, 1)
        dve.wait_ge(self.stat_step, START + 2 * n * (t + 1))
        r = self.root
        inverse_root(dve, r[:, 0, :], r[:, 1, :], r[:, 2, :], r[:, 3, :], self.mv[:, :, 1], 1e-5, ALU.add,
                     self.root_step, ROOT * t)
        dve.wait_ge(self.turned, START + t)
        for k in range(n):
            dve.tensor_scalar(self.xn[:, k, :], self.x_all[:, t * n + k, :], self.mv[:, k, 0:1],
                              r[:, 0, k:k + 1], ALU.subtract, ALU.mult).then_inc(self.normed, 1)

    def tensor(self, pe, t):
        n = self.GROUP
        pe.wait_ge(self.normed, START + n * (t + 1))
        for k in range(n):
            mm = pe.transpose(self.ps[:, k * P:(k + 1) * P], self.xn[:, k, :], self.ident[:, :])
        mm.then_inc(self.turned, 1)


def prepare(nc, g, x_all, va, ident, x, q_w, k_w, v_w, parts_d):
    B, L, D = g.B, g.L, g.D
    HA, HDA = g.a_heads, g.a_hd
    GT = 4 * P
    GROUPS = B * L // GT
    PER = L // GT
    ctx = ExitStack()
    with ctx:
        def sb(name, shape, dt=F32):
            return ctx.enter_context(nc.sbuf_tensor(name, shape, dt))

        def ps(name, shape):
            return ctx.enter_context(nc.psum_tensor(name, shape, F32))

        sems = []

        def sem(name):
            sems.append(ctx.enter_context(nc.semaphore(name)))
            return sems[-1]

        w = sb("w_qkv_a", [P, 3, D])
        xnT = sb("xnT", [P, GT])
        qkf = sb("qkf", [P, 2, GT])
        rest = sb("rest", [P, 2, GT])
        parts = sb("parts", [P, 2, 3, GT], BF16)
        p_turn = ps("p_turn", [P, GT])
        p_qk = ps("p_qk", [P, 2, GT])
        p_v = ps("p_v", [P, GT])
        x_in = sem("x_in")
        w_in = sem("a_w_in")
        xnT_ok = sem("xnT_ok")
        qk_done = sem("a_qk_done")
        v_done = sem("a_v_done")
        qkf_ok = sem("qkf_ok")
        va_ok = sem("va_ok")
        va_pad = sem("va_pad")
        split = sem("split_step")
        stored = sem("parts_stored")
        ln = TokenNorm(nc, ctx, "ln_a", x_all, ident, p_turn)
        block = ctx.enter_context(nc.Block())

        @block.gpsimd
        def _(pool):
            start_all(pool, sems + ln.sems)

        @block.sync
        def _(sp):
            for b in range(B):
                n = L // P
                sp.dma_start(x_all[:, b * n:(b + 1) * n, :], x[b].rearrange("(k p) d -> p k d", p=P)).then_inc(x_in, 16)
            for i, t in enumerate((q_w, k_w, v_w)):
                sp.dma_start(w[:, i, :], t).then_inc(w_in, 16)
            with sp.Fori(0, B) as b:
                for h in range(PER):
                    t = b * PER + h
                    sp.wait_ge(split, START + 8 * (t + 1))
                    for i in range(2):
                        sp.dma_start(parts_d[b, i, :, :, h * GT:(h + 1) * GT].rearrange("s p n -> p s n"),
                                     parts[:, i, :, :]).then_inc(stored, 16)
            sp.wait_ge(stored, START + 32 * GROUPS)

        @block.tensor
        def _(pe):
            pe.wait_ge(w_in, START + 48)
            with pe.Fori(0, GROUPS) as t:
                ln.tensor(pe, t)
                pe.wait_ge(xnT_ok, START + t + 1)
                pe.wait_ge(qkf_ok, START + t * 2)
                pe.wait_ge(va_ok, START + t)
                for i in range(2):
                    pe.matmul(p_qk[:, i, :], w[:, i, :], xnT[:, :], start=True, stop=True).then_inc(qk_done, 1)
                for k in range(4):
                    mm = pe.matmul(p_v[:, k * P:(k + 1) * P], xnT[:, k * P:(k + 1) * P], w[:, 2, :], start=True, stop=True)
                mm.then_inc(v_done, 1)

        @block.scalar
        def _(act):
            act.wait_ge(va_pad, START + 1)
            with act.Fori(0, GROUPS) as t:
                act.wait_ge(ln.turned, START + t + 1)
                act.wait_ge(v_done, START + t)
                act.activation(xnT[:, :], p_turn[:, :], ACT.Copy).then_inc(xnT_ok, 1)
                act.wait_ge(split, START + 8 * t)
                for i in range(2):
                    act.wait_ge(qk_done, START + 2 * t + i + 1)
                    act.activation(qkf[:, i, :], p_qk[:, i, :], ACT.Copy,
                                   scale=1.0 / float(np.sqrt(HDA)) if i == 0 else 1.0).then_inc(qkf_ok, 1)
                act.wait_ge(v_done, START + t + 1)
                act.activation(va[:, bass.ds(t * 4, 4), :, 0:HDA],
                               p_v[:, :].rearrange("p (k h d) -> p k h d", k=4, d=HDA), ACT.Copy).then_inc(va_ok, 1)

        @block.vector
        def _(dve):
            dve.memset(va[:, :, :, :], 1.0).then_inc(va_pad, 1)
            dve.wait_ge(x_in, START + 16 * B)

            def split_group(t):
                dve.wait_ge(stored, START + 32 * t)
                for i in range(2):
                    dve.wait_ge(qkf_ok, START + 2 * t + i + 1)
                    at = 8 * t + 4 * i
                    dve.tensor_copy(parts[:, i, 0, :], qkf[:, i, :]).then_inc(split, 1)
                    dve.wait_ge(split, START + at + 1)
                    dve.tensor_tensor(rest[:, i, :], qkf[:, i, :], parts[:, i, 0, :], ALU.subtract).then_inc(split, 1)
                    dve.wait_ge(split, START + at + 2)
                    dve.tensor_copy(parts[:, i, 1, :], rest[:, i, :]).then_inc(split, 1)
                    dve.wait_ge(split, START + at + 3)
                    dve.tensor_tensor(parts[:, i, 2, :], rest[:, i, :], parts[:, i, 1, :], ALU.subtract).then_inc(split, 1)

            ln.vector(dve, 0)
            with dve.Fori(0, GROUPS - 1) as t:
                ln.vector(dve, t + 1)
                split_group(t)
            split_group(GROUPS - 1)


def hand_over(nc, g, x_all, hT, ident, x1_d):
    GT = 4 * P
    PER = g.L // GT
    ctx = ExitStack()
    with ctx:
        p_turn = ctx.enter_context(nc.psum_tensor("p_turn2", [P, GT], F32))
        kept = ctx.enter_context(nc.semaphore("hT_kept"))
        stored = ctx.enter_context(nc.semaphore("x1_stored"))
        ln = TokenNorm(nc, ctx, "ln_b", x_all, ident, p_turn)
        block = ctx.enter_context(nc.Block())

        @block.gpsimd
        def _(pool):
            start_all(pool, [kept, stored] + ln.sems)

        @block.sync
        def _(sp):
            sp.dma_start(x1_d, x_all[:, :, :]).then_inc(stored, 16)
            sp.wait_ge(stored, START + 16)

        @block.vector
        def _(dve):
            with dve.Fori(0, g.B * PER) as t:
                ln.vector(dve, t)

        @block.tensor
        def _(pe):
            with pe.Fori(0, g.B * PER) as t:
                pe.wait_ge(kept, START + t)
                ln.tensor(pe, t)

        @block.scalar
        def _(act):
            with act.Fori(0, g.B) as b:
                for h in range(PER):
                    act.wait_ge(ln.turned, START + b * PER + h + 1)
                    act.activation(hT[:, b, 1 + h * GT:1 + (h + 1) * GT], p_turn[:, :], ACT.Copy).then_inc(kept, 1)


def causal_attention(nc, g, x_all, va, ident, identb, cmask, o_w, parts_d, bias_d):
    B, L, D = g.B, g.L, g.D
    HA, HDA = g.a_heads, g.a_hd
    NB = L // P
    QUADS = HA // 4
    ROWS = 9 * HDA
    MROW = 96
    PIECES = [(I, c, min(c + 512, P * (I + 1))) for I in range(NB) for c in range(0, P * (I + 1), 512)]
    PACKS = [[(0, 0)], [(1, 0), (7, 7 * P)], [(2, 0), (6, 6 * P)], [(3, 0), (5, 5 * P)], [(4, 0)]]
    NP = len(PACKS)
    NPI = 4 * len(PIECES)
    HEAD = 6
    TURN_AT = [NPI - 6] * (QUADS - 1) + [NPI - 18]
    ctx = ExitStack()
    with ctx:
        def sb(name, shape, dt=F32):
            return ctx.enter_context(nc.sbuf_tensor(name, shape, dt))

        def ps(name, shape):
            return ctx.enter_context(nc.psum_tensor(name, shape, F32))

        sems = []

        def sem(name):
            sems.append(ctx.enter_context(nc.semaphore(name)))
            return sems[-1]

        qst = sb("q_stack", [P, QUADS, 4, L], BF16)
        kst = sb("k_stack", [P, QUADS, 4, L], BF16)
        pt = sb("p_t", [P, 3, 4, L])
        vc = sb("v_cur", [P, NB, HA, HDA + 1])
        mx = sb("mx", [P, 2, 4, NB])
        mrow = sb("mrow", [32, P])
        mrest = sb("mrest", [32, P])
        mparts = sb("mparts", [32, 3, P], BF16)
        ot = sb("ot", [P, L])
        osum = sb("osum", [P, NB, 4])
        on = sb("on", [P, NB, D])
        onT = sb("onT", [P, L])
        wo = sb("wo_a", [P, D])
        p_max = ps("p_max", [P, 2, 512])
        p_exp = ps("p_exp", [P, 2, L])
        p_pv = ps("p_pv", [P, L])

        stacks_clear = sem("stacks_clear")
        k_ones = sem("k_ones")
        wo_in = sem("wo_a_in")
        stacked = [sem(f"stacked{q}") for q in range(QUADS)]
        maxed = sem("max_scores")
        m_read = sem("max_read")
        m_all = sem("max_merged")
        m_turn = sem("max_turned")
        m_step = sem("max_split_step")
        m_rows = sem("max_rows_in")
        st_done = sem("scores_t")
        ex_done = sem("exponentials")
        pv_done = sem("pv_a_done")
        packs_used = sem("packs_used")
        ot_ok = sem("ot_ok")
        ot_turn = sem("ot_turned")
        o_rec = sem("o_reciprocal")
        on_ok = sem("on_ok")
        on_turn = sem("on_turned")
        onT_ok = sem("onT_ok")
        proj_a = sem("o_projected")
        x1_ok = sem("x1_ok")
        v_cur = sem("v_cur_ok")
        dve_gate = sem("dve_gate_a")
        block = ctx.enter_context(nc.Block())
        STACK_DMAS = 2 * 9 + 2

        @block.gpsimd
        def _(pool):
            start_all(pool, sems)
            pool.memset(kst[:, :, :, :], 1.0).then_inc(k_ones, 1)
            pool.wait_ge(k_ones, START + 1)
            pool.memset(kst[0:MROW, :, :, :], 0.0).then_inc(stacks_clear, 1)

        @block.sync
        def _(sp):
            sp.dma_start(wo[:, :], o_w).then_inc(wo_in, 16)
            sp.wait_ge(stacks_clear, START + 2)

            def fill(b, q):
                s = q
                for a in range(3):
                    for c in range(3):
                        r = (a * 3 + c) * HDA
                        for i, (st, part) in enumerate(((qst, a), (kst, c))):
                            src = parts_d[b, i, part, 32 * q:32 * q + 32, :].rearrange("(h d) n -> d h n", d=HDA)
                            sp.dma_start(st[r:r + HDA, s, :, :], src).then_inc(stacked[s], 16)
                for i, st in enumerate((qst, kst)):
                    sp.dma_start(st[ROWS:ROWS + 12, s, :, :],
                                 bias_d[4 * q:4 * q + 4, i, :, :].rearrange("h r n -> r h n")).then_inc(stacked[s], 16)

            def max_rows(b, q):
                G = b * QUADS + q
                sp.wait_ge(m_step, START + 4 * (G + 1))
                for part in range(3):
                    dst = qst[MROW + part:MROW + part + 1, q, :, :].rearrange("p h (i n) -> p (h i) n", n=P)
                    sp.dma_start(dst, mparts[:, part, :]).then_inc(m_rows, 16)

            for q in range(QUADS):
                fill(0, q)
            max_rows(0, 0)
            with sp.Fori(0, B - 1) as b:
                for q in range(QUADS):
                    max_rows(b if q + 1 < QUADS else b + 1, (q + 1) % QUADS)
                    sp.wait_ge(st_done, START + 4 * NP * (b * QUADS + q + 1))
                    fill(b + 1, q)
            for q in range(1, QUADS):
                max_rows(B - 1, q)

        @block.tensor
        def _(pe):
            def max_piece(b, q, n):
                G = b * QUADS + q
                h, (I, c0, c1) = n // len(PIECES), PIECES[n % len(PIECES)]
                N = 4 * len(PIECES) + 1
                s = q
                if n == 0:
                    pe.wait_ge(stacked[s], START + 16 * STACK_DMAS * (b + 1))
                if n >= 2:
                    pe.wait_ge(m_read, START + N * G + n - 1)
                else:
                    pe.wait_ge(m_read, START + N * G)
                out = p_max[:, n % 2, 0:c1 - c0]
                diag = c1 == P * (I + 1)
                mm = pe.matmul(out, qst[0:MROW, s, h, P * I:P * (I + 1)], kst[0:MROW, s, h, c0:c1],
                               start=True, stop=not diag)
                if diag:
                    mm = pe.matmul(out[:, c1 - c0 - P:c1 - c0], identb[:, :], cmask[:, :], start=False, stop=True)
                mm.then_inc(maxed, 1)

            def turn_max(b, q):
                G = b * QUADS + q
                pe.wait_ge(m_all, START + G + 1)
                pe.transpose(p_max[0:32, 0, 0:P], mx[:, 0, :, :].rearrange("p h i -> p (h i)"),
                             ident[:, :]).then_inc(m_turn, 1)

            def scores_t(b, q, k, h):
                G = b * QUADS + q
                U = 4 * NP * G + 4 * k + h
                if k == 0 and h == 0:
                    pe.wait_ge(m_rows, START + 16 * 3 * (G + 1))
                if 4 * k + h >= 2:
                    pe.wait_ge(ex_done, START + U - 1)
                else:
                    pe.wait_ge(ex_done, START + 4 * NP * G)
                s = q
                for J, at in PACKS[k]:
                    lo = J * P
                    while lo < L:
                        o = at + lo - J * P
                        hi = min(L, lo + 512 - o % 512)
                        diag = lo == J * P
                        mm = pe.matmul(p_exp[:, h % 2, o:o + hi - lo], kst[:, s, h, J * P:(J + 1) * P],
                                       qst[:, s, h, lo:hi], start=True, stop=not diag)
                        if diag:
                            mm = pe.matmul(p_exp[:, h % 2, o:o + P], cmask[:, :], identb[:, :],
                                           start=False, stop=True)
                        lo = hi
                mm.then_inc(st_done, 1)

            def pv(b, q, k):
                G = b * QUADS + q
                K = NP * q + k
                pe.wait_ge(ex_done, START + 4 * (NP * G + k + 1))
                if k == 0:
                    pe.wait_ge(v_cur, START + b + 1)
                    pe.wait_ge(on_ok, START + G)
                    pe.wait_ge(x1_ok, START + b)
                for J, at in PACKS[k]:
                    for seg in range(2):
                        lo, hi = max(J * P, 512 * seg), 512 * (seg + 1)
                        if lo >= hi:
                            continue
                        for h in range(4):
                            o = at + lo - J * P
                            mm = pe.matmul(p_pv[32 * h:32 * h + HDA + 1, lo:hi], vc[:, J, 4 * q + h, :],
                                           pt[:, K % 3, h, o:o + hi - lo], start=(J == 0), stop=(k == NP - 1),
                                           skip_group_check=True)
                mm.then_inc(pv_done, 1)

            def turn_o(b, q):
                G = b * QUADS + q
                pe.wait_ge(ot_ok, START + G + 1)
                for i in range(NB):
                    mm = pe.transpose(p_pv[:, i * P:(i + 1) * P], ot[:, i * P:(i + 1) * P], ident[:, :])
                mm.then_inc(ot_turn, 1)

            def turn_all(b):
                pe.wait_ge(on_ok, START + QUADS * (b + 1))
                for i in range(NB):
                    mm = pe.transpose(p_pv[:, i * P:(i + 1) * P], on[:, i, :], ident[:, :])
                mm.then_inc(on_turn, 1)

            def out_proj(b):
                pe.wait_ge(onT_ok, START + b + 1)
                for i in range(NB):
                    mm = pe.matmul(p_pv[:, i * P:(i + 1) * P], onT[:, i * P:(i + 1) * P], wo[:, :], start=True, stop=True)
                mm.then_inc(proj_a, 1)

            def quad(b, q, ahead):
                after = (b, q + 1) if q + 1 < QUADS else (b + 1, 0)
                done = [0]

                def pieces(upto):
                    while ahead and done[0] < upto:
                        max_piece(*after, done[0])
                        done[0] += 1

                first, last = HEAD, TURN_AT[q]
                pieces(first)
                for k in range(NP):
                    for h in range(4):
                        scores_t(b, q, k, h)
                        pieces(first + (last - first) * (4 * k + h + 1) // (4 * NP))
                    if k >= 1:
                        pv(b, q, k - 1)
                pv(b, q, NP - 1)
                pieces(last + 3)
                turn_o(b, q)
                if q == QUADS - 1:
                    pieces(last + 6)
                    turn_all(b)
                    pieces(last + 9)
                    out_proj(b)
                pieces(NPI)
                if ahead:
                    turn_max(*after)

            pe.wait_ge(wo_in, START + 16)
            for n in range(NPI):
                max_piece(0, 0, n)
            turn_max(0, 0)
            with pe.Fori(0, B - 1) as b:
                for q in range(QUADS):
                    quad(b, q, True)
            for q in range(QUADS):
                quad(B - 1, q, q + 1 < QUADS)

        @block.scalar
        def _(act):
            with act.Fori(0, B) as b:
                for q in range(QUADS):
                    G = b * QUADS + q
                    for k in range(NP):
                        K = NP * q + k
                        for h in range(4):
                            U = 4 * NP * G + 4 * k + h
                            act.wait_ge(st_done, START + U + 1)
                            if h == 0:
                                if K >= 3:
                                    act.wait_ge(pv_done, START + NP * QUADS * b + K - 2)
                                else:
                                    act.wait_ge(pv_done, START + NP * QUADS * b)
                            w = L if k < NP - 1 else L // 2
                            act.activation(pt[:, K % 3, h, 0:w], p_exp[:, h % 2, 0:w], ACT.Exp).then_inc(ex_done, 1)
                    act.wait_ge(pv_done, START + NP * (G + 1))
                    act.activation(ot[:, :], p_pv[:, :], ACT.Copy).then_inc(ot_ok, 1)
                act.wait_ge(on_turn, START + b + 1)
                act.activation(onT[:, :], p_pv[:, :], ACT.Copy).then_inc(onT_ok, 1)

        @block.vector
        def _(dve):
            def maxima(b, q, lo, hi):
                G = b * QUADS + q
                for n in range(lo, hi):
                    h, (I, c0, c1) = n // len(PIECES), PIECES[n % len(PIECES)]
                    dve.wait_ge(maxed, START + NPI * G + n + 1)
                    dve.tensor_reduce(mx[:, c0 // 512, h, I:I + 1], p_max[:, n % 2, 0:c1 - c0], X, ALU.max)\
                       .then_inc(m_read, 1)

            def merge(b, q):
                G = b * QUADS + q
                N = NPI + 1
                dve.wait_ge(m_read, START + N * G + NPI)
                half = 512 // P
                dve.tensor_tensor(mx[:, 0, :, half:NB], mx[:, 0, :, half:NB], mx[:, 1, :, half:NB], ALU.max)\
                   .then_inc(m_all, 1)
                dve.wait_ge(m_turn, START + G + 1)
                dve.wait_ge(m_rows, START + 16 * 3 * G)
                dve.tensor_scalar(mrow[:, :], p_max[0:32, 0, 0:P], -1.0, None, ALU.mult).then_inc(m_read, 1)
                dve.wait_ge(m_read, START + N * (G + 1))
                dve.tensor_copy(mparts[:, 0, :], mrow[:, :]).then_inc(m_step, 1)
                dve.wait_ge(m_step, START + 4 * G + 1)
                dve.tensor_tensor(mrest[:, :], mrow[:, :], mparts[:, 0, :], ALU.subtract).then_inc(m_step, 1)
                dve.wait_ge(m_step, START + 4 * G + 2)
                dve.tensor_copy(mparts[:, 1, :], mrest[:, :]).then_inc(m_step, 1)
                dve.wait_ge(m_step, START + 4 * G + 3)
                dve.tensor_tensor(mparts[:, 2, :], mrest[:, :], mparts[:, 1, :], ALU.subtract).then_inc(m_step, 1)

            def normalise(b, q):
                G = b * QUADS + q
                dve.wait_ge(ot_turn, START + G + 1)
                o = p_pv[:, :].rearrange("p (i h r) -> p i h r", h=4, r=32)
                dve.reciprocal(osum[:, :, :], o[:, :, :, HDA]).then_inc(o_rec, 1)
                dve.wait_ge(o_rec, START + G + 1)
                dve.wait_ge(on_turn, START + b)
                dve.tensor_tensor(on[:, :, 32 * q:32 * q + 32].rearrange("p i (h d) -> p i h d", d=HDA),
                                  o[:, :, :, 0:HDA], osum[:, :, :].unsqueeze(3).broadcast_to([P, NB, 4, HDA]),
                                  ALU.mult).then_inc(on_ok, 1)

            dve.memset(qst[:, :, :, :], 0.0)
            dve.memset(p_pv[:, :], 0.0).then_inc(stacks_clear, 1)
            def take_v(b):
                dve.wait_ge(proj_a, START + b)
                dve.sem_inc(dve_gate, 1)
                dve.tensor_copy(vc[:, :, :, :], va[:, bass.ds(b * NB, NB), :, :]).then_inc(v_cur, 1)

            def quad(b, q, ahead):
                after = (b, q + 1) if q + 1 < QUADS else (b + 1, 0)
                at = TURN_AT[q] + 3
                if ahead:
                    maxima(*after, 0, at)
                normalise(b, q)
                if q == QUADS - 1:
                    if ahead:
                        maxima(*after, at, at + 8)
                    dve.wait_ge(proj_a, START + b + 1)
                    xb = x_all[:, bass.ds(b * NB, NB), :]
                    dve.tensor_tensor(xb, xb, p_pv[:, :].rearrange("p (i n) -> p i n", n=P), ALU.add).then_inc(x1_ok, 1)
                    if ahead:
                        take_v(b + 1)
                        at += 8
                if ahead:
                    maxima(*after, at, NPI)
                    merge(*after)

            take_v(0)
            maxima(0, 0, 0, NPI)
            merge(0, 0)
            with dve.Fori(0, B - 1) as b:
                for q in range(QUADS):
                    quad(b, q, True)
            for q in range(QUADS):
                quad(B - 1, q, q + 1 < QUADS)


def deep_layers(nc, g, hT, ident, tabs, maskt, wqkv, qsc, ksc, wo, ln_g, ln_b, w1, b1, w2, b2):
    B, L, D = g.B, g.L, g.D
    NB, H, HD, CH, W, KEYS = g.blocks, g.heads, g.hd, g.chunks, g.window, g.keys
    HALF = HD // 2
    IN = g.inner
    FC = g.fchunks
    F = g.ffn
    GT = 512
    NG = L // GT
    PAIRS = H // 2
    QUADS = H // 4

    ctx = ExitStack()
    with ctx:
        def sb(name, shape, dt=F32):
            return ctx.enter_context(nc.sbuf_tensor(name, shape, dt))

        def ps(name, shape):
            return ctx.enter_context(nc.psum_tensor(name, shape, F32))

        sems = []

        def sem(name):
            sems.append(ctx.enter_context(nc.semaphore(name)))
            return sems[-1]

        wqkv_in = sb("wqkv_in", [P, 3 * IN])
        wqkv_hi = sb("wqkv_hi", [P, 3 * IN], F32R)
        wqkv_lo = sb("wqkv_lo", [P, 3 * IN], F32R)
        wo_in = sb("wo_in", [P, CH, D])
        wo_s = sb("wo_s", [P, CH, D])
        w1_in = sb("w1_in", [P, 2 * FC, P])
        w1_hi = sb("w1_hi", [P, 2 * FC, P], F32R)
        w1_lo = sb("w1_lo", [P, 2 * FC, P], F32R)
        w2_in = sb("w2_in", [P, FC, D])
        w2_s = sb("w2_s", [P, FC, D])
        vec_in = sb("vec_in", [P, 2 * FC + 3])
        vec = sb("vec", [P, 2 * FC + 3])
        scl_in = sb("scl_in", [P, 2, HD])
        rot = sb("rot", [P, 2, 2, NB, HD])
        xs_hi = sb("xs_hi", [P, L], F32R)
        xs_lo = sb("xs_lo", [P, L], F32R)
        sq = sb("sq", [P, 2, IN])
        ss = sb("ss", [P, 2, H])
        rn = sb("rn", [P, 2, 2, H])
        nx = sb("nx", [P, 2, H])
        nxh = sb("nxh", [P, 2, H])
        nt = sb("nt", [P, 2, H])
        mroot = sb("mroot", [P, 4, GT // P])
        one = sb("one", [P, P])
        byc = sb("byc", [P, 2, IN])
        bys = sb("bys", [P, 2, IN])
        qkr = sb("qkr", [P, 2, IN])
        v_s = sb("v_s", [P, 3, IN])
        v_mix = sb("v_mix", [P, IN])
        qTz = sb("qTz", [P, CH, 2, P])
        kT = sb("kT", [P, CH, W + 2 * P])
        pr = sb("pr", [P, H, KEYS])
        nmax = sb("nmax", [P, H])
        psumr = sb("psumr", [P, H])
        rsum = sb("rsum", [P, H])
        pT = sb("pT", [P, H, P])
        oT = sb("oT", [P, CH, P])
        ones = sb("ones", [P, P])
        fs = sb("fs", [P, L])
        cen = sb("cen", [P, GT])
        csq = sb("csq", [P, GT])
        rstd = sb("rstd", [P, GT])
        xn = cen
        xg = csq
        xg_hi = sb("xg_hi", [P, GT], F32R)
        xg_lo = sb("xg_lo", [P, GT], F32R)
        gl = sb("gl", [P, FC, GT])
        u = gl
        o_s = gl

        pq = ps("pq", [P, 2, 2, 512])
        psc = ps("psc", [P, 2, 512])
        ptr = ps("ptr", [P, 2, 512])

        w_in = sem("w_in")
        w_used = sem("w_used")
        w_pool = sem("w_pool")
        w_dve = sem("w_dve")
        pads = sem("pads")
        dve_gate = sem("dve_gate")
        pool_gate = sem("pool_gate")
        xs_sem = sem("xs_split")
        proj = sem("projected")
        squared = sem("squared")
        summed = sem("squares_summed")
        norm_step = sem("norm_step")
        root_step = sem("mlp_root_step")
        rot_mul = sem("rotary_products")
        added = sem("rotary_added")
        rotated = sem("rotated")
        qk_turned = sem("qk_turned")
        qk_kept = sem("qk_kept")
        p_turned = sem("p_turned")
        p_kept = sem("p_kept")
        o_turned = sem("o_turned")
        o_kept = sem("o_kept")
        kcopy = sem("k_prev_copied")
        scored = sem("scored")
        maxed = sem("maxed")
        exped = sem("exped")
        recip = sem("recip")
        pprev = sem("prev_turned")
        mixed = sem("v_mixed")
        v_ok = sem("v_ready")
        pvd = sem("pv_done")
        o_norm = sem("o_normalised")
        wod = sem("wo_done")
        resid = sem("attn_residual")
        fsh = sem("ffn_shift")
        f_mean = sem("f_mean")
        f_cen = sem("f_cen")
        f_sq = sem("f_sq")
        f_var = sem("f_var")
        f_rstd = sem("f_rstd")
        f_spread = sem("f_spread")
        f_xn = sem("f_xn")
        f_xg = sem("f_xg")
        f_hi = sem("f_hi")
        f_lo = sem("f_lo")
        f_gate = sem("f_gate")
        f_a = sem("f_a")
        f_gelu = sem("f_gelu")
        f_u = sem("f_u")
        f_out = sem("f_out")
        f_res = sem("f_res")

        def wo_bank(j):
            return pq[:, 0, 0, 0:P] if j + 1 < NB else psc[:, 1, 0:P]

        def mlp_banks(t):
            if t == 0:
                return pq[:, 0, 0, :], pq[:, 0, 1, :], pq[:, 1, 0, :], pq[:, 1, 1, :]
            return psc[:, 0, :], psc[:, 1, :], ptr[:, 0, :], ptr[:, 1, :]

        block = ctx.enter_context(nc.Block())

        NVEC = 2 * FC + 3
        b1v = b1.rearrange("l (s f) -> l s f", s=2)
        LOADS = 2 + 2 * (2 + FC) + 2 + 3 + 2
        POOL_STEPS = 2 * 3 + 2

        @block.sync
        def _(sp):
            def load(l):
                sp.dma_start(wqkv_in[:, :], wqkv[l]).then_inc(w_in, 16)
                sp.dma_start(wo_in[:, :, :], wo[l].rearrange("(c p) n -> p c n", p=P)).then_inc(w_in, 16)
                for s in range(2):
                    full = F // P * P
                    sp.dma_start(w1_in[:, s * FC:s * FC + F // P, :],
                                 w1[l, :, s * F:s * F + full].rearrange("d (c f) -> d c f", f=P)).then_inc(w_in, 16)
                    sp.dma_start(w1_in[:, s * FC + F // P, 0:F - full],
                                 w1[l, :, s * F + full:(s + 1) * F]).then_inc(w_in, 16)
                    for c in range(FC):
                        m = min(P, F - c * P)
                        sp.dma_start(vec_in[0:m, s * FC + c:s * FC + c + 1],
                                     b1v[l, s, c * P:c * P + m].unsqueeze(1)).then_inc(w_in, 16)
                sp.dma_start(w2_in[:, 0:F // P, :],
                             w2[l, 0:F // P * P, :].rearrange("(c p) n -> p c n", p=P)).then_inc(w_in, 16)
                sp.dma_start(w2_in[0:F - F // P * P, F // P, :], w2[l, F // P * P:F, :]).then_inc(w_in, 16)
                for i, t in enumerate((ln_g, ln_b, b2)):
                    sp.dma_start(vec_in[:, 2 * FC + i:2 * FC + i + 1], t[l].unsqueeze(1)).then_inc(w_in, 16)
                for i, t in enumerate((qsc, ksc)):
                    sp.dma_start(scl_in[:, i, :], t[l].partition_broadcast(P)).then_inc(w_in, 16)

            def mix(n):
                for j in range(1, NB):
                    G = n * NB + j
                    sp.wait_ge(v_ok, START + G + 1)
                    sp.wait_ge(pvd, START + 2 * G)
                    sp.dma_start(v_mix[0:P - W, :], v_s[0:P - W, j % 3, :]).then_inc(mixed, 16)
                    sp.dma_start(v_mix[P - W:P, :], v_s[P - W:P, (j - 1) % 3, :]).then_inc(mixed, 16)

            sp.wait_ge(pads, START + 1)
            load(0)
            with sp.Fori(0, g.depth - 1) as l:
                sp.wait_ge(w_used, START + 2 * l + 2)
                load(l + 1)
                with sp.Fori(0, B) as b:
                    mix(l * B + b)
            with sp.Fori(0, B) as b:
                mix((g.depth - 1) * B + b)

        @block.tensor
        def _(pe):
            def project(n, j, part):
                G = n * NB + j
                if part == 0 and j > 2:
                    pe.wait_ge(resid, START + n * NB + j - 2)
                if part == 0 and j > 0:
                    pe.wait_ge(rot_mul, START + 2 * n * NB + 2 * j - 1)
                    pe.wait_ge(squared, START + 2 * n * NB + 2 * j - 1)
                if part == 1:
                    pe.wait_ge(v_ok, START + G)
                if part == 2:
                    pe.wait_ge(rot_mul, START + 2 * G + 2)
                    pe.wait_ge(squared, START + 2 * G + 2)
                tok = slice(j * P, (j + 1) * P)
                for c in range(IN // 512):
                    col = slice(part * IN + c * 512, part * IN + (c + 1) * 512)
                    out = pq[:, min(part, 1), c, :]
                    pe.matmul(out, xs_hi[:, tok], wqkv_hi[:, col], start=True, stop=False)
                    pe.matmul(out, xs_hi[:, tok], wqkv_lo[:, col], start=False, stop=False)
                    mm = pe.matmul(out, xs_lo[:, tok], wqkv_hi[:, col], start=False, stop=True)
                mm.then_inc(proj, 1)

            def turn_qk(n, j, which):
                G = n * NB + j
                for t in which:
                    part, half = 1 - t // 2, t % 2
                    pe.wait_ge(rotated, START + 2 * G + t // 2 + 1)
                    if t >= 2:
                        pe.wait_ge(qk_kept, START + 4 * G + t - 1)
                    for c in range(4):
                        s = (half * 4 + c) * P
                        mm = pe.transpose(ptr[:, t % 2, c * P:(c + 1) * P], qkr[:, part, s:s + P], ident[:, :])
                    mm.then_inc(qk_turned, 1)

            def scores(n, j, p):
                G = n * NB + j
                if p == 0:
                    pe.wait_ge(qk_kept, START + 4 * G + 4)
                    pe.wait_ge(kcopy, START + n * (NB // 2 - 1) + j // 2)
                    pe.wait_ge(maxed, START + PAIRS * G)
                if p >= 2:
                    pe.wait_ge(maxed, START + PAIRS * G + p - 1)
                k0 = (j % 2) * P
                for h in range(2):
                    if j == 0:
                        rhs = kT[:, p, W:W + P]
                        out = psc[:, p % 2, h * 256 + W:h * 256 + KEYS]
                    else:
                        rhs = kT[:, p, k0:k0 + KEYS]
                        out = psc[:, p % 2, h * 256:h * 256 + KEYS]
                    mm = pe.matmul(out, qTz[:, p, h, :], rhs, start=True, stop=True)
                mm.then_inc(scored, 1)

            def turn_p(n, j, q):
                G = n * NB + j
                pe.wait_ge(exped, START + PAIRS * G + 2 * q + 2)
                for i in range(4):
                    mm = pe.transpose(ptr[:, q % 2, i * P:(i + 1) * P], pr[:, 4 * q + i, W:KEYS], ident[:, :])
                mm.then_inc(p_turned, 1)

            def values(n, j, q):
                G = n * NB + j
                pe.wait_ge(p_kept, START + 4 * G + 1 + q)
                if q == 0:
                    pe.wait_ge(v_ok, START + G + 1)
                    pe.wait_ge(maxed, START + PAIRS * (G + 1))
                    if j > 0:
                        pe.wait_ge(mixed, START + 32 * (n * (NB - 1) + j))
                if j > 0:
                    pe.wait_ge(pprev, START + n * (QUADS * (NB - 1)) + QUADS * (j - 1) + q + 1)
                for i in range(4):
                    h = 4 * q + i
                    for s in range(2):
                        v = v_mix[:, h * HD:(h + 1) * HD] if s == 0 and j > 0 else v_s[:, j % 3, h * HD:(h + 1) * HD]
                        mm = pe.matmul(psc[64 * s:64 * s + 64, q // 2, h % 8 * HD:(h % 8 + 1) * HD],
                                       pT[:, h, 64 * s:64 * s + 64], v, start=True, stop=True)
                if q % 2:
                    mm.then_inc(pvd, 1)

            def turn_o(n, j, c):
                G = n * NB + j
                pe.wait_ge(o_norm, START + 2 * G + c + 1)
                if j + 1 < NB:
                    pe.wait_ge(qk_kept, START + 4 * G + 7 + c)
                for i in range(4):
                    mm = pe.transpose(ptr[:, c, i * P:(i + 1) * P], o_s[:, c, i * P:(i + 1) * P], ident[:, :])
                mm.then_inc(o_turned, 1)

            def out_proj(n, j):
                G = n * NB + j
                if j + 1 < NB:
                    pe.wait_ge(rot_mul, START + 2 * G + 3)
                    pe.wait_ge(squared, START + 2 * G + 3)
                for c in range(CH):
                    if c % 4 == 0:
                        pe.wait_ge(o_kept, START + 2 * G + 1 + c // 4)
                    mm = pe.matmul(wo_bank(j), wo_s[:, c, :], oT[:, c, :], start=(c == 0), stop=(c == CH - 1))
                mm.then_inc(wod, 1)

            def mlp_mean(n, t):
                M = n * NG + t
                if t == 0:
                    pe.wait_ge(rot_mul, START + 2 * NB * n + 2 * NB)
                    pe.wait_ge(squared, START + 2 * NB * n + 2 * NB)
                    pe.wait_ge(v_ok, START + NB * n + NB)
                pe.wait_ge(fsh, START + M + 1)
                pe.matmul(mlp_banks(t)[0], ones[:, :], fs[:, t * GT:(t + 1) * GT], start=True, stop=True).then_inc(f_mean, 1)

            def mlp_var(n, t):
                M = n * NG + t
                pe.wait_ge(f_sq, START + M + 1)
                for k in range(GT // P):
                    mm = pe.matmul(mlp_banks(t)[1][:, k:k + 1], csq[:, k * P:(k + 1) * P], ones[:, 0:1], start=True, stop=True)
                mm.then_inc(f_var, 1)

            def mlp_spread(n, t):
                M = n * NG + t
                pe.wait_ge(f_rstd, START + M + 1)
                pe.matmul(mlp_banks(t)[1], one[:, :], rstd[:, :], start=True, stop=True).then_inc(f_spread, 1)

            def mlp_up(n, t, c):
                M = n * NG + t
                bank = mlp_banks(t)
                if c == 0:
                    pe.wait_ge(f_lo, START + M + 1)
                for s in (1, 0):
                    if c == 2:
                        pe.wait_ge(f_gelu if s else f_u, START + FC * M + 1)
                    ch = s * FC + c
                    out = bank[(3 if c % 2 == 0 else 1) - s]
                    pe.matmul(out, w1_hi[:, ch, :], xg_hi[:, :], start=True, stop=False)
                    pe.matmul(out, w1_hi[:, ch, :], xg_lo[:, :], start=False, stop=False)
                    pe.matmul(out, w1_lo[:, ch, :], xg_hi[:, :], start=False, stop=True)\
                        .then_inc(f_gate if s else f_a, 1)

            def mlp_down(n, t):
                M = n * NG + t
                for c in (1, 0, 2):
                    pe.wait_ge(f_u, START + FC * M + max(c, 1) + 1)
                    mm = pe.matmul(mlp_banks(t)[0], w2_s[:, c, :], u[:, c, :], start=(c == 1), stop=(c == 2))
                mm.then_inc(f_out, 1)

            def sequence(l, n, ahead, after=None):
                for i in range(NB + 1):
                    last = i == NB
                    if i + 1 < NB:
                        project(n, i + 1, 0)
                        project(n, i + 1, 1)
                    if last:
                        mlp_mean(n, 0)
                    if i >= 1:
                        values(n, i - 1, 0)
                        turn_p(n, i - 1, 2)
                        values(n, i - 1, 1)
                        turn_p(n, i - 1, 3)
                    if last:
                        mlp_var(n, 0)
                    if i >= 1:
                        values(n, i - 1, 2)
                    if i == 0:
                        pe.wait_ge(f_res, START + NG * n)
                    if not last:
                        turn_qk(n, i, (0,))
                    if i >= 1:
                        values(n, i - 1, 3)
                    if not last:
                        turn_qk(n, i, (1, 2, 3))
                    if last:
                        mlp_spread(n, 0)
                    if i >= 1:
                        turn_o(n, i - 1, 0)
                        turn_o(n, i - 1, 1)
                    if i + 1 < NB:
                        project(n, i + 1, 2)
                    if i == 1:
                        pe.wait_ge(w_pool, START + POOL_STEPS * (l + 1))
                    if i >= 1:
                        out_proj(n, i - 1)
                    if not last:
                        for p in range(PAIRS):
                            if p >= PAIRS - 2:
                                turn_p(n, i, p - (PAIRS - 2))
                            scores(n, i, p)
                pe.wait_ge(w_dve, START + 5 * (l + 1))
                mlp_up(n, 0, 0)
                mlp_up(n, 0, 1)
                mlp_mean(n, 1)
                mlp_up(n, 0, 2)
                mlp_var(n, 1)
                mlp_down(n, 0)
                if after is not None:
                    pe.wait_ge(w_dve, START + 5 * after + 2)
                if ahead:
                    pe.wait_ge(xs_sem, START + 4 * n + 8)
                    pe.wait_ge(f_res, START + NG * n + 1)
                    project(n + 1, 0, 0)
                    project(n + 1, 0, 1)
                mlp_spread(n, 1)
                for c in range(FC):
                    mlp_up(n, 1, c)
                if ahead:
                    project(n + 1, 0, 2)
                mlp_down(n, 1)

            pe.wait_ge(pads, START + 1)
            pe.wait_ge(w_dve, START + 2)
            pe.wait_ge(xs_sem, START + 4)
            for part in range(3):
                project(0, 0, part)

            def layer(l, after):
                with pe.Fori(0, B - 1) as b:
                    sequence(l, l * B + b, True)
                sequence(l, l * B + (B - 1), after is not None, after)

            with pe.Fori(0, g.depth - 1) as l:
                layer(l, l + 1)
            layer(g.depth - 1, None)

        @block.scalar
        def _(act):
            def square(n, j, part):
                G = n * NB + j
                act.wait_ge(rot_mul, START + 2 * G + part + 1)
                act.wait_ge(summed, START + 2 * G)
                act.activation(sq[:, part, :], pq[:, part, :, :].rearrange("p a n -> p (a n)"),
                               ACT.Square).then_inc(squared, 1)

            def keep_v(n, j):
                G = n * NB + j
                act.wait_ge(proj, START + 3 * G + 3)
                if j > 2:
                    act.wait_ge(mixed, START + 32 * (n * (NB - 1) + j - 2))
                act.activation(v_s[:, j % 3, :], pq[:, 1, :, :].rearrange("p a n -> p (a n)"),
                               ACT.Copy).then_inc(v_ok, 1)

            def keep_qk(n, j, which):
                G = n * NB + j
                for t in which:
                    part, half = 1 - t // 2, t % 2
                    act.wait_ge(qk_turned, START + 4 * G + t + 1)
                    src = ptr[:, t % 2, :].rearrange("p (c n) -> p c n", c=4)
                    if part == 0:
                        act.activation(qTz[0:64, 4 * half:4 * half + 4, 0, :], src[0:64], ACT.Copy)
                        op = act.activation(qTz[64:P, 4 * half:4 * half + 4, 1, :], src[64:P], ACT.Copy)
                    else:
                        o = W + (j % 2) * P
                        op = act.activation(kT[:, 4 * half:4 * half + 4, o:o + P], src, ACT.Copy)
                    op.then_inc(qk_kept, 1)
                    if t == 3 and j % 2 == 0 and j > 0:
                        act.wait_ge(qk_kept, START + 4 * G)
                        act.activation(kT[:, :, 0:W], kT[:, :, 2 * P:2 * P + W], ACT.Copy).then_inc(kcopy, 1)

            def exps(n, j, p):
                G = n * NB + j
                act.wait_ge(maxed, START + PAIRS * G + p + 1)
                if p == 0:
                    act.wait_ge(recip, START + G)
                k0 = W if j == 0 else 0
                for h in (2 * p, 2 * p + 1):
                    op = act.activation(pr[:, h, k0:KEYS], pr[:, h, k0:KEYS], ACT.Exp, bias=nmax[:, h:h + 1],
                                        scale=-1.0, accum_out=psumr[:, h:h + 1])
                op.then_inc(exped, 1)

            def keep_p(n, j, q):
                G = n * NB + j
                act.wait_ge(p_turned, START + 4 * G + 1 + q)
                act.activation(pT[:, 4 * q:4 * q + 4, :].rearrange("p h n -> p (h n)"), ptr[:, q % 2, :],
                               ACT.Copy).then_inc(p_kept, 1)

            def keep_o(n, j, c):
                G = n * NB + j
                act.wait_ge(o_turned, START + 2 * G + c + 1)
                act.activation(oT[:, 4 * c:4 * c + 4, :].rearrange("p h n -> p (h n)"), ptr[:, c, :],
                               ACT.Copy).then_inc(o_kept, 1)

            def mlp_square(n, t):
                M = n * NG + t
                act.wait_ge(f_cen, START + M + 1)
                act.wait_ge(f_lo, START + M)
                act.activation(csq[:, :], cen[:, :], ACT.Square).then_inc(f_sq, 1)

            def mlp_gain(n, t):
                M = n * NG + t
                act.wait_ge(f_xn, START + M + 1)
                act.activation(xg[:, :], xn[:, :], ACT.Identity, bias=vec[:, 2 * FC + 1:2 * FC + 2],
                               scale=vec[:, 2 * FC:2 * FC + 1]).then_inc(f_xg, 1)

            def mlp_gelu(n, t, c):
                M = n * NG + t
                act.wait_ge(f_gate, START + FC * M + c + 1)
                if c == 0:
                    if t == 0:
                        act.wait_ge(o_turned, START + 2 * NB * n + 2 * NB)
                    act.wait_ge(f_out, START + M)
                act.activation(gl[:, c, :], mlp_banks(t)[2 if c % 2 == 0 else 0], ACT.Gelu,
                               bias=vec[:, FC + c:FC + c + 1]).then_inc(f_gelu, 1)

            def sequence(l, n, ahead):
                for i in range(NB):
                    if i >= 1:
                        keep_p(n, i - 1, 2)
                    if i + 1 < NB:
                        square(n, i + 1, 0)
                    if i >= 1:
                        keep_p(n, i - 1, 3)
                    keep_qk(n, i, range(4))
                    if i + 1 < NB:
                        square(n, i + 1, 1)
                    if i >= 1:
                        keep_o(n, i - 1, 0)
                        keep_o(n, i - 1, 1)
                    if i + 1 < NB:
                        keep_v(n, i + 1)
                    for p in range(PAIRS):
                        if PAIRS - 4 < p < PAIRS - 1:
                            keep_p(n, i, p - (PAIRS - 3))
                        exps(n, i, p)
                mlp_square(n, 0)
                keep_p(n, NB - 1, 2)
                keep_p(n, NB - 1, 3)
                keep_o(n, NB - 1, 0)
                keep_o(n, NB - 1, 1)
                act.wait_ge(w_dve, START + 5 * (l + 1))
                mlp_gain(n, 0)
                mlp_gelu(n, 0, 0)
                mlp_gelu(n, 0, 1)
                mlp_square(n, 1)
                mlp_gelu(n, 0, 2)
                mlp_gain(n, 1)
                if ahead:
                    square(n + 1, 0, 0)
                    square(n + 1, 0, 1)
                for c in range(FC):
                    mlp_gelu(n, 1, c)
                if ahead:
                    keep_v(n + 1, 0)

            act.wait_ge(pads, START + 1)
            square(0, 0, 0)
            square(0, 0, 1)
            keep_v(0, 0)

            def layer(l, last):
                with act.Fori(0, B - 1) as b:
                    sequence(l, l * B + b, True)
                sequence(l, l * B + (B - 1), not last)

            with act.Fori(0, g.depth - 1) as l:
                layer(l, False)
            layer(g.depth - 1, True)

        @block.vector
        def _(dve):
            def sums(n, j, part):
                G = n * NB + j
                dve.wait_ge(squared, START + 2 * G + part + 1)
                dve.tensor_reduce(ss[:, part, :], sq[:, part, :].rearrange("p (h d) -> p h d", d=HD), X, ALU.add)\
                    .then_inc(summed, 1)

            def norms(n, j):
                G = n * NB + j
                dve.wait_ge(summed, START + 2 * G + 2)
                flat = [t.rearrange("p a h -> p (a h)") for t in (rn[:, j % 2, :, :], nx[:, :, :], nxh[:, :, :],
                                                                  nt[:, :, :], ss[:, :, :])]
                inverse_root(dve, *flat, 1e-24, ALU.max, norm_step, ROOT * G)

            def rotary_sines(n, j, part):
                G = n * NB + j
                dve.wait_ge(proj, START + 3 * G + part + 1)
                dve.wait_ge(rotated, START + 2 * G)
                src = pq[:, part, :, :].rearrange("p a (h s d) -> p (a h) s d", s=2, d=HALF)
                dst = bys[:, part, :].rearrange("p (h s d) -> p h s d", s=2, d=HALF)
                for s in range(2):
                    t = rot[:, part, 1, j, s * HALF:(s + 1) * HALF].unsqueeze(1).broadcast_to([P, H, HALF])
                    dve.tensor_tensor(dst[:, :, s, :], src[:, :, 1 - s, :], t, ALU.mult)

            def rotary_cosines(n, j, part):
                dve.tensor_tensor(byc[:, part, :].rearrange("p (h d) -> p h d", d=HD),
                                  pq[:, part, :, :].rearrange("p a (h d) -> p (a h) d", d=HD),
                                  rot[:, part, 0, j, :].unsqueeze(1).broadcast_to([P, H, HD]),
                                  ALU.mult).then_inc(rot_mul, 1)

            def rotary_products(n, j, part):
                rotary_sines(n, j, part)
                rotary_cosines(n, j, part)

            def smax(n, j, p):
                G = n * NB + j
                dve.wait_ge(scored, START + PAIRS * G + p + 1)
                k0 = W if j == 0 else 0
                dve.sem_inc(dve_gate, 1)
                for h in range(2):
                    op = dve.tensor_tensor_reduce(pr[:, 2 * p + h, k0:KEYS], psc[:, p % 2, h * 256 + k0:h * 256 + KEYS],
                                                  maskt[:, k0:KEYS], -1.0, 3e38, ALU.add, ALU.min,
                                                  nmax[:, 2 * p + h:2 * p + h + 1])
                op.then_inc(maxed, 1)

            def reciprocal(n, j):
                G = n * NB + j
                dve.wait_ge(exped, START + PAIRS * (G + 1))
                dve.reciprocal(rsum[:, :], psumr[:, :]).then_inc(recip, 1)

            def prev_turn(n, j, q):
                G = n * NB + j
                dve.wait_ge(p_kept, START + 4 * G + 1 + q)
                dve.transpose(pT[P - W:P, 4 * q:4 * q + 4, 0:W], pr[0:W, 4 * q:4 * q + 4, 0:W]).then_inc(pprev, 1)

            def normalise(n, j, c):
                G = n * NB + j
                dve.wait_ge(pvd, START + 2 * G + c + 1)
                dve.wait_ge(recip, START + G + 1)
                dve.wait_ge(o_turned, START + 2 * G)
                dve.tensor_tensor(o_s[:, c, :].rearrange("p (h d) -> p h d", d=HD),
                                  psc[:, c, :].rearrange("p (h d) -> p h d", d=HD),
                                  rsum[:, 8 * c:8 * c + 8].unsqueeze(2).broadcast_to([P, 8, HD]),
                                  ALU.mult).then_inc(o_norm, 1)

            def residual(n, b, j):
                G = n * NB + j
                dve.wait_ge(wod, START + G + 1)
                dve.tensor_tensor(hT[:, b, 1 + j * P:1 + (j + 1) * P], hT[:, b, 1 + j * P:1 + (j + 1) * P],
                                  wo_bank(j), ALU.add).then_inc(resid, 1)

            def shifted(n, b):
                dve.sem_inc(dve_gate, 1)
                for s in range(2):
                    lo, off = 64 * s, 1 - s
                    dve.tensor_copy(xs_hi[lo:lo + 64, :], hT[lo:lo + 64, b, off:off + L]).then_inc(xs_sem, 1)
                dve.wait_ge(xs_sem, START + 4 * n + 2)
                for s in range(2):
                    lo, off = 64 * s, 1 - s
                    dve.tensor_tensor(xs_lo[lo:lo + 64, :], hT[lo:lo + 64, b, off:off + L],
                                      xs_hi[lo:lo + 64, :].bitcast(F32), ALU.subtract).then_inc(xs_sem, 1)

            def mlp_shift(n, b, t):
                dve.wait_ge(resid, START + NB * n + (t + 1) * (NB // NG))
                dve.sem_inc(dve_gate, 1)
                dve.tensor_copy(fs[0:64, t * GT:(t + 1) * GT], hT[0:64, b, 1 + t * GT:1 + (t + 1) * GT])
                lo, hi = t * GT + min(t, 1), min((t + 1) * GT + 1, L)
                dve.tensor_copy(fs[64:P, lo:hi], hT[64:P, b, lo:hi]).then_inc(fsh, 1)

            def mlp_centre(n, t):
                M = n * NG + t
                dve.wait_ge(f_mean, START + M + 1)
                dve.wait_ge(f_xg, START + M)
                dve.tensor_tensor(cen[:, :], fs[:, t * GT:(t + 1) * GT], mlp_banks(t)[0], ALU.subtract).then_inc(f_cen, 1)

            def mlp_deviation(n, t):
                M = n * NG + t
                dve.wait_ge(f_var, START + M + 1)
                inverse_root(dve, mroot[:, 0, :], mroot[:, 1, :], mroot[:, 2, :], mroot[:, 3, :],
                             mlp_banks(t)[1][:, 0:GT // P], 1e-5, ALU.add, root_step, ROOT * M)
                for k in range(GT // P):
                    op = dve.tensor_scalar(rstd[:, k * P:(k + 1) * P], ident[:, :], mroot[:, 0, k:k + 1], None, ALU.mult)
                op.then_inc(f_rstd, 1)

            def mlp_normalise(n, t):
                M = n * NG + t
                dve.wait_ge(f_spread, START + M + 1)
                dve.wait_ge(f_cen, START + M + 1)
                dve.wait_ge(f_sq, START + M + 1)
                dve.tensor_tensor(xn[:, :], cen[:, :], mlp_banks(t)[1], ALU.mult).then_inc(f_xn, 1)

            def mlp_split(n, t):
                M = n * NG + t
                dve.wait_ge(f_xg, START + M + 1)
                dve.wait_ge(f_a, START + FC * M)
                dve.sem_inc(dve_gate, 1)
                dve.tensor_copy(xg_hi[:, :], xg[:, :]).then_inc(f_hi, 1)
                dve.wait_ge(f_hi, START + M + 1)
                dve.tensor_tensor(xg_lo[:, :], xg[:, :], xg_hi[:, :].bitcast(F32), ALU.subtract).then_inc(f_lo, 1)

            def mlp_gate(n, t, c):
                M = n * NG + t
                dve.wait_ge(f_a, START + FC * M + c + 1)
                dve.wait_ge(f_gelu, START + FC * M + c + 1)
                dve.scalar_tensor_tensor(u[:, c, :], mlp_banks(t)[3 if c % 2 == 0 else 1], vec[:, c:c + 1], gl[:, c, :],
                                         ALU.add, ALU.mult).then_inc(f_u, 1)

            def mlp_residual(n, b, t):
                M = n * NG + t
                dve.wait_ge(f_out, START + M + 1)
                h = hT[:, b, 1 + t * GT:1 + (t + 1) * GT]
                dve.scalar_tensor_tensor(h, mlp_banks(t)[0], vec[:, 2 * FC + 2:2 * FC + 3], h,
                                         ALU.add, ALU.add).then_inc(f_res, 1)

            def sequence(n, b, ahead, after=None):
                for i in range(NB):
                    if i > 1:
                        prev_turn(n, i - 1, 0)
                        prev_turn(n, i - 1, 1)
                    if i + 1 < NB:
                        rotary_products(n, i + 1, 0)
                    if i + 1 < NB:
                        rotary_sines(n, i + 1, 1)
                    if i > 1:
                        prev_turn(n, i - 1, 2)
                        prev_turn(n, i - 1, 3)
                    if i + 1 < NB:
                        rotary_cosines(n, i + 1, 1)
                    if i >= 1:
                        reciprocal(n, i - 1)
                        normalise(n, i - 1, 0)
                        normalise(n, i - 1, 1)
                    if i + 1 < NB:
                        sums(n, i + 1, 0)
                        sums(n, i + 1, 1)
                        norms(n, i + 1)
                    if i >= 1:
                        residual(n, b, i - 1)
                    if i == NB - 1 and after is not None:
                        split_attention(after)
                    for p in range(PAIRS):
                        smax(n, i, p)
                j = NB - 1
                mlp_shift(n, b, 0)
                mlp_centre(n, 0)
                prev_turn(n, j, 0)
                prev_turn(n, j, 1)
                reciprocal(n, j)
                prev_turn(n, j, 2)
                prev_turn(n, j, 3)
                mlp_deviation(n, 0)
                normalise(n, j, 0)
                normalise(n, j, 1)
                if ahead:
                    dve.wait_ge(proj, START + 3 * NB * (n + 1))
                    shifted(n + 1, b + 1 if after is None else 0)
                mlp_normalise(n, 0)
                mlp_split(n, 0)
                residual(n, b, j)
                mlp_shift(n, b, 1)
                mlp_gate(n, 0, 0)
                mlp_centre(n, 1)
                mlp_gate(n, 0, 1)
                mlp_gate(n, 0, 2)
                mlp_deviation(n, 1)
                mlp_residual(n, b, 0)
                mlp_normalise(n, 1)
                if after is not None:
                    dve.wait_ge(w_pool, START + POOL_STEPS * after + 6)
                if ahead:
                    rotary_products(n + 1, 0, 0)
                mlp_split(n, 1)
                if ahead:
                    rotary_products(n + 1, 0, 1)
                    sums(n + 1, 0, 0)
                mlp_gate(n, 1, 0)
                mlp_gate(n, 1, 1)
                if ahead:
                    sums(n + 1, 0, 1)
                mlp_gate(n, 1, 2)
                if ahead:
                    norms(n + 1, 0)
                mlp_residual(n, b, 1)

            def split_attention(l):
                dve.wait_ge(w_in, START + 16 * LOADS * (l + 1))
                dve.wait_ge(proj, START + 3 * NB * B * l)
                dve.sem_inc(dve_gate, 1)
                dve.tensor_copy(wqkv_hi[:, :], wqkv_in[:, :]).then_inc(w_dve, 1)
                dve.wait_ge(w_dve, START + 5 * l + 1)
                dve.tensor_tensor(wqkv_lo[:, :], wqkv_in[:, :], wqkv_hi[:, :].bitcast(F32), ALU.subtract).then_inc(w_dve, 1)

            def split_mlp(l):
                dve.wait_ge(f_out, START + NG * B * l)
                dve.wait_ge(f_res, START + NG * B * l)
                dve.sem_inc(dve_gate, 1)
                dve.tensor_copy(w1_hi[:, :, :], w1_in[:, :, :]).then_inc(w_dve, 1)
                dve.tensor_copy(vec[:, :], vec_in[:, :]).then_inc(w_dve, 1)
                dve.wait_ge(w_dve, START + 5 * l + 3)
                dve.tensor_tensor(w1_lo[:, :, :], w1_in[:, :, :], w1_hi[:, :, :].bitcast(F32), ALU.subtract).then_inc(w_dve, 1)
                dve.wait_ge(w_dve, START + 5 * l + 5)
                dve.sem_inc(w_used, 1)

            dve.memset(hT[:, :, 0:1], 0.0)
            dve.memset(ones[:, :], 1.0 / D)
            dve.memset(one[:, :], 1.0)
            dve.memset(qTz[:, :, :, :], 0.0)
            dve.memset(w1_in[:, :, :], 0.0)
            dve.memset(w2_in[:, :, :], 0.0)
            dve.memset(vec_in[:, :], 0.0).then_inc(pads, 1)
            dve.wait_ge(pads, START + 1)
            split_attention(0)
            shifted(0, 0)
            dve.wait_ge(w_pool, START + 6)
            rotary_products(0, 0, 0)
            rotary_products(0, 0, 1)
            sums(0, 0, 0)
            sums(0, 0, 1)
            norms(0, 0)
            dve.sem_inc(dve_gate, 1)

            def layer(l, after):
                split_mlp(l)
                with dve.Fori(0, B - 1) as b:
                    sequence(l * B + b, b, True)
                sequence(l * B + (B - 1), B - 1, after is not None, after)

            with dve.Fori(0, g.depth - 1) as l:
                layer(l, l + 1)
            layer(g.depth - 1, None)

        @block.gpsimd
        def _(pool):
            start_all(pool, sems)

            def add(n, j, part):
                G = n * NB + j
                pool.wait_ge(rot_mul, START + 2 * G + part + 1)
                pool.tensor_tensor(byc[:, part, :], byc[:, part, :], bys[:, part, :], ALU.add).then_inc(added, 1)

            def scale(n, j, part):
                G = n * NB + j
                pool.wait_ge(added, START + 2 * G + part + 1)
                pool.wait_ge(norm_step, START + ROOT * (G + 1))
                if j > 0:
                    pool.wait_ge(qk_turned, START + 4 * n * NB + 4 * j - 2 * part)
                pool.tensor_tensor(qkr[:, part, :].rearrange("p (h d) -> p h d", d=HD),
                                   byc[:, part, :].rearrange("p (h d) -> p h d", d=HD),
                                   rn[:, j % 2, part, :].unsqueeze(2).broadcast_to([P, H, HD]),
                                   ALU.mult).then_inc(rotated, 1)

            def rotate(n, j):
                add(n, j, 0)
                add(n, j, 1)
                scale(n, j, 1)
                scale(n, j, 0)

            def sequence(n):
                for j in range(1, NB):
                    rotate(n, j)

            pool.wait_ge(pads, START + 1)
            def tables(l):
                pool.wait_ge(w_in, START + 16 * LOADS * (l + 1))
                pool.wait_ge(rot_mul, START + 2 * NB * B * l)
                for i in range(2):
                    s = scl_in[:, i, :].rearrange("p (s d) -> p s d", s=2)
                    pool.tensor_tensor(rot[:, i, 0, :, :], tabs[:, i, 0, :, :],
                                       scl_in[:, i, :].unsqueeze(1).broadcast_to([P, NB, HD]),
                                       ALU.mult).then_inc(w_pool, 1)
                    for a in range(2):
                        o = slice(a * HALF, (a + 1) * HALF)
                        pool.tensor_tensor(rot[:, i, 1, :, o], tabs[:, i, 1, :, o],
                                           s[:, 1 - a, :].unsqueeze(1).broadcast_to([P, NB, HALF]),
                                           ALU.mult).then_inc(w_pool, 1)

            def layer(l, after):
                pool.wait_ge(f_out, START + NG * B * l)
                pool.sem_inc(pool_gate, 1)
                pool.tensor_copy(wo_s[:, :, :], wo_in[:, :, :]).then_inc(w_pool, 1)
                pool.tensor_copy(w2_s[:, :, :], w2_in[:, :, :]).then_inc(w_pool, 1)
                pool.wait_ge(w_pool, START + POOL_STEPS * (l + 1))
                pool.sem_inc(w_used, 1)
                with pool.Fori(0, B - 1) as b:
                    sequence(l * B + b)
                    rotate(l * B + b + 1, 0)
                sequence(l * B + (B - 1))
                if after is not None:
                    tables(after)
                    rotate(l * B + B, 0)

            tables(0)
            rotate(0, 0)
            with pool.Fori(0, g.depth - 1) as l:
                layer(l, l + 1)
            layer(g.depth - 1, None)


def finish(nc, g, hT, ident, x1_d, out):
    GT = 4 * P
    PER = g.L // GT
    GROUPS = g.B * PER
    ctx = ExitStack()
    with ctx:
        x1 = ctx.enter_context(nc.sbuf_tensor("x1_back", [P, GROUPS, GT], F32))
        p_out = ctx.enter_context(nc.psum_tensor("p_out", [P, 2, GT], F32))
        loaded = ctx.enter_context(nc.semaphore("x1_loaded"))
        turned = ctx.enter_context(nc.semaphore("h_turned"))
        summed = ctx.enter_context(nc.semaphore("out_summed"))
        stored = ctx.enter_context(nc.semaphore("out_stored"))
        block = ctx.enter_context(nc.Block())

        @block.sync
        def _(sp):
            sp.dma_start(x1[:, :, :].rearrange("p g n -> p (g n)"), x1_d.rearrange("p k d -> p (k d)")).then_inc(loaded, 16)
            for t in range(GROUPS):
                b, h = t // PER, t % PER
                sp.wait_ge(summed, t + 1)
                sp.dma_start(out[b, h * GT:(h + 1) * GT, :].rearrange("(k p) d -> p k d", p=P),
                             x1[:, t, :].rearrange("p (k d) -> p k d", d=P)).then_inc(stored, 16)
            sp.wait_ge(stored, 16 * GROUPS)

        @block.tensor
        def _(pe):
            for t in range(GROUPS):
                if t >= 2:
                    pe.wait_ge(summed, t - 1)
                for k in range(4):
                    o = 1 + (t % PER) * GT + k * P
                    mm = pe.transpose(p_out[:, t % 2, k * P:(k + 1) * P], hT[:, t // PER, o:o + P], ident[:, :])
                mm.then_inc(turned, 1)

        @block.vector
        def _(dve):
            dve.wait_ge(loaded, 16)
            for t in range(GROUPS):
                dve.wait_ge(turned, t + 1)
                dve.tensor_tensor(x1[:, t, :], x1[:, t, :], p_out[:, t % 2, :], ALU.add).then_inc(summed, 1)


def build(nc, x, q_w, k_w, v_w, o_w, wqkv, qsc, ksc, wo, ln_g, ln_b, w1, b1, w2, b2,
          identity, identity_b, causal, bias, window_mask, rotary, out):
    g = Geometry(x, wqkv, qsc, w1, wo)
    parts_d = nc.dram_tensor("qk_parts", [g.B, 2, 3, g.D, g.L], BF16, kind="Internal").ap()
    x1_d = nc.dram_tensor("x1_kept", [P, g.B * g.blocks, g.D], F32, kind="Internal").ap()
    ctx = ExitStack()
    with ctx:
        def sb(name, shape, dt=F32):
            return ctx.enter_context(nc.sbuf_tensor(name, shape, dt))

        hT = sb("h_t", [P, g.B, 1 + g.L])
        ident = sb("ident", [P, P])
        identb = sb("ident_b", [P, P], BF16)
        cmask = sb("causal_mask", [P, P], BF16)
        maskt = sb("window_mask_s", [P, g.keys])
        consts = ctx.enter_context(nc.semaphore("consts"))
        with nc.Block() as block:
            @block.sync
            def _(sp):
                for dst, src in ((ident, identity), (identb, identity_b), (cmask, causal), (maskt, window_mask)):
                    sp.dma_start(dst[:, :], src).then_inc(consts, 16)
                sp.wait_ge(consts, 64)
        with ExitStack() as first:
            x_all = first.enter_context(nc.sbuf_tensor("x_all", [P, g.B * g.blocks, g.D], F32))
            va = first.enter_context(nc.sbuf_tensor("v_all", [P, g.B * g.blocks, g.a_heads, g.a_hd + 1], F32))
            prepare(nc, g, x_all, va, ident, x, q_w, k_w, v_w, parts_d)
            causal_attention(nc, g, x_all, va, ident, identb, cmask, o_w, parts_d, bias)
            hand_over(nc, g, x_all, hT, ident, x1_d)
        with ExitStack() as second:
            tabs = second.enter_context(nc.sbuf_tensor("rotary_s", [P, 2, 2, g.blocks, g.hd], F32))
            got = second.enter_context(nc.semaphore("rotary_in"))
            with nc.Block() as block:
                @block.sync
                def _(sp):
                    sp.dma_start(tabs[:, :, :, :, :], rotary).then_inc(got, 16)
                    sp.wait_ge(got, 16)
            deep_layers(nc, g, hT, ident, tabs, maskt, wqkv, qsc, ksc, wo, ln_g, ln_b, w1, b1, w2, b2)
        finish(nc, g, hT, ident, x1_d, out)


def _split3(a):
    bf = _bf16()
    h = a.astype(bf)
    m = (a - h.astype(np.float32)).astype(bf)
    low = (a - h.astype(np.float32) - m.astype(np.float32)).astype(bf)
    return [h, m, low]


def _bf16():
    return np.dtype("bfloat16")


def _alibi_rows(heads, length):
    ratio = 2.0 ** (-8.0 / heads)
    slopes = np.asarray([ratio ** (i + 1) for i in range(heads)], np.float32)
    pos = np.arange(length)
    at = [(pos // 8 * 8).astype(np.float32), (pos % 8).astype(np.float32)]
    rows = np.zeros((heads, 2, 12, length), _bf16())
    for n, s in enumerate(_split3(slopes)):
        for k in range(2):
            rows[:, 0, 2 * n + k] = s[:, None]
            rows[:, 1, 2 * n + k] = at[k]
            rows[:, 0, 6 + 2 * n + k] = at[k]
            rows[:, 1, 6 + 2 * n + k] = -s[:, None]
    return rows


def _rotary(length, hd, window, qk_scale):
    half = np.arange(0, hd, 2, dtype=np.float32)
    freq = (1.0 / 10000.0 ** (half / hd)).astype(np.float32)
    t = np.arange(length, dtype=np.float32)
    angle = np.tile(t[:, None] * freq[None, :], (1, 2)).astype(np.float64)
    base = ((half + 0.4 * hd) / (1.4 * hd)).astype(np.float64)
    scale = np.tile(base[None, :] ** ((t - length // 2) / (window // 2))[:, None], (1, 2))
    sign = np.repeat([-1.0, 1.0], hd // 2)
    c, s = np.cos(angle), np.sin(angle) * sign
    t4 = np.stack([np.stack([c * scale, s * scale]) * qk_scale, np.stack([c / scale, s / scale])])
    return np.ascontiguousarray(t4.reshape(2, 2, length // P, P, hd).transpose(3, 0, 1, 2, 4).astype(np.float32))


def _window_mask(window):
    q = np.arange(P)[:, None]
    k = np.arange(P + window)[None, :] - window
    seen = (k <= q) & (k >= q - window)
    return np.where(seen, 0.0, MASKED).astype(np.float32)


def kernel(**inputs):
    import concourse.bacc as _bacc
    from concourse.bass_utils import run_bass_kernel_spmd as _run

    nc = _bacc.Bacc("TRN2", target_bir_lowering=False, num_devices=1)
    names = ["L0_attn_x", "L0_attn_q_w", "L0_attn_k_w", "L0_attn_v_w", "L0_attn_o_w", "L0_ffn_Wqkv",
             "L0_ffn_q_scale", "L0_ffn_k_scale", "L0_ffn_Wo", "L0_ffn_ln_g", "L0_ffn_ln_b", "L0_ffn_W1",
             "L0_ffn_b1", "L0_ffn_W2", "L0_ffn_b2"]
    arrays = {f"in_{n}": np.ascontiguousarray(inputs[n]) for n in names}
    length = arrays["in_L0_attn_x"].shape[1]
    bf = _bf16()
    causal = np.where(np.arange(P)[None, :] > np.arange(P)[:, None], -1e30, 0.0)
    arrays |= {
        "c_identity": np.eye(P, dtype=np.float32),
        "c_identity_b": np.eye(P, dtype=np.float32).astype(bf),
        "c_causal": causal.astype(np.float32).astype(bf),
        "c_bias": _alibi_rows(16, length),
        "c_window": _window_mask(32),
        "c_rotary": _rotary(length, arrays["in_L0_ffn_q_scale"].shape[1], 32, 8.0),
    }
    args = [nc.dram_tensor(n, a.shape, mybir.dt.from_np(a.dtype), kind="ExternalInput").ap() for n, a in arrays.items()]
    shape = arrays["in_L0_attn_x"].shape
    args.append(nc.dram_tensor("out_0", shape, F32, kind="ExternalOutput").ap())
    build(nc, *args)
    r = _run(nc, [arrays], core_ids=[0])
    return r.results[0]["out_0"]
```
